# Optimizing a Trainium2 kernel written in Bass

```python
import numpy as np
import jax
import jax.numpy as jnp

def _softmax(x, axis=-1):
    return jax.nn.softmax(x, axis=axis)

def _gelu(x):
    return jax.nn.gelu(x, approximate=True)

def _silu(x):
    return jax.nn.silu(x)

def _sigmoid(x):
    return jax.nn.sigmoid(x)

def _layernorm(x, axis=-1, eps=1e-05):
    m = jnp.mean(x, axis=axis, keepdims=True)
    v = jnp.var(x, axis=axis, keepdims=True)
    return (x - m) / jnp.sqrt(v + eps)

def _scatter_add(tgt, idx, src, axis=0):
    return tgt.at[idx].add(src)

def _segment_sum(src, seg, n):
    return jax.ops.segment_sum(src, seg, n)
kernel_name = 'mk_gnn_ffn_d4_gnn_r32_789de1'

def setup_inputs(seed: int=0):
    np.random.seed(seed)
    _w = jnp.asarray

    def _rec_inputs():
        import jax
        import jax.numpy as jnp
        _gk = jax.random.key(seed)
        x = -0.0002117 + 1 * jax.random.normal(jax.random.fold_in(_gk, 1), (3125, 256), jnp.float32)
        _s = jax.random.randint(jax.random.fold_in(_gk, 2), (25000,), 0, 3125, jnp.int32)
        _d = jax.random.randint(jax.random.fold_in(_gk, 3), (25000,), 0, 3125, jnp.int32)
        _loop = jnp.arange(3125, dtype=jnp.int32)
        src = jnp.concatenate([_s, _d, _loop])
        dst = jnp.concatenate([_d, _s, _loop])
        _o = jnp.argsort(dst, stable=True)
        src = src[_o]
        dst = dst[_o]
        edge_attr_16 = -0.000153872 + 1.00011 * jax.random.normal(jax.random.fold_in(_gk, 11), (53125, 16), jnp.float32)
        edge_attr_2 = jax.random.uniform(jax.random.fold_in(_gk, 12), (53125, 2), jnp.float32, 0.0, 1)
        edge_attr_32 = 0.000268479 + 0.999861 * jax.random.normal(jax.random.fold_in(_gk, 13), (53125, 32), jnp.float32)
        edge_attr_4 = 0.0007022 + 0.999661 * jax.random.normal(jax.random.fold_in(_gk, 14), (53125, 4), jnp.float32)
        edge_weight = jax.random.uniform(jax.random.fold_in(_gk, 16), (53125,), jnp.float32, 0.0, 0.999999)
        return (x, src, dst, edge_attr_16, edge_attr_2, edge_attr_32, edge_attr_4, edge_weight)
    x, src, dst, edge_attr_16, edge_attr_2, edge_attr_32, edge_attr_4, edge_weight = _rec_inputs()

    def _L0_gnn_setup():
        import jax, jax.numpy as jnp
        import numpy as np
        N_NODES = 3125
        N_EDGES = 50000
        IN_FEATS = 256
        OUT_FEATS = 64
        NUM_HEADS = 4
        key = jax.random.key(seed)
        k_h, k_adj, k_dir, k_wf, k_wr, k_af = jax.random.split(key, 6)
        h = jax.random.normal(k_h, (N_NODES, IN_FEATS), dtype=jnp.float32)
        adj = jax.random.randint(k_adj, (2, N_EDGES), 0, N_NODES, dtype=jnp.int64)
        bit = jax.random.randint(k_dir, (N_EDGES,), 0, 2).astype(jnp.float32)
        direction = jnp.stack([bit, 1.0 - bit], axis=1)
        s_w = float(np.sqrt(6.0 / (IN_FEATS + OUT_FEATS)))
        s_a = float(np.sqrt(6.0 / (NUM_HEADS + OUT_FEATS)))
        W_forward = jax.random.uniform(k_wf, (OUT_FEATS, IN_FEATS), jnp.float32, -s_w, s_w)
        W_reverse = jax.random.uniform(k_wr, (OUT_FEATS, IN_FEATS), jnp.float32, -s_w, s_w)
        attn_forward = jax.random.uniform(k_af, (1, NUM_HEADS, OUT_FEATS), jnp.float32, -s_a, s_a)
        return {'h': h, 'adj': adj, 'direction': direction, 'W_forward': W_forward, 'W_reverse': W_reverse, 'attn_forward': attn_forward}
    _L0_gnn_all = _L0_gnn_setup()
    _L0_gnn_in = {k: v for k, v in _L0_gnn_all.items() if k in ('W_forward', 'W_reverse', 'attn_forward')}
    del _L0_gnn_all

    def _L0_ffn_setup():
        import math
        import jax, jax.numpy as jnp
        import numpy as np
        CAPACITY_FACTOR = 1.25
        key = jax.random.key(seed)
        ks = jax.random.split(key, 5)
        B, L, D, F, E = (8, 256, 256, 1024, 8)
        h = jax.random.normal(ks[0], (B, L, D), dtype=jnp.float32)
        gate_w = jax.random.normal(ks[1], (D, E), dtype=jnp.float32) * 0.02
        gate_b = jnp.zeros((E,), dtype=jnp.float32)
        w1 = jax.random.normal(ks[2], (E, D, F), dtype=jnp.float32) * (1.0 / math.sqrt(D))
        b1 = jnp.zeros((E, F), dtype=jnp.float32)
        w2 = jax.random.normal(ks[3], (E, F, D), dtype=jnp.float32) * (1.0 / math.sqrt(F))
        b2 = jnp.zeros((E, D), dtype=jnp.float32)
        return {'h': h, 'gate_w': gate_w, 'gate_b': gate_b, 'w1': w1, 'b1': b1, 'w2': w2, 'b2': b2}
    _L0_ffn_all = _L0_ffn_setup()
    _L0_ffn_in = {k: v for k, v in _L0_ffn_all.items() if k in ('gate_w', 'gate_b', 'w1', 'b1', 'w2', 'b2')}
    del _L0_ffn_all

    def _L1_gnn_setup():
        import jax, jax.numpy as jnp
        import numpy as np
        N_NODES = 18870
        N_EDGES = 37500
        DIM = 256
        EPS = 1e-05

        def _layer_norm(x, g, b):
            mu = jnp.mean(x, axis=-1, keepdims=True)
            var = jnp.mean(jnp.square(x - mu), axis=-1, keepdims=True)
            return (x - mu) * jax.lax.rsqrt(var + EPS) * g + b

        def _gcn_conv(x, edge_index, edge_weight, W, b):
            n = x.shape[0]
            row, col = (edge_index[0], edge_index[1])
            loop = jnp.arange(n, dtype=row.dtype)
            row = jnp.concatenate([row, loop])
            col = jnp.concatenate([col, loop])
            ew = jnp.concatenate([edge_weight, jnp.ones((n,), dtype=x.dtype)])
            deg = jax.ops.segment_sum(ew, col, num_segments=n)
            dis = jnp.where(deg > 0, jax.lax.rsqrt(jnp.where(deg > 0, deg, 1.0)), 0.0)
            norm = dis[row] * ew * dis[col]
            h = x @ W.T
            msg = h[row] * norm[:, None]
            out = jax.ops.segment_sum(msg, col, num_segments=n)
            return out + b

        def _block(x, edge_index, edge_weight, g, bln, W, b):
            h = _layer_norm(x, g, bln)
            h = _gcn_conv(h, edge_index, edge_weight, W, b)
            h = jax.nn.relu(h)
            return x + h
        key = jax.random.key(seed)
        ks = jax.random.split(key, 8)
        s = 0.05
        return {'x': jax.random.normal(ks[0], (N_NODES, DIM), dtype=jnp.float32), 'edge_index': jax.random.randint(ks[1], (2, N_EDGES), 0, N_NODES, dtype=jnp.int64) if jax.config.jax_enable_x64 else jax.random.randint(ks[1], (2, N_EDGES), 0, N_NODES).astype(jnp.int32), 'edge_weight': jax.random.uniform(ks[2], (N_EDGES,), dtype=jnp.float32), 'ln6_g': jnp.ones((DIM,), jnp.float32), 'ln6_b': jnp.zeros((DIM,), jnp.float32), 'W6': jax.random.normal(ks[3], (DIM, DIM), jnp.float32) * s, 'b6': jnp.zeros((DIM,), jnp.float32), 'ln7_g': jnp.ones((DIM,), jnp.float32), 'ln7_b': jnp.zeros((DIM,), jnp.float32), 'W7': jax.random.normal(ks[4], (DIM, DIM), jnp.float32) * s, 'b7': jnp.zeros((DIM,), jnp.float32), 'Wp': jax.random.normal(ks[5], (DIM, DIM), jnp.float32) * s, 'bp': jnp.zeros((DIM,), jnp.float32)}
    _L1_gnn_all = _L1_gnn_setup()
    _L1_gnn_in = {k: v for k, v in _L1_gnn_all.items() if k in ('ln6_g', 'ln6_b', 'W6', 'b6', 'ln7_g', 'ln7_b', 'W7', 'b7', 'Wp', 'bp')}
    del _L1_gnn_all

    def _L1_ffn_setup():
        import jax, jax.numpy as jnp
        import numpy as np
        TOP_K = 2
        LN_EPS = 1e-05
        key = jax.random.key(seed)
        ks = jax.random.split(key, 8)
        B, S, D, E, H = (16, 1024, 256, 8, 1024)
        x = jax.random.normal(ks[0], (B, S, D), dtype=jnp.float32)
        Wr = jax.random.normal(ks[1], (D, E), dtype=jnp.float32) * 0.1
        br = jnp.zeros((E,), dtype=jnp.float32)
        ln_g = jnp.ones((E, D), dtype=jnp.float32)
        ln_b = jnp.zeros((E, D), dtype=jnp.float32)
        W1 = jax.random.normal(ks[2], (E, D, H), dtype=jnp.float32) * (1.0 / np.sqrt(D))
        b1 = jnp.zeros((E, H), dtype=jnp.float32)
        W2 = jax.random.normal(ks[3], (E, H, D), dtype=jnp.float32) * (1.0 / np.sqrt(H))
        b2 = jnp.zeros((E, D), dtype=jnp.float32)
        return {'x': x, 'Wr': Wr, 'br': br, 'ln_g': ln_g, 'ln_b': ln_b, 'W1': W1, 'b1': b1, 'W2': W2, 'b2': b2}
    _L1_ffn_all = _L1_ffn_setup()
    _L1_ffn_in = {k: v for k, v in _L1_ffn_all.items() if k in ('Wr', 'br', 'ln_g', 'ln_b', 'W1', 'b1', 'W2', 'b2')}
    del _L1_ffn_all

    def _L2_gnn_setup():
        import jax, jax.numpy as jnp
        import numpy as np
        N = 625
        E = 10000
        IN_DIM = 256
        OUT_DIM = 64
        HEADS = 4
        EDGE_DIM = 32
        NEG_SLOPE = 0.2

        def _gat_forward(x, edge_attr, lin_W, att_src, att_dst, lin_edge_W, att_edge, bias, edge_index):
            n = x.shape[0]
            loops = jnp.arange(n, dtype=edge_index.dtype)
            ei = jnp.concatenate([edge_index, jnp.stack([loops, loops])], axis=1)
            ea = jnp.concatenate([edge_attr, jnp.zeros((n, edge_attr.shape[1]), edge_attr.dtype)], axis=0)
            src, dst = (ei[0], ei[1])
            x_proj = (x @ lin_W.T).reshape(n, HEADS, OUT_DIM)
            s_src = jnp.einsum('nhd,hd->nh', x_proj, att_src)
            s_dst = jnp.einsum('nhd,hd->nh', x_proj, att_dst)
            att = s_src[src] + s_dst[dst]
            e_proj = (ea @ lin_edge_W.T).reshape(-1, HEADS, OUT_DIM)
            att = att + jnp.einsum('ehd,hd->eh', e_proj, att_edge)
            att = jnp.where(att >= 0, att, NEG_SLOPE * att)
            seg_max = jax.ops.segment_max(att, dst, num_segments=n)
            exps = jnp.exp(att - seg_max[dst])
            denom = jax.ops.segment_sum(exps, dst, num_segments=n)
            alpha = exps / (denom[dst] + 1e-12)
            m = x_proj[src] * alpha[:, :, None]
            out = jax.ops.segment_sum(m, dst, num_segments=n)
            out = out.reshape(n, HEADS * OUT_DIM) + bias
            return out
        key = jax.random.key(seed)
        ks = jax.random.split(key, 10)
        HD = HEADS * OUT_DIM
        x = jax.random.normal(ks[0], (N, IN_DIM), dtype=jnp.float32)
        edge_index = jax.random.randint(ks[1], (2, E), 0, N, dtype=jnp.int64)
        edge_attr = jax.random.normal(ks[2], (E, EDGE_DIM), dtype=jnp.float32)

        def xavier(k, shape):
            fan_in, fan_out = (shape[1], shape[0])
            a = np.sqrt(2.0) * np.sqrt(6.0 / (fan_in + fan_out))
            return jax.random.uniform(k, shape, jnp.float32, -a, a)
        lin_W = xavier(ks[3], (HD, IN_DIM))
        att_src = xavier(ks[4], (HEADS, OUT_DIM))
        att_dst = xavier(ks[5], (HEADS, OUT_DIM))
        lin_edge_W = xavier(ks[6], (HD, EDGE_DIM))
        att_edge = xavier(ks[7], (HEADS, OUT_DIM))
        bias = jnp.zeros((HD,), dtype=jnp.float32)
        return {'x': x, 'edge_index': edge_index, 'edge_attr': edge_attr, 'lin_W': lin_W, 'att_src': att_src, 'att_dst': att_dst, 'lin_edge_W': lin_edge_W, 'att_edge': att_edge, 'bias': bias}
    _L2_gnn_all = _L2_gnn_setup()
    _L2_gnn_in = {k: v for k, v in _L2_gnn_all.items() if k in ('lin_W', 'att_src', 'att_dst', 'lin_edge_W', 'att_edge', 'bias')}
    del _L2_gnn_all

    def _L2_ffn_setup():
        import jax, jax.numpy as jnp
        import numpy as np
        BN_EPS = 0.001

        def _bn(h, g, b, m, v):
            return g * (h - m) * jax.lax.rsqrt(v + BN_EPS) + b
        key = jax.random.key(seed)
        ks = jax.random.split(key, 8)
        B, F, Df = (256, 64, 256)
        E, H, D = (8, 256, 256)
        s1 = 1.0 / np.sqrt(Df)
        s2 = 1.0 / np.sqrt(H)
        return {'x': jax.random.normal(ks[0], (B, F, Df), jnp.float32), 'Wr': jax.random.normal(ks[1], (Df, E), jnp.float32) * s1, 'br': jnp.zeros((E,), jnp.float32), 'W1': jax.random.normal(ks[2], (E, Df, H), jnp.float32) * s1, 'b1': jnp.zeros((E, H), jnp.float32), 'g1': jnp.ones((E, H), jnp.float32), 'be1': jnp.zeros((E, H), jnp.float32), 'm1': jnp.zeros((E, H), jnp.float32), 'v1': jnp.ones((E, H), jnp.float32), 'W2': jax.random.normal(ks[3], (E, H, H), jnp.float32) * s2, 'b2': jnp.zeros((E, H), jnp.float32), 'g2': jnp.ones((E, H), jnp.float32), 'be2': jnp.zeros((E, H), jnp.float32), 'm2': jnp.zeros((E, H), jnp.float32), 'v2': jnp.ones((E, H), jnp.float32), 'Wo': jax.random.normal(ks[4], (E, H, D), jnp.float32) * s2, 'bo': jnp.zeros((E, D), jnp.float32)}
    _L2_ffn_all = _L2_ffn_setup()
    _L2_ffn_in = {k: v for k, v in _L2_ffn_all.items() if k in ('Wr', 'br', 'W1', 'b1', 'g1', 'be1', 'm1', 'v1', 'W2', 'b2', 'g2', 'be2', 'm2', 'v2', 'Wo', 'bo')}
    del _L2_ffn_all

    def _L3_gnn_setup():
        import jax, jax.numpy as jnp
        import numpy as np
        N, E, C, R, HID = (50000, 15625, 64, 16, 64)
        key = jax.random.key(seed)
        ks = jax.random.split(key, 24)
        g = lambda k, shape, s=1.0: jax.random.normal(k, shape, dtype=jnp.float32) * s
        cs = C ** (-0.5)
        inp = {'h': g(ks[0], (N, 4 * C)), 'edge_index': jax.random.randint(ks[1], (2, E), 0, N), 'edge_sh': g(ks[2], (E, 4)), 'edge_rbf': g(ks[3], (E, R)), 'W_up0': g(ks[4], (C, C), cs), 'W_up1': g(ks[5], (C, C), cs), 'M1': g(ks[6], (R, HID), R ** (-0.5)), 'M2': g(ks[7], (HID, HID), HID ** (-0.5)), 'M3': g(ks[8], (HID, HID), HID ** (-0.5)), 'M4': g(ks[9], (HID, 4 * C), HID ** (-0.5)), 'W_lin0': g(ks[10], (C, C), cs), 'W_lin1': g(ks[11], (C, C), cs), 'Wsc0': g(ks[12], (C, C), cs), 'Wsc1': g(ks[13], (C, C), cs), 'Wc0': g(ks[14], (C, 5)), 'Wc1': g(ks[15], (C, 4)), 'WB0': g(ks[16], (C, C), cs), 'WB1': g(ks[17], (C, C), cs), 'gamma0': jnp.ones((C,), jnp.float32), 'beta0': jnp.zeros((C,), jnp.float32), 'gamma1': jnp.ones((C,), jnp.float32)}
        return inp
    _L3_gnn_all = _L3_gnn_setup()
    _L3_gnn_in = {k: v for k, v in _L3_gnn_all.items() if k in ('W_up0', 'W_up1', 'M1', 'M2', 'M3', 'M4', 'W_lin0', 'W_lin1', 'Wsc0', 'Wsc1', 'Wc0', 'Wc1', 'WB0', 'WB1', 'gamma0', 'beta0', 'gamma1')}
    del _L3_gnn_all

    def _L3_ffn_setup():
        import jax, jax.numpy as jnp
        import numpy as np
        DIM = 256
        H = 8
        D = 64
        G = 64
        INNER = H * D
        SCALE = D ** (-0.5)
        key = jax.random.key(seed)
        ks = jax.random.split(key, 12)
        B, N = (4, 512)
        x = jax.random.normal(ks[0], (B, N, DIM), dtype=jnp.float32)
        s = lambda fan_in: 1.0 / np.sqrt(fan_in)
        W_fx = jax.random.normal(ks[1], (DIM, INNER), dtype=jnp.float32) * s(DIM)
        b_fx = jnp.zeros((INNER,), dtype=jnp.float32)
        W_x = jax.random.normal(ks[2], (DIM, INNER), dtype=jnp.float32) * s(DIM)
        b_x = jnp.zeros((INNER,), dtype=jnp.float32)
        A = jax.random.normal(ks[3], (G, D), dtype=jnp.float32)
        Q, _ = jnp.linalg.qr(A.T)
        W_slice = Q[:, :G].astype(jnp.float32)
        b_slice = jnp.zeros((G,), dtype=jnp.float32)
        W_q = jax.random.normal(ks[4], (D, D), dtype=jnp.float32) * s(D)
        W_k = jax.random.normal(ks[5], (D, D), dtype=jnp.float32) * s(D)
        W_v = jax.random.normal(ks[6], (D, D), dtype=jnp.float32) * s(D)
        W_out = jax.random.normal(ks[7], (INNER, DIM), dtype=jnp.float32) * s(INNER)
        b_out = jnp.zeros((DIM,), dtype=jnp.float32)
        temperature = jnp.ones((1, H, 1, 1), dtype=jnp.float32) * 0.5
        return {'x': x, 'W_fx': W_fx, 'b_fx': b_fx, 'W_x': W_x, 'b_x': b_x, 'W_slice': W_slice, 'b_slice': b_slice, 'W_q': W_q, 'W_k': W_k, 'W_v': W_v, 'W_out': W_out, 'b_out': b_out, 'temperature': temperature}
    _L3_ffn_all = _L3_ffn_setup()
    _L3_ffn_in = {k: v for k, v in _L3_ffn_all.items() if k in ('W_fx', 'b_fx', 'W_x', 'b_x', 'W_slice', 'b_slice', 'W_q', 'W_k', 'W_v', 'W_out', 'b_out', 'temperature')}
    del _L3_ffn_all
    return {'x': x, 'src': src, 'dst': dst, 'edge_attr_16': edge_attr_16, 'edge_attr_2': edge_attr_2, 'edge_attr_32': edge_attr_32, 'edge_attr_4': edge_attr_4, 'edge_weight': edge_weight, 'L0_gnn_W_forward': _L0_gnn_in['W_forward'], 'L0_gnn_W_reverse': _L0_gnn_in['W_reverse'], 'L0_gnn_attn_forward': _L0_gnn_in['attn_forward'], 'L0_ffn_gate_w': _L0_ffn_in['gate_w'], 'L0_ffn_gate_b': _L0_ffn_in['gate_b'], 'L0_ffn_w1': _L0_ffn_in['w1'], 'L0_ffn_b1': _L0_ffn_in['b1'], 'L0_ffn_w2': _L0_ffn_in['w2'], 'L0_ffn_b2': _L0_ffn_in['b2'], 'L1_gnn_ln6_g': _L1_gnn_in['ln6_g'], 'L1_gnn_ln6_b': _L1_gnn_in['ln6_b'], 'L1_gnn_W6': _L1_gnn_in['W6'], 'L1_gnn_b6': _L1_gnn_in['b6'], 'L1_gnn_ln7_g': _L1_gnn_in['ln7_g'], 'L1_gnn_ln7_b': _L1_gnn_in['ln7_b'], 'L1_gnn_W7': _L1_gnn_in['W7'], 'L1_gnn_b7': _L1_gnn_in['b7'], 'L1_gnn_Wp': _L1_gnn_in['Wp'], 'L1_gnn_bp': _L1_gnn_in['bp'], 'L1_ffn_Wr': _L1_ffn_in['Wr'], 'L1_ffn_br': _L1_ffn_in['br'], 'L1_ffn_ln_g': _L1_ffn_in['ln_g'], 'L1_ffn_ln_b': _L1_ffn_in['ln_b'], 'L1_ffn_W1': _L1_ffn_in['W1'], 'L1_ffn_b1': _L1_ffn_in['b1'], 'L1_ffn_W2': _L1_ffn_in['W2'], 'L1_ffn_b2': _L1_ffn_in['b2'], 'L2_gnn_lin_W': _L2_gnn_in['lin_W'], 'L2_gnn_att_src': _L2_gnn_in['att_src'], 'L2_gnn_att_dst': _L2_gnn_in['att_dst'], 'L2_gnn_lin_edge_W': _L2_gnn_in['lin_edge_W'], 'L2_gnn_att_edge': _L2_gnn_in['att_edge'], 'L2_gnn_bias': _L2_gnn_in['bias'], 'L2_ffn_Wr': _L2_ffn_in['Wr'], 'L2_ffn_br': _L2_ffn_in['br'], 'L2_ffn_W1': _L2_ffn_in['W1'], 'L2_ffn_b1': _L2_ffn_in['b1'], 'L2_ffn_g1': _L2_ffn_in['g1'], 'L2_ffn_be1': _L2_ffn_in['be1'], 'L2_ffn_m1': _L2_ffn_in['m1'], 'L2_ffn_v1': _L2_ffn_in['v1'], 'L2_ffn_W2': _L2_ffn_in['W2'], 'L2_ffn_b2': _L2_ffn_in['b2'], 'L2_ffn_g2': _L2_ffn_in['g2'], 'L2_ffn_be2': _L2_ffn_in['be2'], 'L2_ffn_m2': _L2_ffn_in['m2'], 'L2_ffn_v2': _L2_ffn_in['v2'], 'L2_ffn_Wo': _L2_ffn_in['Wo'], 'L2_ffn_bo': _L2_ffn_in['bo'], 'L3_gnn_W_up0': _L3_gnn_in['W_up0'], 'L3_gnn_W_up1': _L3_gnn_in['W_up1'], 'L3_gnn_M1': _L3_gnn_in['M1'], 'L3_gnn_M2': _L3_gnn_in['M2'], 'L3_gnn_M3': _L3_gnn_in['M3'], 'L3_gnn_M4': _L3_gnn_in['M4'], 'L3_gnn_W_lin0': _L3_gnn_in['W_lin0'], 'L3_gnn_W_lin1': _L3_gnn_in['W_lin1'], 'L3_gnn_Wsc0': _L3_gnn_in['Wsc0'], 'L3_gnn_Wsc1': _L3_gnn_in['Wsc1'], 'L3_gnn_Wc0': _L3_gnn_in['Wc0'], 'L3_gnn_Wc1': _L3_gnn_in['Wc1'], 'L3_gnn_WB0': _L3_gnn_in['WB0'], 'L3_gnn_WB1': _L3_gnn_in['WB1'], 'L3_gnn_gamma0': _L3_gnn_in['gamma0'], 'L3_gnn_beta0': _L3_gnn_in['beta0'], 'L3_gnn_gamma1': _L3_gnn_in['gamma1'], 'L3_ffn_W_fx': _L3_ffn_in['W_fx'], 'L3_ffn_b_fx': _L3_ffn_in['b_fx'], 'L3_ffn_W_x': _L3_ffn_in['W_x'], 'L3_ffn_b_x': _L3_ffn_in['b_x'], 'L3_ffn_W_slice': _L3_ffn_in['W_slice'], 'L3_ffn_b_slice': _L3_ffn_in['b_slice'], 'L3_ffn_W_q': _L3_ffn_in['W_q'], 'L3_ffn_W_k': _L3_ffn_in['W_k'], 'L3_ffn_W_v': _L3_ffn_in['W_v'], 'L3_ffn_W_out': _L3_ffn_in['W_out'], 'L3_ffn_b_out': _L3_ffn_in['b_out'], 'L3_ffn_temperature': _L3_ffn_in['temperature']}

def reference(x, src, dst, edge_attr_16, edge_attr_2, edge_attr_32, edge_attr_4, edge_weight, L0_gnn_W_forward, L0_gnn_W_reverse, L0_gnn_attn_forward, L0_ffn_gate_w, L0_ffn_gate_b, L0_ffn_w1, L0_ffn_b1, L0_ffn_w2, L0_ffn_b2, L1_gnn_ln6_g, L1_gnn_ln6_b, L1_gnn_W6, L1_gnn_b6, L1_gnn_ln7_g, L1_gnn_ln7_b, L1_gnn_W7, L1_gnn_b7, L1_gnn_Wp, L1_gnn_bp, L1_ffn_Wr, L1_ffn_br, L1_ffn_ln_g, L1_ffn_ln_b, L1_ffn_W1, L1_ffn_b1, L1_ffn_W2, L1_ffn_b2, L2_gnn_lin_W, L2_gnn_att_src, L2_gnn_att_dst, L2_gnn_lin_edge_W, L2_gnn_att_edge, L2_gnn_bias, L2_ffn_Wr, L2_ffn_br, L2_ffn_W1, L2_ffn_b1, L2_ffn_g1, L2_ffn_be1, L2_ffn_m1, L2_ffn_v1, L2_ffn_W2, L2_ffn_b2, L2_ffn_g2, L2_ffn_be2, L2_ffn_m2, L2_ffn_v2, L2_ffn_Wo, L2_ffn_bo, L3_gnn_W_up0, L3_gnn_W_up1, L3_gnn_M1, L3_gnn_M2, L3_gnn_M3, L3_gnn_M4, L3_gnn_W_lin0, L3_gnn_W_lin1, L3_gnn_Wsc0, L3_gnn_Wsc1, L3_gnn_Wc0, L3_gnn_Wc1, L3_gnn_WB0, L3_gnn_WB1, L3_gnn_gamma0, L3_gnn_beta0, L3_gnn_gamma1, L3_ffn_W_fx, L3_ffn_b_fx, L3_ffn_W_x, L3_ffn_b_x, L3_ffn_W_slice, L3_ffn_b_slice, L3_ffn_W_q, L3_ffn_W_k, L3_ffn_W_v, L3_ffn_W_out, L3_ffn_b_out, L3_ffn_temperature):
    import jax
    import jax.numpy as jnp

    def _L0_gnn_ref(h, adj, direction, W_forward, W_reverse, attn_forward):
        import jax, jax.numpy as jnp
        import numpy as np
        N_NODES = 3125
        N_EDGES = 50000
        IN_FEATS = 256
        OUT_FEATS = 64
        NUM_HEADS = 4
        N = h.shape[0]
        H = attn_forward.shape[1]
        h_fwd = h @ W_forward.T
        h_rev = h @ W_reverse.T
        src, dst = (adj[0], adj[1])
        messages = h_fwd[src] * direction[:, 0:1] + h_rev[src] * direction[:, 1:2]
        scores = jnp.einsum('ef,hf->eh', messages, attn_forward[0])
        scores = jax.nn.leaky_relu(scores, negative_slope=0.2)
        exp_scores = jnp.exp(scores - scores.max(axis=0, keepdims=True))
        sum_exp = jax.ops.segment_sum(exp_scores, dst, num_segments=N)
        norm = exp_scores / (sum_exp[dst] + 1e-10)
        outs = [jax.ops.segment_sum(messages * norm[:, hd:hd + 1], dst, num_segments=N) for hd in range(H)]
        out = jnp.stack(outs, axis=1)
        return out.reshape(N, -1)

    def _L0_ffn_ref(h, gate_w, gate_b, w1, b1, w2, b2):
        import math
        import jax, jax.numpy as jnp
        import numpy as np
        CAPACITY_FACTOR = 1.25
        B, L, D = h.shape
        E = gate_w.shape[1]
        T = B * L
        C = max(1, math.ceil(CAPACITY_FACTOR * T / E))
        x = h.reshape(T, D)
        logits = x @ gate_w + gate_b
        probs = jax.nn.softmax(logits, axis=-1)
        idx = jnp.argmax(probs, axis=-1)
        prb = jnp.take_along_axis(probs, idx[:, None], axis=1)[:, 0]
        one_hot = jax.nn.one_hot(idx, E, dtype=jnp.float32)
        pos = (jnp.cumsum(one_hot, axis=0) * one_hot).sum(-1).astype(jnp.int32) - 1
        kept = pos < C
        pos_safe = jnp.where(kept, pos, C)
        buf = jnp.zeros((E, C, D), dtype=h.dtype).at[idx, pos_safe].set(x, mode='drop')
        hmid = jax.nn.relu(jnp.einsum('ecd,edf->ecf', buf, w1) + b1[:, None, :])
        ybuf = jnp.einsum('ecf,efd->ecd', hmid, w2) + b2[:, None, :]
        pos_g = jnp.minimum(pos, C - 1)
        y_tok = ybuf[idx, pos_g] * (prb * kept)[:, None]
        y = y_tok.reshape(B, L, D)
        y = jnp.nan_to_num(y, nan=0.0, posinf=10000.0, neginf=-10000.0)
        return y

    def _L1_gnn_ref(x, edge_index, edge_weight, ln6_g, ln6_b, W6, b6, ln7_g, ln7_b, W7, b7, Wp, bp):
        import jax, jax.numpy as jnp
        import numpy as np
        N_NODES = 18870
        N_EDGES = 37500
        DIM = 256
        EPS = 1e-05

        def _layer_norm(x, g, b):
            mu = jnp.mean(x, axis=-1, keepdims=True)
            var = jnp.mean(jnp.square(x - mu), axis=-1, keepdims=True)
            return (x - mu) * jax.lax.rsqrt(var + EPS) * g + b

        def _gcn_conv(x, edge_index, edge_weight, W, b):
            n = x.shape[0]
            row, col = (edge_index[0], edge_index[1])
            loop = jnp.arange(n, dtype=row.dtype)
            row = jnp.concatenate([row, loop])
            col = jnp.concatenate([col, loop])
            ew = jnp.concatenate([edge_weight, jnp.ones((n,), dtype=x.dtype)])
            deg = jax.ops.segment_sum(ew, col, num_segments=n)
            dis = jnp.where(deg > 0, jax.lax.rsqrt(jnp.where(deg > 0, deg, 1.0)), 0.0)
            norm = dis[row] * ew * dis[col]
            h = x @ W.T
            msg = h[row] * norm[:, None]
            out = jax.ops.segment_sum(msg, col, num_segments=n)
            return out + b

        def _block(x, edge_index, edge_weight, g, bln, W, b):
            h = _layer_norm(x, g, bln)
            h = _gcn_conv(h, edge_index, edge_weight, W, b)
            h = jax.nn.relu(h)
            return x + h
        x = _block(x, edge_index, edge_weight, ln6_g, ln6_b, W6, b6)
        x = _block(x, edge_index, edge_weight, ln7_g, ln7_b, W7, b7)
        return x @ Wp.T + bp

    def _L1_ffn_ref(x, Wr, br, ln_g, ln_b, W1, b1, W2, b2):
        import jax, jax.numpy as jnp
        import numpy as np
        TOP_K = 2
        LN_EPS = 1e-05
        B, S, D = x.shape
        N = B * S
        xt = x.reshape(N, D)
        logits = xt @ Wr + br
        probs = jax.nn.softmax(logits, axis=-1)
        top_p, top_idx = jax.lax.top_k(probs, TOP_K)
        weights = top_p / top_p.sum(axis=-1, keepdims=True)
        mu = xt.mean(axis=-1, keepdims=True)
        var = ((xt - mu) ** 2).mean(axis=-1, keepdims=True)
        xn = (xt - mu) * jax.lax.rsqrt(var + LN_EPS)
        xe = xn[None, :, :] * ln_g[:, None, :] + ln_b[:, None, :]
        h = jax.nn.gelu(jnp.einsum('end,edh->enh', xe, W1) + b1[:, None, :], approximate=False)
        y = jnp.einsum('enh,ehd->end', h, W2) + b2[:, None, :]
        y_tok = jnp.transpose(y, (1, 0, 2))
        sel = jnp.take_along_axis(y_tok, top_idx[:, :, None], axis=1)
        out = (weights[:, :, None] * sel).sum(axis=1)
        return out.reshape(B, S, D)

    def _L2_gnn_ref(x, edge_index, edge_attr, lin_W, att_src, att_dst, lin_edge_W, att_edge, bias):
        import jax, jax.numpy as jnp
        import numpy as np
        N = 625
        E = 10000
        IN_DIM = 256
        OUT_DIM = 64
        HEADS = 4
        EDGE_DIM = 32
        NEG_SLOPE = 0.2

        def _gat_forward(x, edge_attr, lin_W, att_src, att_dst, lin_edge_W, att_edge, bias, edge_index):
            n = x.shape[0]
            loops = jnp.arange(n, dtype=edge_index.dtype)
            ei = jnp.concatenate([edge_index, jnp.stack([loops, loops])], axis=1)
            ea = jnp.concatenate([edge_attr, jnp.zeros((n, edge_attr.shape[1]), edge_attr.dtype)], axis=0)
            src, dst = (ei[0], ei[1])
            x_proj = (x @ lin_W.T).reshape(n, HEADS, OUT_DIM)
            s_src = jnp.einsum('nhd,hd->nh', x_proj, att_src)
            s_dst = jnp.einsum('nhd,hd->nh', x_proj, att_dst)
            att = s_src[src] + s_dst[dst]
            e_proj = (ea @ lin_edge_W.T).reshape(-1, HEADS, OUT_DIM)
            att = att + jnp.einsum('ehd,hd->eh', e_proj, att_edge)
            att = jnp.where(att >= 0, att, NEG_SLOPE * att)
            seg_max = jax.ops.segment_max(att, dst, num_segments=n)
            exps = jnp.exp(att - seg_max[dst])
            denom = jax.ops.segment_sum(exps, dst, num_segments=n)
            alpha = exps / (denom[dst] + 1e-12)
            m = x_proj[src] * alpha[:, :, None]
            out = jax.ops.segment_sum(m, dst, num_segments=n)
            out = out.reshape(n, HEADS * OUT_DIM) + bias
            return out
        return _gat_forward(x, edge_attr, lin_W, att_src, att_dst, lin_edge_W, att_edge, bias, edge_index)

    def _L2_ffn_ref(x, Wr, br, W1, b1, g1, be1, m1, v1, W2, b2, g2, be2, m2, v2, Wo, bo):
        import jax, jax.numpy as jnp
        import numpy as np
        BN_EPS = 0.001

        def _bn(h, g, b, m, v):
            return g * (h - m) * jax.lax.rsqrt(v + BN_EPS) + b
        feat = jnp.mean(x, axis=0)
        w = jax.nn.softmax(feat @ Wr + br, axis=-1)
        h = jnp.einsum('bfd,edh->bfeh', x, W1) + b1
        h = jax.nn.relu(_bn(h, g1, be1, m1, v1))
        h = jnp.einsum('bfeh,ehk->bfek', h, W2) + b2
        h = jax.nn.relu(_bn(h, g2, be2, m2, v2))
        y = jnp.einsum('bfeh,ehd->bfed', h, Wo) + bo
        return jnp.einsum('bfed,fe->bfd', y, w)

    def _L3_gnn_ref(h, edge_index, edge_sh, edge_rbf, W_up0, W_up1, M1, M2, M3, M4, W_lin0, W_lin1, Wsc0, Wsc1, Wc0, Wc1, WB0, WB1, gamma0, beta0, gamma1):
        import jax, jax.numpy as jnp
        import numpy as np
        N, E, C, R, HID = (50000, 15625, 64, 16, 64)
        n = h.shape[0]
        h0 = h[:, :C]
        h1 = h[:, C:].reshape(n, C, 3)
        up0 = h0 @ W_up0
        up1 = jnp.einsum('ncx,cd->ndx', h1, W_up1)
        r = jax.nn.silu(edge_rbf @ M1)
        r = jax.nn.silu(r @ M2)
        r = jax.nn.silu(r @ M3)
        tpw = (r @ M4).reshape(-1, 4, C)
        snd, rcv = (edge_index[0], edge_index[1])
        x0 = up0[snd]
        x1 = up1[snd]
        sh0 = edge_sh[:, 0]
        sh1 = edge_sh[:, 1:]
        inv3 = 1.0 / jnp.sqrt(jnp.float32(3.0))
        m0e = tpw[:, 0] * x0 * sh0[:, None] + tpw[:, 3] * jnp.einsum('ecx,ex->ec', x1, sh1) * inv3
        m1e = tpw[:, 1][:, :, None] * x0[:, :, None] * sh1[:, None, :] + tpw[:, 2][:, :, None] * x1 * sh0[:, None, None]
        msg0 = jax.ops.segment_sum(m0e, rcv, num_segments=n)
        msg1 = jax.ops.segment_sum(m1e, rcv, num_segments=n)
        A0 = msg0 @ W_lin0
        A1 = jnp.einsum('ncx,cd->ndx', msg1, W_lin1)
        sc0 = h0 @ Wsc0
        sc1 = jnp.einsum('ncx,cd->ndx', h1, Wsc1)
        vv = jnp.sum(A1 * A1, -1)
        B0 = Wc0[:, 0] * A0 + Wc0[:, 1] * A0 * A0 + Wc0[:, 2] * vv + Wc0[:, 3] * A0 ** 3 + Wc0[:, 4] * A0 * vv
        B1 = (Wc1[:, 0] + Wc1[:, 1] * A0 + Wc1[:, 2] * A0 * A0 + Wc1[:, 3] * vv)[..., None] * A1
        o0 = B0 @ WB0 + sc0
        o1 = jnp.einsum('ncx,cd->ndx', B1, WB1) + sc1
        eps = jnp.float32(1e-05)
        mu = jnp.mean(o0, 0)
        xc = o0 - mu
        var = jnp.mean(xc * xc, 0)
        n0 = xc * jax.lax.rsqrt(var + eps) * gamma0 + beta0
        nrm1 = jnp.mean(jnp.sum(o1 * o1, -1) / 3.0, 0)
        n1 = o1 * (jax.lax.rsqrt(nrm1 + eps) * gamma1)[None, :, None]
        return jnp.concatenate([n0, n1.reshape(n, 3 * C)], -1)

    def _L3_ffn_ref(x, W_fx, b_fx, W_x, b_x, W_slice, b_slice, W_q, W_k, W_v, W_out, b_out, temperature):
        import jax, jax.numpy as jnp
        import numpy as np
        DIM = 256
        H = 8
        D = 64
        G = 64
        INNER = H * D
        SCALE = D ** (-0.5)
        B, N, _ = x.shape
        fx_mid = (x @ W_fx + b_fx).reshape(B, N, H, D).transpose(0, 2, 1, 3)
        x_mid = (x @ W_x + b_x).reshape(B, N, H, D).transpose(0, 2, 1, 3)
        temp = jnp.clip(temperature, 0.1, 5.0)
        slice_weights = jax.nn.softmax((x_mid @ W_slice + b_slice) / temp, axis=-1)
        slice_norm = slice_weights.sum(axis=2)
        slice_token = jnp.einsum('bhnc,bhng->bhgc', fx_mid, slice_weights)
        slice_token = slice_token / (slice_norm[..., None] + 1e-05)
        q = slice_token @ W_q
        k = slice_token @ W_k
        v = slice_token @ W_v
        attn = jax.nn.softmax(jnp.einsum('bhgc,bhkc->bhgk', q, k) * SCALE, axis=-1)
        out_slice = jnp.einsum('bhgk,bhkc->bhgc', attn, v)
        out_x = jnp.einsum('bhgc,bhng->bhnc', out_slice, slice_weights)
        out_x = out_x.transpose(0, 2, 1, 3).reshape(B, N, INNER)
        return out_x @ W_out + b_out
    edge_index = jnp.stack([src, dst])
    x = x + _L0_gnn_ref(_layernorm(x, axis=-1), edge_index, edge_attr_2, L0_gnn_W_forward, L0_gnn_W_reverse, L0_gnn_attn_forward)
    x = x + _L0_ffn_ref(_layernorm(x, axis=-1)[None], L0_ffn_gate_w, L0_ffn_gate_b, L0_ffn_w1, L0_ffn_b1, L0_ffn_w2, L0_ffn_b2)[0]
    x = x + _L1_gnn_ref(_layernorm(x, axis=-1), edge_index, edge_weight, L1_gnn_ln6_g, L1_gnn_ln6_b, L1_gnn_W6, L1_gnn_b6, L1_gnn_ln7_g, L1_gnn_ln7_b, L1_gnn_W7, L1_gnn_b7, L1_gnn_Wp, L1_gnn_bp)
    x = x + _L1_ffn_ref(_layernorm(x, axis=-1)[None], L1_ffn_Wr, L1_ffn_br, L1_ffn_ln_g, L1_ffn_ln_b, L1_ffn_W1, L1_ffn_b1, L1_ffn_W2, L1_ffn_b2)[0]
    x = x + _L2_gnn_ref(_layernorm(x, axis=-1), edge_index, edge_attr_32, L2_gnn_lin_W, L2_gnn_att_src, L2_gnn_att_dst, L2_gnn_lin_edge_W, L2_gnn_att_edge, L2_gnn_bias)
    x = x + _L2_ffn_ref(_layernorm(x, axis=-1)[None], L2_ffn_Wr, L2_ffn_br, L2_ffn_W1, L2_ffn_b1, L2_ffn_g1, L2_ffn_be1, L2_ffn_m1, L2_ffn_v1, L2_ffn_W2, L2_ffn_b2, L2_ffn_g2, L2_ffn_be2, L2_ffn_m2, L2_ffn_v2, L2_ffn_Wo, L2_ffn_bo)[0]
    x = x + _L3_gnn_ref(_layernorm(x, axis=-1), edge_index, edge_attr_4, edge_attr_16, L3_gnn_W_up0, L3_gnn_W_up1, L3_gnn_M1, L3_gnn_M2, L3_gnn_M3, L3_gnn_M4, L3_gnn_W_lin0, L3_gnn_W_lin1, L3_gnn_Wsc0, L3_gnn_Wsc1, L3_gnn_Wc0, L3_gnn_Wc1, L3_gnn_WB0, L3_gnn_WB1, L3_gnn_gamma0, L3_gnn_beta0, L3_gnn_gamma1)
    x = x + _L3_ffn_ref(_layernorm(x, axis=-1)[None], L3_ffn_W_fx, L3_ffn_b_fx, L3_ffn_W_x, L3_ffn_b_x, L3_ffn_W_slice, L3_ffn_b_slice, L3_ffn_W_q, L3_ffn_W_k, L3_ffn_W_v, L3_ffn_W_out, L3_ffn_b_out, L3_ffn_temperature)[0]
    return x

_drawn_inputs = setup_inputs


def setup_inputs(seed=0):
    import zlib

    import numpy as np

    out = dict(_drawn_inputs(seed))
    spreads = {'L0_ffn_gate_b': (0.0, 0.1),
     'L0_ffn_b1': (0.0, 0.1),
     'L0_ffn_b2': (0.0, 0.1),
     'L1_gnn_ln6_g': (1.0, 0.2),
     'L1_gnn_ln6_b': (0.0, 0.1),
     'L1_gnn_b6': (0.0, 0.1),
     'L1_gnn_ln7_g': (1.0, 0.2),
     'L1_gnn_ln7_b': (0.0, 0.1),
     'L1_gnn_b7': (0.0, 0.1),
     'L1_gnn_bp': (0.0, 0.1),
     'L1_ffn_br': (0.0, 0.1),
     'L1_ffn_ln_g': (1.0, 0.2),
     'L1_ffn_ln_b': (0.0, 0.1),
     'L1_ffn_b1': (0.0, 0.1),
     'L1_ffn_b2': (0.0, 0.1),
     'L2_gnn_bias': (0.0, 0.1),
     'L2_ffn_br': (0.0, 0.735),
     'L2_ffn_b1': (0.0, 0.549),
     'L2_ffn_g1': (1.0, 0.54),
     'L2_ffn_be1': (0.0, 0.564),
     'L2_ffn_m1': (0.0, 0.556),
     'L2_ffn_v1': (1.0, 0.6),
     'L2_ffn_b2': (0.0, 0.386),
     'L2_ffn_g2': (1.0, 0.2),
     'L2_ffn_be2': (0.0, 0.412),
     'L2_ffn_m2': (0.0, 0.384),
     'L2_ffn_v2': (1.0, 0.6),
     'L2_ffn_bo': (0.0, 0.279),
     'L3_gnn_gamma0': (1.0, 0.2),
     'L3_gnn_beta0': (0.0, 0.328),
     'L3_gnn_gamma1': (1.0, 0.2),
     'L3_ffn_b_fx': (0.0, 0.1),
     'L3_ffn_b_x': (0.0, 0.8),
     'L3_ffn_b_slice': (0.0, 0.8),
     'L3_ffn_b_out': (0.0, 0.1),
     'L3_ffn_temperature': (0.5, 0.6)}
    factors = {'L3_ffn_W_x': 8.0, 'L3_ffn_W_slice': 8.0, 'L3_ffn_W_q': 8.0, 'L3_ffn_W_k': 8.0}
    for name, (base, spread) in spreads.items():
        noise = np.random.default_rng([zlib.crc32(name.encode()), seed]).standard_normal(out[name].shape)
        drawn = base * np.exp(spread * noise) if base else spread * noise
        out[name] = jnp.asarray(drawn.astype(out[name].dtype))
    for name, factor in factors.items():
        out[name] = (out[name] * factor).astype(out[name].dtype)
    return out
```

```python
from contextlib import ExitStack

import concourse.bass as bass
import numpy as np
from concourse import mybir

F32 = mybir.dt.float32
I32 = mybir.dt.int32
ALU = mybir.AluOpType
ACT = mybir.ActivationFunctionType
AX = mybir.AxisListType.X
ds = bass.ds

N = 3125
D = 256
T = 25
P = N // T
KD = D // 128
E = 53125
ET = E // P
LANES = 128
NT = 440
LAG = 2
NTL = NT + LAG
NTX = NT + 8
SRC, DL1, DIR, WGT, VALID = 0, 1, 2, 4, 5
HB = 10
SH, EAT, RBF = 6, 10, 16
ROW = 32
EF = 32
BIG = 1.0e30
ROUND = 12582912.0
NH = 4
HD = 64

assert E // LANES + T <= NT and P * T == N and ET * P == E and NT % 8 == 0


POOL_DMA_SEM_BASE = 100
SEM_BASE = 170


class Phase:

    opened = 0
    pool_dma_sems = 0

    def __init__(self, nc, name):
        Phase.opened += 1
        self.nc, self.name, self.stack = nc, f"{name}_{Phase.opened}", ExitStack()
        self.sems = 0

    def __enter__(self):
        self.stack.__enter__()
        return self

    def __exit__(self, *what):
        if what[0] is None:
            self.nc.all_engine_barrier(sems_to_clear=range(SEM_BASE, SEM_BASE + self.sems))
        self.stack.__exit__(*what)
        return False

    def sem(self, name):
        self.sems += 1
        return self.stack.enter_context(
            self.nc.semaphore(f"{self.name}_{name}", num=SEM_BASE + self.sems - 1))

    def sems_of(self, name, n):
        return [self.sem(f"{name}{i}") for i in range(n)]

    def pool_dma_sem(self, name):
        Phase.pool_dma_sems += 1
        return self.stack.enter_context(
            self.nc.semaphore(f"{self.name}_{name}", num=POOL_DMA_SEM_BASE + Phase.pool_dma_sems - 1))

    def sb(self, name, shape, dt=F32):
        return self.stack.enter_context(self.nc.sbuf_tensor(f"{self.name}_{name}", shape, dt))

    def ring(self, name, n, shape, dt=F32):
        return [self.sb(f"{name}{i}", shape, dt) for i in range(n)]

    def ps(self, name, n=1):
        return [self.stack.enter_context(self.nc.psum_tensor(f"{self.name}_{name}{i}", [128, 512], F32))
                for i in range(n)]


class Count:

    def __init__(self, sem, ahead=0):
        self.sem, self.ahead = sem, ahead

    def done(self, k):
        return k + 1 + self.ahead

    def freed(self, k, ring):
        return k + 1 - ring + self.ahead


class Chain:

    def __init__(self, eng, sem):
        self.eng, self.sem, self.n = eng, sem, 0

    def __call__(self, ins):
        self.n += 1
        ins.then_inc(self.sem, 1)
        self.eng.wait_ge(self.sem, self.n)

    def restart(self):
        self.eng.sem_clear(self.sem)
        self.n = 0


def blocks_of(eng, regs, blk_i, k):
    eng.load(regs, blk_i[0:1, ds(k, len(regs))])
    return [eng.snap(r, min_val=0, max_val=T - 1) for r in regs]


def flat(t):
    return t[:].rearrange("p a b -> p (a b)")


def over(ap, shape):
    return ap.unsqueeze(2).to_broadcast(shape)


def load_constants(nc, x, X, C):
    with Phase(nc, "setup") as ph:
        s_x, s_zero, s_made = ph.sem("x"), ph.sem("zero"), ph.sem("made")
        with nc.Block() as block:

            @block.sync
            def _(sp):
                sp.dma_start(X[:].rearrange("p (t d) -> p t d", d=D),
                             x.rearrange("(t p) d -> p t d", p=P)).then_inc(s_x, 16)
                sp.wait_ge(s_x, 16)

            @block.gpsimd
            def _(pool):
                pool.memset(C["ident"][:], 0.0).then_inc(s_zero, 1)
                pool.memset(C["tri"][:], 1.0).then_inc(s_zero, 1)
                pool.memset(C["ones"][:], 1.0).then_inc(s_zero, 1)
                pool.memset(C["zeros"][:], 0.0).then_inc(s_zero, 1)
                pool.wait_ge(s_zero, 4)
                pool.affine_select(out=C["ident"][:], in_=C["ident"][:], compare_op=ALU.not_equal, fill=1.0,
                                   base=0, pattern=[[-1, 128]], channel_multiplier=1).then_inc(s_made, 1)
                pool.affine_select(out=C["tri"][:], in_=C["tri"][:], compare_op=ALU.is_gt, fill=0.0,
                                   base=0, pattern=[[1, 128]], channel_multiplier=-1).then_inc(s_made, 1)
                pool.iota(C["nodes"][:], [[1, P]], base=1, channel_multiplier=0,
                          allow_small_or_imprecise_dtypes=True).then_inc(s_made, 1)
                pool.iota(C["row"][:], [[1, NT]], base=0, channel_multiplier=0,
                          allow_small_or_imprecise_dtypes=True).then_inc(s_made, 1)
                pool.wait_ge(s_made, 4)


def sort_edges(nc, C, dst, sorted_rows, slots, loc1, blk_i):
    with Phase(nc, "rank") as ph:
        s_dst, s_fill, s_ch = ph.sem("dst"), ph.sem("fill"), ph.sem("ch")
        s_zero, s_tot, s_pref, s_done = ph.sem("zero"), ph.sem("tot"), ph.sem("pref"), ph.sem("done")
        dst_i = ph.sb("dst_i", [P, ET], I32)
        dstf = ph.sb("dstf", [P, ET])
        blk = ph.sb("blk", [P, ET])
        eq = ph.sb("eq", [P, ET])
        cum = ph.sb("cum", [P, ET])
        slotf = ph.sb("slotf", [P, ET])
        zeros = ph.sb("zeros", [128, NT * ROW // 8])
        tot = ph.sb("tot", [P, T])
        tiles = ph.sb("tiles", [P, T])
        ends = ph.sb("ends", [P, T])
        base = ph.sb("base", [P, T])
        which = ph.sb("which", [1, NT])
        ps_pref, ps_all = ph.ps("pref"), ph.ps("all")
        zrows = sorted_rows.rearrange("(p r) c -> p (r c)", p=128)
        with nc.Block() as block:

            @block.sync
            def _(sp):
                sp.dma_start(dst_i[:], dst.rearrange("(p t) -> p t", p=P)).then_inc(s_dst, 16)
                sp.wait_ge(s_zero, 1)
                n = NT * ROW // 8
                for q in range(8):
                    sp.dma_start(zrows[:, q * n:(q + 1) * n], zeros[:]).then_inc(s_fill, 16)
                sp.wait_ge(s_fill, 8 * 16)

            @block.gpsimd
            def _(pool):
                pool.memset(zeros[:], 0.0).then_inc(s_zero, 1)

            @block.tensor
            def _(pe):
                pe.wait_ge(s_tot, 1)
                pe.matmul(ps_pref[0][0:P, 0:T], C["tri"][0:P, 0:P], tot[:], start=True, stop=True).then_inc(s_pref, 1)
                pe.matmul(ps_all[0][0:P, 0:T], C["ones"][0:P, 0:P], tot[:], start=True, stop=True).then_inc(s_pref, 1)

            @block.vector
            def _(v):
                ch = Chain(v, s_ch)
                v.wait_ge(s_dst, 16)
                ch(v.tensor_copy(dstf[:], dst_i[:]))
                ch(v.tensor_scalar(blk[:], dstf[:], float((P - 1) // 2), 1.0 / P, ALU.subtract, ALU.mult))
                ch(v.tensor_scalar(blk[:], blk[:], ROUND, ROUND, ALU.add, ALU.subtract))
                ch(v.scalar_tensor_tensor(loc1[:], blk[:], -float(P), dstf[:], ALU.mult, ALU.add))
                ch(v.tensor_scalar(loc1[:], loc1[:], 1.0, None, ALU.add))
                ch(v.memset(slotf[:], -1.0))
                ch(v.memset(which[:], 0.0))
                with v.Fori(0, T) as b:
                    ch.restart()
                    ch(v.tensor_scalar(eq[:], blk[:], C["row"][0:P, ds(b, 1)], None, ALU.is_equal))
                    ch(v.tensor_reduce(tot[:, ds(b, 1)], eq[:], AX, ALU.add))
                v.sem_inc(s_tot, 1)
                ch.restart()
                v.wait_ge(s_pref, 2)
                ch(v.tensor_scalar(tiles[:], ps_all[0][0:P, 0:T], 1.0 / LANES, (LANES - 1) / 2.0 / LANES,
                                   ALU.mult, ALU.add))
                ch(v.tensor_scalar(tiles[:], tiles[:], ROUND, ROUND, ALU.add, ALU.subtract))
                ch(v.tensor_tensor_scan(ends[:], C["ones"][0:P, 0:1].to_broadcast([P, T]), tiles[:], 0.0,
                                        ALU.mult, ALU.add))
                ch(v.tensor_tensor(base[:], ends[:], tiles[:], ALU.subtract))
                ch(v.scalar_tensor_tensor(base[:], base[:], float(LANES), ps_pref[0][0:P, 0:T], ALU.mult, ALU.add))
                with v.Fori(0, T) as b:
                    ch.restart()
                    ch(v.tensor_scalar(eq[:], blk[:], C["row"][0:P, ds(b, 1)], None, ALU.is_equal))
                    ch(v.tensor_tensor_scan(cum[:], C["ones"][0:P, 0:1].to_broadcast([P, ET]), eq[:], 0.0, ALU.mult, ALU.add))
                    ch(v.scalar_tensor_tensor(cum[:], cum[:], base[:, ds(b, 1)], eq[:], ALU.add, ALU.mult))
                    ch(v.tensor_tensor(slotf[:], slotf[:], cum[:], ALU.add))
                    ch(v.scalar_tensor_tensor(which[:], C["row"][0:1, 0:NT], ends[0:1, ds(b, 1)], which[:],
                                              ALU.is_ge, ALU.add))
                ch.restart()
                ch(v.tensor_scalar(which[:], which[:], float(T - 1), None, ALU.min))
                ch(v.tensor_copy(blk_i[:], which[:]))
                ch(v.tensor_copy(slots[:], slotf[:]))


def scatter_edges(nc, src, attr2, weight, attr4, attr16, attr32, edge_att, slots, loc1, sorted_rows):
    CH = 25
    NCH = ET // CH
    with Phase(nc, "scatter") as ph:
        s_in, s_used, s_sent, s_init = ph.sem("in"), ph.sem("used"), ph.pool_dma_sem("sent"), ph.sem("init")
        s_out, s_prod = ph.sem("out"), ph.sem("prod")
        pay = ph.sb("pay", [P, CH * ROW])
        st_src = ph.sb("src", [P, CH], I32)
        st2 = ph.sb("st2", [P, CH * 2])
        stw = ph.sb("stw", [P, CH])
        st4 = ph.sb("st4", [P, CH * 4])
        st16 = ph.sb("st16", [P, CH * 16])
        st32 = ph.sb("st32", [P, CH * EF])
        sl = ph.sb("sl", [P, CH], I32)
        prod = ph.sb("prod", [P, CH * NH * EF])

        def field(a, n):
            return pay[:].rearrange("p (c w) -> p c w", w=ROW)[:, :, a:a + n]

        def parts(t, n):
            return t[:].rearrange("p (c w) -> p c w", w=n)

        with nc.Block() as block:

            @block.sync
            def _(sp):
                sp.wait_ge(s_init, 1)
                sp.sem_inc(s_used, 8)
                with sp.Fori(0, NCH) as c:
                    sp.wait_ge(s_used, c * 8 + 8)
                    for t, a, n in ((st_src, src, 1), (st2, attr2, 2), (stw, weight, 1), (st4, attr4, 4),
                                    (st16, attr16, 16), (st32, attr32, EF)):
                        rows = (a.rearrange("(p t) -> p t", p=P) if n == 1
                                else a.rearrange("(p t) w -> p (t w)", p=P))
                        sp.dma_start(t[:], rows[:, ds(c * (CH * n), CH * n)]).then_inc(s_in, 16)

            @block.vector
            def _(v):
                v.memset(pay[:], 0.0).then_inc(s_init, 1)
                v.wait_ge(s_init, 1)
                v.memset(field(VALID, 1), 1.0).then_inc(s_init, 1)
                v.wait_ge(s_init, 2)
                with v.Fori(0, NCH) as c:
                    v.wait_ge(s_in, c * 96 + 96)
                    v.wait_ge(s_out, c + 1)
                    v.tensor_copy(field(SRC, 1).bitcast(I32), parts(st_src, 1)).then_inc(s_used, 1)
                    v.tensor_copy(field(DIR, 2), parts(st2, 2)).then_inc(s_used, 1)
                    v.tensor_copy(field(WGT, 1), parts(stw, 1)).then_inc(s_used, 1)
                    p4 = prod[:].rearrange("p (c h f) -> p c h f", h=NH, f=EF)
                    v.wait_ge(s_used, c * 8 + 8)
                    for h in range(NH):
                        last = v.tensor_tensor(p4[:, :, h, :], parts(st32, EF),
                                               edge_att[0:P, h * EF:(h + 1) * EF].unsqueeze(1).to_broadcast([P, CH, EF]),
                                               ALU.mult)
                    last.then_inc(s_prod, 1)
                    v.wait_ge(s_prod, c + 1)
                    v.tensor_reduce(field(EAT, NH), p4, AX, ALU.add).then_inc(s_used, 1)
                    v.tensor_copy(field(DL1, 1), loc1[:, ds(c * CH, CH)].unsqueeze(2)).then_inc(s_used, 1)
                    v.tensor_copy(sl[:], slots[:, ds(c * CH, CH)]).then_inc(s_used, 1)

            @block.scalar
            def _(act):
                act.wait_ge(s_init, 2)
                with act.Fori(0, NCH) as c:
                    act.wait_ge(s_in, c * 96 + 96)
                    act.wait_ge(s_out, c + 1)
                    act.activation(field(RBF, 16), parts(st16, 16), ACT.Copy).then_inc(s_used, 1)
                    act.activation(field(SH, 4), parts(st4, 4), ACT.Copy).then_inc(s_used, 1)

            @block.gpsimd
            def _(pool):
                pool.sem_inc(s_out, 1)
                with pool.Fori(0, NCH) as c:
                    pool.wait_ge(s_used, c * 8 + 16)
                    pool.nop(nofuse=True)
                    for t in range(CH):
                        pool.indirect_dma_start(
                            out=sorted_rows, out_offset=bass.IndirectOffsetOnAxis(ap=sl[:, t:t + 1], axis=0),
                            in_=pay[:, t * ROW:(t + 1) * ROW], in_offset=None).then_inc(s_sent, 16)
                    pool.wait_ge(s_sent, c * (16 * CH) + 16 * CH)
                    pool.sem_inc(s_out, 1)


def load_headers(nc, sorted_rows, hdr):
    with Phase(nc, "headers") as ph:
        s_h, s_z = ph.sem("h"), ph.sem("z")
        rows = sorted_rows.rearrange("(t p) c -> p t c", p=LANES)
        with nc.Block() as block:

            @block.sync
            def _(sp):
                sp.dma_start(hdr[:].rearrange("p (t c) -> p t c", c=HB)[:, 0:NT, :], rows[:, :, 0:HB]).then_inc(s_h, 16)
                sp.wait_ge(s_h, 16)

            @block.vector
            def _(v):
                v.memset(hdr[:, NT * HB:NTX * HB], 0.0).then_inc(s_z, 1)
                v.wait_ge(s_z, 1)


def row_stats(nc, src, rstd, nbias, eps):
    with Phase(nc, "stats") as ph:
        s_st, s_ch, s_var, s_sq = ph.sem("st"), ph.sem("ch"), ph.sem("var"), ph.sem("sq")
        st = ph.sb("st", [P, T * 6])
        mean = ph.sb("mean", [P, T])
        dif = ph.sb("dif", [P, T])
        var = ph.sb("var", [P, T])
        s6 = st[:].rearrange("p (t s) -> p t s", s=6)
        with nc.Block() as block:

            @block.vector
            def _(v):
                ch = Chain(v, s_ch)
                with v.Fori(0, T // 5) as i:
                    for u in range(5):
                        v.bn_stats(st[:, ds(i * 30 + u * 6, 6)], src[:, ds(i * (5 * D) + u * D, D)]).then_inc(s_st, 1)
                v.wait_ge(s_st, T)
                ch(v.tensor_tensor(mean[:], s6[:, :, 1], s6[:, :, 4], ALU.add))
                ch(v.tensor_tensor(dif[:], s6[:, :, 1], s6[:, :, 4], ALU.subtract))
                ch(v.tensor_tensor(var[:], s6[:, :, 2], s6[:, :, 5], ALU.add))
                ch(v.tensor_scalar(var[:], var[:], 1.0 / D, eps, ALU.mult, ALU.add))
                ch(v.tensor_tensor(dif[:], dif[:], dif[:], ALU.mult))
                v.scalar_tensor_tensor(var[:], dif[:], 0.25, var[:], ALU.mult, ALU.add).then_inc(s_var, 1)
                v.wait_ge(s_sq, 1)
                ch(v.reciprocal(rstd[:], var[:]))
                ch(v.scalar_tensor_tensor(nbias[:], mean[:], -0.5, rstd[:], ALU.mult, ALU.mult))

            @block.scalar
            def _(act):
                act.wait_ge(s_var, 1)
                act.activation(var[:], var[:], ACT.Sqrt).then_inc(s_sq, 1)


def project(nc, C, src, rstd, nbias, gain=None, keep=None, keepT=None, w=None, F=0, brow=None, out=None,
            scale=None, add_to=None, kd=KD):
    U = 5
    with Phase(nc, "project") as ph:
        s_norm, s_aff, s_tr, s_ev, s_mm, s_res = (ph.sem(n) for n in ("norm", "aff", "tr", "ev", "mm", "res"))
        s_keep = ph.sem("keep")
        xt = ph.ring("xt", U, [P, kd * 128])
        xT = ph.ring("xT", U, [128, kd * P])
        pT = ph.ps("pT", 3)
        pO = ph.ps("pO", U) if w is not None else None
        norm = Count(s_norm, 0)
        tr = Count(s_tr, U)
        nev = (w is not None) + (keepT is not None)
        mm = Count(s_mm, U)
        res = Count(s_res, U)

        def slot(u):
            return pT[u % 3][:, 0:kd * P]

        with nc.Block() as block:

            @block.scalar
            def _(act):
                with act.Fori(0, T // U) as i:
                    for u in range(U):
                        k = i * U + u
                        act.wait_ge(s_tr, tr.freed(k, U))
                        act.activation(xt[u][:], src[:, ds(k * (kd * 128), kd * 128)], ACT.Identity, bias=nbias[:, ds(k, 1)],
                                       scale=rstd[:, ds(k, 1)]).then_inc(s_norm, 1)
                        if keep is not None:
                            act.activation(keep[:, ds(k * D, D)], src[:, ds(k * D, D)], ACT.Identity,
                                           bias=nbias[:, ds(k, 1)], scale=rstd[:, ds(k, 1)]).then_inc(s_keep, 1)
                if keep is not None:
                    act.wait_ge(s_keep, T)

            @block.tensor
            def _(pe):
                pe.sem_inc(s_tr, U)
                if w is not None:
                    pe.sem_inc(s_mm, U)
                with pe.Fori(0, T // U) as i:
                    for u in range(U):
                        k = i * U + u
                        if gain is None:
                            pe.wait_ge(s_norm, norm.done(k))
                        else:
                            pe.wait_ge(s_aff, k * 2 + 2)
                        pe.wait_ge(s_ev, (k + U - (2 if u < 2 else 3)) * nev + nev)
                        for c in range(kd):
                            last = pe.transpose(slot(u)[:, c * P:(c + 1) * P], xt[u][:, c * 128:(c + 1) * 128],
                                                C["ident"][0:P, 0:P])
                        last.then_inc(s_tr, 1)
                    for u in range(U if w is not None else 0):
                        k = i * U + u
                        pe.wait_ge(s_ev, k * nev + nev * (U + 1))
                        pe.wait_ge(s_res, res.freed(k, U))
                        for c in range(kd):
                            last = pe.matmul(pO[u][0:P, 0:F], xT[u][:, c * P:(c + 1) * P], w[:, c * F:(c + 1) * F],
                                             start=(c == 0), stop=(c == kd - 1 and brow is None))
                        if brow is not None:
                            last = pe.matmul(pO[u][0:P, 0:F], C["ones"][0:1, 0:P], brow, start=False, stop=True)
                        last.then_inc(s_mm, 1)

            @block.vector
            def _(v):
                v.sem_inc(s_ev, U * nev)
                v.sem_inc(s_res, U)
                with v.Fori(0, T // U) as i:
                    for u in range(U):
                        k = i * U + u
                        v.wait_ge(s_norm, norm.done(k))
                        if gain is not None:
                            v.tensor_tensor(xt[u][:], xt[u][:], gain[0][:], ALU.mult).then_inc(s_aff, 1)
                            v.wait_ge(s_aff, k * 2 + 1)
                            v.tensor_tensor(xt[u][:], xt[u][:], gain[1][:], ALU.add).then_inc(s_aff, 1)
                    for u in range(U):
                        k = i * U + u
                        v.wait_ge(s_tr, tr.done(k))
                        if w is not None:
                            v.wait_ge(s_mm, mm.freed(k, U))
                            v.tensor_copy(xT[u][:], slot(u)).then_inc(s_ev, 1)
                        if keepT is not None:
                            v.tensor_copy(keepT[:].rearrange("p (c n) -> p c n", c=kd)[:, :, ds(k * P, P)],
                                          slot(u).rearrange("p (c n) -> p c n", c=kd)).then_inc(s_ev, 1)
                    for u in range(U if w is not None else 0):
                        k = i * U + u
                        v.wait_ge(s_mm, mm.done(k))
                        if add_to is not None:
                            v.tensor_tensor(add_to[:, ds(k * F, F)], add_to[:, ds(k * F, F)], pO[u][0:P, 0:F],
                                            ALU.add).then_inc(s_res, 1)
                        elif scale is not None:
                            v.tensor_scalar(out[:, ds(k * F, F)], pO[u][0:P, 0:F], scale[:, ds(k, 1)], None,
                                            ALU.mult).then_inc(s_res, 1)
                        else:
                            v.tensor_copy(out[:, ds(k * F, F)], pO[u][0:P, 0:F]).then_inc(s_res, 1)


def store_table(nc, res, table, F):
    with Phase(nc, "table") as ph:
        s = ph.sem("stored")
        with nc.Block() as block:

            @block.sync
            def _(sp):
                sp.dma_start(table.rearrange("(t p) f -> p t f", p=P),
                             res[:].rearrange("p (t f) -> p t f", f=F)).then_inc(s, 16)
                sp.wait_ge(s, 16)


def load_many(nc, pairs):
    with Phase(nc, "load") as ph:
        s = ph.sem("in")
        with nc.Block() as block:

            @block.sync
            def _(sp):
                for dst, src in pairs:
                    sp.dma_start(dst, src).then_inc(s, 16)
                sp.wait_ge(s, 16 * len(pairs))


F0 = 136
H0 = 68
A0 = 65
S0 = NH * A0 + 1


def gnn0_weights(nc, wf, wr, attnT, wfT, wrT, W):
    with Phase(nc, "w0") as ph:
        s_in, s_mm, s_ev = ph.sem("in"), ph.sem("mm"), ph.sem("ev")
        nat = ph.ring("nat", 2, [HD, D])
        at = ph.sb("at", [HD, NH])
        pW = ph.ps("pW", 4)
        Wv = W[:].rearrange("p (c f) -> p c f", c=KD)
        with nc.Block() as block:

            @block.sync
            def _(sp):
                sp.dma_start(nat[0][:], wf).then_inc(s_in, 16)
                sp.dma_start(nat[1][:], wr).then_inc(s_in, 16)
                sp.dma_start(at[:], attnT).then_inc(s_in, 16)
                sp.dma_start(Wv[:, :, 0:HD], wfT.rearrange("(c p) f -> p c f", p=128)).then_inc(s_in, 16)
                sp.dma_start(Wv[:, :, H0:H0 + HD], wrT.rearrange("(c p) f -> p c f", p=128)).then_inc(s_in, 16)
                sp.wait_ge(s_in, 80)

            @block.tensor
            def _(pe):
                pe.wait_ge(s_in, 80)
                for j in range(2):
                    for c in range(KD):
                        pe.matmul(pW[j * 2 + c][:, 0:NH], nat[j][:, c * 128:(c + 1) * 128], at[:], start=True,
                                  stop=True).then_inc(s_mm, 1)

            @block.vector
            def _(v):
                v.wait_ge(s_mm, 4)
                v.wait_ge(s_in, 80)
                for j in range(2):
                    for c in range(KD):
                        v.tensor_copy(Wv[:, c, j * H0 + HD:(j + 1) * H0],
                                      pW[j * 2 + c][:, 0:NH]).then_inc(s_ev, 1)
                v.wait_ge(s_ev, 4)


def gnn0_messages(nc, table, hdr, M):
    R = 8
    with Phase(nc, "msg0") as ph:
        s_cur, s_msg, s_tmp, s_init = ph.sem("cur"), ph.sem("msg"), ph.sem("tmp"), ph.sem("init")
        s_g = [ph.pool_dma_sem(f"g{i}") for i in range(R)]
        cur = ph.sb("cur", [128, R], I32)
        G = ph.ring("G", R, [128, F0])
        tmp = ph.ring("tmp", 2, [128, H0])
        cu, msg, tm = Count(s_cur), Count(s_msg, R), Count(s_tmp)
        with nc.Block() as block:

            @block.scalar
            def _(act):
                with act.Fori(0, NT // R) as i:
                    for u in range(R):
                        k = i * R + u
                        act.wait_ge(s_msg, msg.freed(k, R))
                        act.activation(cur[:, u:u + 1], hdr[:, ds(k * HB + SRC, 1)].bitcast(I32), ACT.Copy).then_inc(s_cur, 1)

            @block.gpsimd
            def _(pool):
                with pool.Fori(0, NT // R) as i:
                    for u in range(R):
                        k = i * R + u
                        pool.wait_ge(s_cur, cu.done(k))
                        pool.nop(nofuse=True)
                        pool.indirect_dma_start(out=G[u][:], out_offset=None, in_=table,
                                                in_offset=bass.IndirectOffsetOnAxis(ap=cur[:, u:u + 1], axis=0)
                                                ).then_inc(s_g[u], 16)

            @block.vector
            def _(v):
                v.memset(M[:, NT * H0:NTL * H0], 0.0).then_inc(s_init, 1)
                v.sem_inc(s_msg, R)
                with v.Fori(0, NT // R) as i:
                    for u in range(R):
                        k = i * R + u
                        v.wait_ge(s_g[u], i * 16 + 16)
                        v.wait_ge(s_msg, msg.freed(k, 2))
                        v.tensor_scalar(tmp[u % 2][:], G[u][:, H0:F0], hdr[:, ds(k * HB + DIR + 1, 1)], None,
                                        ALU.mult).then_inc(s_tmp, 1)
                        v.wait_ge(s_tmp, tm.done(k))
                        v.scalar_tensor_tensor(M[:, ds(k * H0, H0)], G[u][:, 0:H0], hdr[:, ds(k * HB + DIR, 1)],
                                               tmp[u % 2][:], ALU.mult, ALU.add).then_inc(s_msg, 1)
                v.wait_ge(s_msg, NT + R)


def gnn0_softmax(nc, hdr, M, ex):
    with Phase(nc, "soft0") as ph:
        s_ch, s_mx, s_all, s_ex, s_low = ph.sem("ch"), ph.sem("mx"), ph.sem("all"), ph.sem("ex"), ph.sem("low")
        low = ph.sb("low", [128, NTL])
        mx = ph.sb("mx", [128, NH])
        am = ph.sb("am", [128, NH])
        M3 = M[:].rearrange("p (t f) -> p t f", f=H0)
        sc = M3[:, :, HD:H0]
        e3 = ex[:].rearrange("p (t h) -> p t h", h=NH)
        h3 = hdr[:].rearrange("p (t c) -> p t c", c=HB)
        with nc.Block() as block:

            @block.vector
            def _(v):
                ch = Chain(v, s_ch)
                ch(v.scalar_tensor_tensor(e3, sc, 0.2, sc, ALU.mult, ALU.max))
                ch(v.tensor_scalar(low[:], h3[:, 0:NTL, VALID], 1.0, BIG, ALU.subtract, ALU.mult))
                ch(v.tensor_tensor(e3, e3, over(low[:], [128, NTL, NH]), ALU.add))
                v.tensor_reduce(mx[:], ex[:].rearrange("p (t h) -> p h t", h=NH), AX, ALU.max).then_inc(s_mx, 1)
                ch(v.memset(M3[:, :, HD:HD + 1], 1.0))
                v.wait_ge(s_all, 1)
                ch(v.tensor_tensor(e3, e3, am[:].unsqueeze(1).to_broadcast([128, NTL, NH]), ALU.subtract))
                v.sem_inc(s_low, 1)

            @block.gpsimd
            def _(pool):
                pool.wait_ge(s_mx, 1)
                pool.partition_all_reduce(am[:], mx[:], 128, bass.bass_isa.ReduceOp.max).then_inc(s_all, 1)

            @block.scalar
            def _(act):
                act.wait_ge(s_low, 1)
                act.activation(ex[:], ex[:], ACT.Exp).then_inc(s_ex, 1)
                act.wait_ge(s_ex, 1)


def gnn0_sum(nc, C, hdr, blk_i, M, ex, acc):
    R = 4
    G = 8
    with Phase(nc, "sum0") as ph:
        s_oh, s_mm, s_acc, s_z, s_w = ph.sem("oh"), ph.sem("mm"), ph.sem("acc"), ph.sem("z"), ph.sem("w")
        OH = ph.ring("OH", R, [128, P])
        Wt = ph.ring("Wt", R, [128, S0])
        pS = ph.ps("pS", R)
        oh, mm, ac = Count(s_oh), Count(s_mm, R), Count(s_acc, R)
        with nc.Block() as block:

            @block.vector
            def _(v):
                v.memset(acc[:], 0.0).then_inc(s_z, 1)
                v.wait_ge(s_z, 1)
                v.sem_inc(s_acc, R)

                def prepare(k, u):
                    v.wait_ge(s_mm, mm.freed(k, R))
                    v.tensor_scalar(OH[u][:], C["nodes"][:], hdr[:, ds(k * HB + DL1, 1)], None, ALU.is_equal).then_inc(s_oh, 1)
                    v.tensor_copy(Wt[u][:, S0 - 1:S0], hdr[:, ds(k * HB + WGT, 1)]).then_inc(s_oh, 1)
                    v.tensor_tensor(Wt[u][:, 0:NH * A0].rearrange("p (h f) -> p h f", h=NH),
                                    M[:, ds(k * H0, A0)].unsqueeze(1).to_broadcast([128, NH, A0]),
                                    over(ex[:, ds(k * NH, NH)], [128, NH, A0]), ALU.mult).then_inc(s_oh, 1)

                for u in range(LAG):
                    prepare(u, u)
                regs = [v.alloc_register(f"sum0_block{u}") for u in range(G)]
                with v.Fori(0, NT // G) as i:
                    blocks = blocks_of(v, regs, blk_i, i * G)
                    for u in range(G):
                        k = i * G + u
                        prepare(k + LAG, (u + LAG) % R)
                        v.wait_ge(s_mm, mm.done(k))
                        v.wait_ge(s_acc, ac.freed(k, 1))
                        a = acc[:, ds(blocks[u] * S0, S0)]
                        v.tensor_tensor(a, pS[u % R][0:P, 0:S0], a, ALU.add).then_inc(s_acc, 1)
                v.wait_ge(s_acc, NT + R)
                v.wait_ge(s_oh, 3 * NTL)

            @block.tensor
            def _(pe):
                pe.sem_inc(s_mm, R)
                with pe.Fori(0, NT // R) as i:
                    for u in range(R):
                        k = i * R + u
                        pe.wait_ge(s_oh, k * 3 + 3)
                        pe.wait_ge(s_acc, ac.freed(k, R))
                        pe.matmul(pS[u][0:P, 0:S0], OH[u][:], Wt[u][:], start=True, stop=True).then_inc(s_mm, 1)


def gnn0_update(nc, acc, X, dis):
    with Phase(nc, "upd0") as ph:
        s_ch, s_d, s_sq = ph.sem("ch"), ph.sem("d"), ph.sem("sq")
        den = ph.sb("den", [P, T * NH])
        deg = ph.sb("deg", [P, T])
        pos = ph.sb("pos", [P, T])
        a3 = acc[:].rearrange("p (t s) -> p t s", s=S0)
        x3 = X[:].rearrange("p (t d) -> p t d", d=D)
        with nc.Block() as block:

            @block.vector
            def _(v):
                ch = Chain(v, s_ch)
                ch(v.tensor_scalar(deg[:], a3[:, :, S0 - 1], 1.0, None, ALU.add))
                ch(v.tensor_scalar(pos[:], deg[:], 0.0, None, ALU.is_gt))
                ch(v.tensor_tensor(deg[:], deg[:], pos[:], ALU.mult))
                ch(v.tensor_tensor(deg[:], deg[:], pos[:], ALU.subtract))
                v.tensor_scalar(deg[:], deg[:], 1.0, None, ALU.add).then_inc(s_d, 1)
                d3 = den[:].rearrange("p (t h) -> p t h", h=NH)
                for h in range(NH):
                    ch(v.tensor_scalar(d3[:, :, h], a3[:, :, h * A0 + HD], 1e-10, None, ALU.add))
                ch(v.reciprocal(den[:], den[:]))
                for h in range(NH):
                    m = a3[:, :, h * A0:h * A0 + HD]
                    ch(v.tensor_tensor(m, m, over(d3[:, :, h], [P, T, HD]), ALU.mult))
                    xh = x3[:, :, h * HD:(h + 1) * HD]
                    ch(v.tensor_tensor(xh, xh, m, ALU.add))
                v.wait_ge(s_sq, 1)
                ch(v.reciprocal(deg[:], deg[:]))
                ch(v.tensor_tensor(dis[:], deg[:], pos[:], ALU.mult))

            @block.scalar
            def _(act):
                act.wait_ge(s_d, 1)
                act.activation(deg[:], deg[:], ACT.Sqrt).then_inc(s_sq, 1)


def normalise(nc, src, rstd, nbias, out):
    with Phase(nc, "norm") as ph:
        s_a, s_v = ph.sem("a"), ph.sem("v")
        with nc.Block() as block:

            @block.scalar
            def _(act):
                with act.Fori(0, T // 5) as i:
                    for u in range(5):
                        k = i * 5 + u
                        act.activation(out[:, ds(k * D, D)], src[:, ds(k * D, D)], ACT.Identity,
                                       bias=nbias[:, ds(k, 1)], scale=rstd[:, ds(k, 1)]).then_inc(s_a, 1)
                act.wait_ge(s_a, T)


def weighted_neighbour_sum(nc, C, hdr, blk_i, table, acc):
    R = 8
    RP = 4
    with Phase(nc, "conv") as ph:
        s_cur, s_oh, s_mm, s_acc = ph.sem("cur"), ph.sem("oh"), ph.sem("mm"), ph.sem("acc")
        s_g = [ph.pool_dma_sem(f"g{i}") for i in range(R)]
        cur = ph.sb("cur", [128, R], I32)
        G = ph.ring("G", R, [128, D])
        OH = ph.ring("OH", RP, [128, P])
        pS = ph.ps("pS", RP)
        cu, mm, ac = Count(s_cur), Count(s_mm, R), Count(s_acc, R)
        with nc.Block() as block:

            @block.scalar
            def _(act):
                with act.Fori(0, NT // R) as i:
                    for u in range(R):
                        k = i * R + u
                        act.wait_ge(s_mm, mm.freed(k, R))
                        act.activation(cur[:, u:u + 1], hdr[:, ds(k * HB + SRC, 1)].bitcast(I32), ACT.Copy).then_inc(s_cur, 1)

            @block.gpsimd
            def _(pool):
                with pool.Fori(0, NT // R) as i:
                    for u in range(R):
                        k = i * R + u
                        pool.wait_ge(s_cur, cu.done(k))
                        pool.nop(nofuse=True)
                        pool.indirect_dma_start(out=G[u][:], out_offset=None, in_=table,
                                                in_offset=bass.IndirectOffsetOnAxis(ap=cur[:, u:u + 1], axis=0)
                                                ).then_inc(s_g[u], 16)

            @block.vector
            def _(v):
                v.sem_inc(s_acc, R)

                def prepare(k, u):
                    v.wait_ge(s_mm, mm.freed(k, RP))
                    v.tensor_scalar(OH[u][:], C["nodes"][:], hdr[:, ds(k * HB + DL1, 1)],
                                    hdr[:, ds(k * HB + WGT, 1)], ALU.is_equal, ALU.mult).then_inc(s_oh, 1)

                for u in range(LAG):
                    prepare(u, u)
                regs = [v.alloc_register(f"{ph.name}_block{u}") for u in range(R)]
                with v.Fori(0, NT // R) as i:
                    blocks = blocks_of(v, regs, blk_i, i * R)
                    for u in range(R):
                        k = i * R + u
                        prepare(k + LAG, (u + LAG) % RP)
                        v.wait_ge(s_mm, mm.done(k))
                        v.wait_ge(s_acc, ac.freed(k, 1))
                        a = acc[:, ds(blocks[u] * D, D)]
                        v.tensor_tensor(a, pS[u % RP][0:P, 0:D], a, ALU.add).then_inc(s_acc, 1)
                v.wait_ge(s_acc, NT + R)
                v.wait_ge(s_oh, NTL)

            @block.tensor
            def _(pe):
                pe.sem_inc(s_mm, R)
                with pe.Fori(0, NT // R) as i:
                    for u in range(R):
                        k = i * R + u
                        pe.wait_ge(s_oh, k + 1)
                        pe.wait_ge(s_g[u], i * 16 + 16)
                        pe.wait_ge(s_acc, ac.freed(k, RP))
                        pe.matmul(pS[u % RP][0:P, 0:D], OH[u % RP][:], G[u][:], start=True, stop=True).then_inc(s_mm, 1)


def conv_update(nc, acc, dis, brow, Y):
    with Phase(nc, "convup") as ph:
        s_ch = ph.sem("ch")
        a3 = acc[:].rearrange("p (t d) -> p t d", d=D)
        y3 = Y[:].rearrange("p (t d) -> p t d", d=D)
        with nc.Block() as block:

            @block.vector
            def _(v):
                ch = Chain(v, s_ch)
                ch(v.tensor_tensor(a3, a3, over(dis[:], [P, T, D]), ALU.mult))
                ch(v.tensor_tensor(a3, a3, brow[:].unsqueeze(1).to_broadcast([P, T, D]), ALU.add))
                ch(v.scalar_tensor_tensor(y3, a3, 0.0, y3, ALU.max, ALU.add))


def gnn1(nc, C, hdr, blk_i, X, dis, rstd, nbias, dr, table):
    with ExitStack() as st:
        sb = lambda n, s: st.enter_context(nc.sbuf_tensor(f"g1_{n}", s, F32))
        Y, acc = sb("Y", [P, T * D]), sb("acc", [P, T * D])
        rows = {n: sb(n, [P, D]) for n in ("ln6_g", "ln6_b", "ln7_g", "ln7_b", "b6", "b7")}
        bp = sb("bp", [1, D])
        Ws = {n: sb(n, [128, KD * D]) for n in ("W6", "W7", "Wp")}
        load_many(nc, [(rows[n][:], dr[n].unsqueeze(0).to_broadcast([P, D])) for n in rows]
                  + [(bp[:], dr["bp"].unsqueeze(0))]
                  + [(Ws[n][:].rearrange("p (c f) -> p c f", c=KD), dr[n].rearrange("(c p) f -> p c f", p=128)) for n in Ws])
        row_stats(nc, X, rstd, nbias, 1e-5)
        normalise(nc, X, rstd, nbias, Y)
        for j in "67":
            row_stats(nc, Y, rstd, nbias, 1e-5)
            project(nc, C, Y, rstd, nbias, gain=(rows[f"ln{j}_g"], rows[f"ln{j}_b"]), w=Ws[f"W{j}"], F=D, out=acc, scale=dis)
            store_table(nc, acc, table, D)
            weighted_neighbour_sum(nc, C, hdr, blk_i, table, acc)
            conv_update(nc, acc, dis, rows[f"b{j}"], Y)
        plain(nc, rstd, nbias)
        project(nc, C, Y, rstd, nbias, w=Ws["Wp"], F=D, brow=bp[:], add_to=X)


def plain(nc, rstd, nbias):
    with Phase(nc, "plain") as ph:
        s = ph.sem("s")
        with nc.Block() as block:

            @block.vector
            def _(v):
                v.memset(rstd[:], 1.0).then_inc(s, 1)
                v.memset(nbias[:], 0.0).then_inc(s, 1)
                v.wait_ge(s, 2)


NE = 8
FH = 1024
KF = FH // 128
CAP = 489
ER = 123
EJ = 4
ES = ER * EJ
Q = 5
QN = Q * P
QA = 3 * P
BUF = NE * ES + N
assert CAP == -(-5 * N // (4 * NE)) and CAP <= ES and ER <= 128


def softmax_parts(ch, v, l3, m, s, shape):
    ch(v.tensor_reduce(m[:], l3, AX, ALU.max))
    ch(v.tensor_tensor(l3, l3, over(m[:], shape), ALU.subtract))


def first_of(ch, v, out3, p3, m, tmp3, iota3, ix, shape):
    ch(v.tensor_tensor(out3, p3, over(m[:], shape), ALU.is_equal))
    ch(v.scalar_tensor_tensor(tmp3, iota3, -float(NE), out3, ALU.add, ALU.mult))
    ch(v.tensor_reduce(ix[:], tmp3, AX, ALU.min))
    ch(v.tensor_scalar(ix[:], ix[:], float(NE), None, ALU.add))
    ch(v.tensor_tensor(out3, iota3, over(ix[:], shape), ALU.is_equal))


def route0(nc, C, logits, gslot, sslot, gate):
    sh = [P, T, NE]
    with Phase(nc, "route0") as ph:
        s_ch, s_a, s_b, s_oh, s_pf, s_io = (ph.sem(n) for n in ("ch", "a", "b", "oh", "pf", "io"))
        m, s, ix = ph.sb("m", [P, T]), ph.sb("s", [P, T]), ph.sb("ix", [P, T])
        oh, tmp = ph.sb("oh", [P, T * NE]), ph.sb("tmp", [P, T * NE])
        before, pos, kept = ph.sb("before", [P, T * NE]), ph.sb("pos", [P, T]), ph.sb("kept", [P, T])
        trash = ph.sb("trash", [P, T])
        pP, pA = ph.ps("pP"), ph.ps("pA")
        v3 = lambda t: t[:].rearrange("p (t e) -> p t e", e=NE)
        with nc.Block() as block:

            @block.gpsimd
            def _(pool):
                pool.iota(trash[:], [[P, T]], base=NE * ES, channel_multiplier=1,
                          allow_small_or_imprecise_dtypes=True).then_inc(s_io, 1)

            @block.scalar
            def _(act):
                act.wait_ge(s_a, 1)
                act.activation(logits[:], logits[:], ACT.Exp).then_inc(s_b, 1)

            @block.tensor
            def _(pe):
                pe.wait_ge(s_oh, 1)
                pe.matmul(pP[0][0:P, 0:T * NE], C["tri"][0:P, 0:P], oh[:], start=True, stop=True).then_inc(s_pf, 1)
                pe.matmul(pA[0][0:P, 0:T * NE], C["ones"][0:P, 0:P], oh[:], start=True, stop=True).then_inc(s_pf, 1)

            @block.vector
            def _(v):
                ch = Chain(v, s_ch)
                io3 = C["row"][0:P, 0:NE].unsqueeze(1).to_broadcast(sh)
                softmax_parts(ch, v, v3(logits), m, s, sh)
                v.sem_inc(s_a, 1)
                v.wait_ge(s_b, 1)
                ch(v.tensor_reduce(s[:], v3(logits), AX, ALU.add))
                ch(v.reciprocal(s[:], s[:]))
                ch(v.tensor_tensor(v3(logits), v3(logits), over(s[:], sh), ALU.mult))
                ch(v.tensor_reduce(m[:], v3(logits), AX, ALU.max))
                first_of(ch, v, v3(oh), v3(logits), m, v3(tmp), io3, ix, sh)
                v.sem_inc(s_oh, 1)
                v.wait_ge(s_pf, 2)
                ch(v.tensor_copy(tmp[:], pA[0][0:P, 0:T * NE]))
                for e in range(NE):
                    ch(v.tensor_tensor_scan(v3(before)[:, :, e], C["ones"][0:P, 0:1].to_broadcast([P, T]),
                                            v3(tmp)[:, :, e], 0.0, ALU.mult, ALU.add))
                ch(v.tensor_tensor(before[:], before[:], tmp[:], ALU.subtract))
                ch(v.tensor_tensor(before[:], before[:], pP[0][0:P, 0:T * NE], ALU.add))
                ch(v.tensor_tensor(before[:], before[:], oh[:], ALU.mult))
                ch(v.tensor_reduce(pos[:], v3(before), AX, ALU.add))
                ch(v.tensor_scalar(kept[:], pos[:], float(CAP), None, ALU.is_lt))
                ch(v.tensor_tensor(gate[:], m[:], kept[:], ALU.mult))
                ch(v.tensor_scalar(pos[:], pos[:], float(CAP - 1), None, ALU.min))
                ch(v.scalar_tensor_tensor(pos[:], ix[:], float(ES), pos[:], ALU.mult, ALU.add))
                ch(v.tensor_copy(gslot[:], pos[:]))
                v.wait_ge(s_io, 1)
                ch(v.tensor_tensor(pos[:], pos[:], trash[:], ALU.subtract))
                ch(v.tensor_tensor(pos[:], pos[:], kept[:], ALU.mult))
                ch(v.tensor_tensor(pos[:], pos[:], trash[:], ALU.add))
                ch(v.tensor_copy(sslot[:], pos[:]))


def dispatch0(nc, C, Y, sslot, buf):
    with Phase(nc, "disp0") as ph:
        s_z, s_f, s_s = ph.sem("z"), ph.sem("f"), ph.pool_dma_sem("s")
        zeros = ph.sb("zeros", [ER, NE * EJ * D])
        with nc.Block() as block:

            @block.sync
            def _(sp):
                sp.wait_ge(s_z, 1)
                sp.dma_start(buf[0:NE * ES, :].rearrange("(p r) d -> p (r d)", p=ER), zeros[:]).then_inc(s_f, 16)
                sp.wait_ge(s_f, 16)

            @block.vector
            def _(v):
                v.memset(zeros[:], 0.0).then_inc(s_z, 1)

            @block.gpsimd
            def _(pool):
                pool.wait_ge(s_f, 16)
                for t in range(T):
                    pool.indirect_dma_start(out=buf, out_offset=bass.IndirectOffsetOnAxis(ap=sslot[:, t:t + 1], axis=0),
                                            in_=Y[:, t * D:(t + 1) * D], in_offset=None).then_inc(s_s, 16)
                pool.wait_ge(s_s, 16 * T)


def experts0(nc, C, w1, b1T, w2, b2, buf, ybuf):
    with Phase(nc, "exp0") as ph:
        s_row, s_tr, s_bt, s_h, s_ha, s_y, s_yv = (ph.sem(n) for n in ("row", "tr", "bt", "h", "ha", "y", "yv"))
        s_st, s_free = ph.pool_dma_sem("st"), ph.sem("free")
        s_ld = ph.sems_of("ld", 2)
        b1s, b2s = ph.sb("b1", [128, NE * KF]), ph.sb("b2", [1, NE * D])
        w1s, w2s = ph.ring("w1", 2, [128, KD * FH]), ph.ring("w2", 2, [128, KF * D])
        bufs = ph.ring("buf", 2, [ER, EJ * D])
        bT = ph.sb("bT", [128, KD * ES])
        hT = ph.sb("hT", [128, KF * ES])
        ys = ph.ring("y", 2, [ER, EJ * D])
        pT, pH, pY = ph.ps("pT", 2), ph.ps("pH", 2), ph.ps("pY", 2)
        tr, bt, h, ha, y, yv = Count(s_tr, EJ), Count(s_bt, EJ), Count(s_h), Count(s_ha, 2), Count(s_y, 2 * EJ), Count(s_yv, EJ)
        with nc.Block() as block:

            @block.sync
            def _(sp):
                sp.dma_start(b1s[:], b1T).then_inc(s_row, 16)
                sp.dma_start(b2s[:], b2.rearrange("e d -> (e d)").unsqueeze(0)).then_inc(s_row, 16)
                with sp.Fori(0, NE // 2) as i:
                    for s in range(2):
                        e = i * 2 + s
                        sp.wait_ge(s_y, e * EJ + EJ)
                        sp.dma_start(w1s[s][:].rearrange("p (c f) -> p c f", c=KD),
                                     w1[ds(e * D, D), :].rearrange("(c p) f -> p c f", p=128)).then_inc(s_ld[s], 16)
                        sp.dma_start(w2s[s][:].rearrange("p (c d) -> p c d", c=KF),
                                     w2[ds(e * FH, FH), :].rearrange("(c p) d -> p c d", p=128)).then_inc(s_ld[s], 16)
                        sp.dma_start(bufs[s][:].rearrange("p (j d) -> p j d", j=EJ),
                                     buf[ds(e * ES, ES), :].rearrange("(j p) d -> p j d", p=ER)).then_inc(s_ld[s], 16)

            @block.tensor
            def _(pe):
                pe.sem_inc(s_tr, EJ)
                pe.sem_inc(s_y, 2 * EJ)
                pe.wait_ge(s_row, 32)
                with pe.Fori(0, NE // 2) as i:
                    for s in range(2):
                        e = i * 2 + s
                        pe.wait_ge(s_ld[s], i * 48 + 48)
                        for j in range(EJ):
                            k = e * EJ + j
                            pe.wait_ge(s_bt, bt.freed(k, 2))
                            for c in range(KD):
                                last = pe.transpose(pT[j % 2][:, c * ER:(c + 1) * ER],
                                                    bufs[s][:, j * D + c * 128:j * D + (c + 1) * 128],
                                                    C["ident"][0:ER, 0:ER])
                            last.then_inc(s_tr, 1)
                        pe.wait_ge(s_bt, bt.done(e * EJ + EJ - 1))
                        for f in range(KF):
                            k = e * KF + f
                            pe.wait_ge(s_ha, ha.freed(k, 2))
                            for c in range(KD):
                                last = pe.matmul(pH[f % 2][:, 0:ES], w1s[s][:, c * FH + f * 128:c * FH + (f + 1) * 128],
                                                 bT[:, c * ES:(c + 1) * ES], start=(c == 0), stop=(c == KD - 1))
                            last.then_inc(s_h, 1)
                        pe.wait_ge(s_ha, ha.done(e * KF + KF - 1))
                        for j in range(EJ):
                            k = e * EJ + j
                            pe.wait_ge(s_yv, yv.freed(k, 2))
                            for f in range(KF):
                                pe.matmul(pY[j % 2][0:ER, 0:D], hT[:, f * ES + j * ER:f * ES + (j + 1) * ER],
                                          w2s[s][:, f * D:(f + 1) * D], start=(f == 0), stop=False)
                            pe.matmul(pY[j % 2][0:ER, 0:D], C["ones"][0:1, 0:ER], b2s[:, ds(e * D, D)], start=False,
                                      stop=True).then_inc(s_y, 1)

            @block.scalar
            def _(act):
                act.sem_inc(s_ha, 2)
                act.wait_ge(s_row, 32)
                with act.Fori(0, NE // 2) as i:
                    for s in range(2):
                        e = i * 2 + s
                        for f in range(KF):
                            act.wait_ge(s_h, h.done(e * KF + f))
                            act.activation(hT[:, f * ES:(f + 1) * ES], pH[f % 2][:, 0:ES], ACT.Relu,
                                           bias=b1s[:, ds(e * KF + f, 1)]).then_inc(s_ha, 1)

            @block.vector
            def _(v):
                v.sem_inc(s_bt, EJ)
                v.sem_inc(s_yv, EJ)
                b3 = bT[:].rearrange("p (c n) -> p c n", c=KD)
                with v.Fori(0, NE // 2) as i:
                    for s in range(2):
                        e = i * 2 + s
                        for j in range(EJ):
                            v.wait_ge(s_tr, tr.done(e * EJ + j))
                            v.tensor_copy(b3[:, :, j * ER:(j + 1) * ER],
                                          pT[j % 2][:, 0:KD * ER].rearrange("p (c n) -> p c n", c=KD)).then_inc(s_bt, 1)
                        v.wait_ge(s_free, e + 1)
                        for j in range(EJ):
                            v.wait_ge(s_y, e * EJ + j + 1 + 2 * EJ)
                            v.tensor_copy(ys[s][:, j * D:(j + 1) * D], pY[j % 2][0:ER, 0:D]).then_inc(s_yv, 1)

            @block.gpsimd
            def _(pool):
                pool.sem_inc(s_free, 2)
                with pool.Fori(0, NE // 2) as i:
                    for s in range(2):
                        e = i * 2 + s
                        pool.wait_ge(s_yv, yv.done(e * EJ + EJ - 1))
                        pool.dma_start(ybuf[ds(e * ES, ES), :].rearrange("(j p) d -> p j d", p=ER),
                                       ys[s][:].rearrange("p (j d) -> p j d", j=EJ)).then_inc(s_st, 16)
                        pool.wait_ge(s_st, e * 16 + 16)
                        pool.sem_inc(s_free, 1)


def combine0(nc, ybuf, gslot, gate, X):
    U = 5
    with Phase(nc, "comb0") as ph:
        s_g, s_ch, s_k = ph.pool_dma_sem("g"), ph.sem("ch"), ph.sem("k")
        YG = ph.sb("YG", [P, T * D])
        mask = ph.ring("mask", 3, [P, D], I32)
        val = ph.ring("val", 3, [P, D])
        yt = ph.sb("yt", [P, D])
        with nc.Block() as block:

            @block.gpsimd
            def _(pool):
                for t in range(T):
                    pool.indirect_dma_start(out=YG[:, t * D:(t + 1) * D], out_offset=None, in_=ybuf,
                                            in_offset=bass.IndirectOffsetOnAxis(ap=gslot[:, t:t + 1], axis=0)
                                            ).then_inc(s_g, 16)

            @block.vector
            def _(v):
                ch = Chain(v, s_ch)
                for j, x in enumerate((0.0, 10000.0, -10000.0)):
                    ch(v.memset(val[j][:], x))
                v.wait_ge(s_g, 16 * T)
                with v.Fori(0, T) as t:
                    ch.restart()
                    y = yt[:]
                    ch(v.tensor_scalar(y, YG[:, ds(t * D, D)], gate[:, ds(t, 1)], None, ALU.mult))
                    ch(v.tensor_tensor(mask[0][:], y, y, ALU.not_equal))
                    ch(v.tensor_scalar(mask[1][:], y, 3.4028234e38, None, ALU.is_gt))
                    ch(v.tensor_scalar(mask[2][:], y, -3.4028234e38, None, ALU.is_lt))
                    for j in range(3):
                        ch(v.copy_predicated(y, mask[j][:], val[j][:]))
                    ch(v.tensor_tensor(X[:, ds(t * D, D)], X[:, ds(t * D, D)], y, ALU.add))


def ffn0(nc, C, X, rstd, nbias, dr, buf, ybuf):
    with ExitStack() as st:
        sb = lambda n, s, d=F32: st.enter_context(nc.sbuf_tensor(f"f0_{n}", s, d))
        gslot, sslot, gate = sb("gslot", [P, T], I32), sb("sslot", [P, T], I32), sb("gate", [P, T])
        with ExitStack() as s2:
            sc = lambda n, s: s2.enter_context(nc.sbuf_tensor(f"f0_{n}", s, F32))
            Y, logits, gw, gb = sc("Y", [P, T * D]), sc("logits", [P, T * NE]), sc("gw", [128, KD * NE]), sc("gb", [1, NE])
            load_many(nc, [(gw[:].rearrange("p (c f) -> p c f", c=KD), dr["gate_w"].rearrange("(c p) f -> p c f", p=128)),
                           (gb[:], dr["gate_b"].unsqueeze(0))])
            row_stats(nc, X, rstd, nbias, 1e-5)
            project(nc, C, X, rstd, nbias, keep=Y, w=gw, F=NE, brow=gb[:], out=logits)
            route0(nc, C, logits, gslot, sslot, gate)
            dispatch0(nc, C, Y, sslot, buf)
        experts0(nc, C, dr["w1"].rearrange("e d f -> (e d) f"), dr["b1T"], dr["w2"].rearrange("e f d -> (e f) d"),
                 dr["b2"], buf, ybuf)
        combine0(nc, ybuf, gslot, gate, X)


def gates1(nc, C, logits, gates):
    sh = [P, T, NE]
    with Phase(nc, "gate1") as ph:
        s_ch, s_a, s_b = ph.sem("ch"), ph.sem("a"), ph.sem("b")
        m, s, ix, m2 = ph.sb("m", [P, T]), ph.sb("s", [P, T]), ph.sb("ix", [P, T]), ph.sb("m2", [P, T])
        o1, o2, tmp, rest = (ph.sb(n, [P, T * NE]) for n in ("o1", "o2", "tmp", "rest"))
        v3 = lambda t: t[:].rearrange("p (t e) -> p t e", e=NE)
        with nc.Block() as block:

            @block.scalar
            def _(act):
                act.wait_ge(s_a, 1)
                act.activation(logits[:], logits[:], ACT.Exp).then_inc(s_b, 1)

            @block.vector
            def _(v):
                ch = Chain(v, s_ch)
                io3 = C["row"][0:P, 0:NE].unsqueeze(1).to_broadcast(sh)
                softmax_parts(ch, v, v3(logits), m, s, sh)
                v.sem_inc(s_a, 1)
                v.wait_ge(s_b, 1)
                ch(v.tensor_reduce(s[:], v3(logits), AX, ALU.add))
                ch(v.reciprocal(s[:], s[:]))
                ch(v.tensor_tensor(v3(logits), v3(logits), over(s[:], sh), ALU.mult))
                ch(v.tensor_reduce(m[:], v3(logits), AX, ALU.max))
                first_of(ch, v, v3(o1), v3(logits), m, v3(tmp), io3, ix, sh)
                ch(v.scalar_tensor_tensor(v3(rest), v3(o1), -2.0, v3(logits), ALU.mult, ALU.add))
                ch(v.tensor_reduce(m2[:], v3(rest), AX, ALU.max))
                first_of(ch, v, v3(o2), v3(rest), m2, v3(tmp), io3, ix, sh)
                ch(v.tensor_tensor(s[:], m[:], m2[:], ALU.add))
                ch(v.reciprocal(s[:], s[:]))
                ch(v.tensor_tensor(m[:], m[:], s[:], ALU.mult))
                ch(v.tensor_tensor(m2[:], m2[:], s[:], ALU.mult))
                ch(v.tensor_tensor(v3(gates), v3(o1), over(m[:], sh), ALU.mult))
                ch(v.tensor_tensor(v3(o2), v3(o2), over(m2[:], sh), ALU.mult))
                ch(v.tensor_tensor(gates[:], gates[:], o2[:], ALU.add))


def gates2(nc, logits, gates):
    sh = [P, T, NE]
    with Phase(nc, "gate2") as ph:
        s_ch, s_a, s_b = ph.sem("ch"), ph.sem("a"), ph.sem("b")
        m, s = ph.sb("m", [P, T]), ph.sb("s", [P, T])
        v3 = lambda t: t[:].rearrange("p (t e) -> p t e", e=NE)
        with nc.Block() as block:

            @block.scalar
            def _(act):
                act.wait_ge(s_a, 1)
                act.activation(logits[:], logits[:], ACT.Exp).then_inc(s_b, 1)

            @block.vector
            def _(v):
                ch = Chain(v, s_ch)
                softmax_parts(ch, v, v3(logits), m, s, sh)
                v.sem_inc(s_a, 1)
                v.wait_ge(s_b, 1)
                ch(v.tensor_reduce(s[:], v3(logits), AX, ALU.add))
                ch(v.reciprocal(s[:], s[:]))
                ch(v.tensor_tensor(v3(gates), v3(logits), over(s[:], sh), ALU.mult))


def experts1(nc, C, YT, gates, w1, b1T, gT, bT, w2, b2, X):
    with Phase(nc, "exp1") as ph:
        s_row, s_w, s_bm, s_bs, s_gs, s_h, s_ha, s_y, s_yv = (
            ph.sem(n) for n in ("row", "w", "bm", "bs", "gs", "h", "ha", "y", "yv"))
        s_ld = ph.sems_of("ld", 2)
        b1s, b2s = ph.sb("b1", [128, NE * KF]), ph.sb("b2", [1, NE * D])
        gs, lbs = ph.sb("gs", [128, NE * KD]), ph.sb("lbs", [128, NE * KD])
        w1s, w2s = ph.ring("w1", 2, [128, KD * FH]), ph.ring("w2", 2, [128, KF * D])
        bc = ph.ring("bc", 2, [128, KF])
        hT = ph.sb("hT", [128, KF * QN])
        pHa, pHb, pY, pB = ph.ps("pHa", 2), ph.ps("pHb", 2), ph.ps("pY", 2), ph.ps("pB")
        NK = Q * Q
        h, ha, y, yv = Count(s_h), Count(s_ha, 2), Count(s_y, 2 * NK), Count(s_yv, 2)
        with nc.Block() as block:

            @block.sync
            def _(sp):
                sp.dma_start(b1s[:], b1T).then_inc(s_row, 16)
                sp.dma_start(b2s[:], b2.rearrange("e d -> (e d)").unsqueeze(0)).then_inc(s_row, 16)
                sp.dma_start(gs[:], gT).then_inc(s_row, 16)
                sp.dma_start(lbs[:], bT).then_inc(s_row, 16)
                with sp.Fori(0, NE // 2) as i:
                    for s in range(2):
                        e = i * 2 + s
                        sp.wait_ge(s_y, e * NK + NK)
                        sp.dma_start(w1s[s][:].rearrange("p (c f) -> p c f", c=KD),
                                     w1[ds(e * D, D), :].rearrange("(c p) f -> p c f", p=128)).then_inc(s_ld[s], 16)
                        sp.dma_start(w2s[s][:].rearrange("p (c d) -> p c d", c=KF),
                                     w2[ds(e * FH, FH), :].rearrange("(c p) d -> p c d", p=128)).then_inc(s_ld[s], 16)

            @block.tensor
            def _(pe):
                pe.sem_inc(s_y, 2 * NK)
                pe.wait_ge(s_row, 64)
                with pe.Fori(0, NE // 2) as i:
                    for s in range(2):
                        e = i * 2 + s
                        pe.wait_ge(s_ld[s], i * 32 + 32)
                        pe.wait_ge(s_bs, e + 1)
                        for f in range(KF):
                            for c in range(KD):
                                last = pe.matmul(pB[0][:, f:f + 1], w1s[s][:, c * FH + f * 128:c * FH + (f + 1) * 128],
                                                 lbs[:, ds(e * KD + c, 1)], start=(c == 0), stop=(c == KD - 1))
                        last.then_inc(s_bm, 1)
                        with pe.Fori(0, Q) as q:
                            n = e * Q + q
                            pe.wait_ge(s_gs, e * KD + KD)
                            for f in range(KF):
                                pe.wait_ge(s_ha, ha.freed(n * KF + f, 2))
                                for bank, a, m in ((pHa, 0, QA), (pHb, QA, QN - QA)):
                                    for c in range(KD):
                                        last = pe.matmul(bank[f % 2][:, 0:m],
                                                         w1s[s][:, c * FH + f * 128:c * FH + (f + 1) * 128],
                                                         YT[:, ds(q * QN + c * N + a, m)], start=(c == 0),
                                                         stop=(c == KD - 1))
                                last.then_inc(s_h, 1)
                            pe.wait_ge(s_ha, ha.done(n * KF + KF - 1))
                            for j in range(Q):
                                pe.wait_ge(s_yv, yv.freed(n * Q + j, 2) if j else n * Q + 2)
                                for f in range(KF):
                                    pe.matmul(pY[j % 2][0:P, 0:D], hT[:, f * QN + j * P:f * QN + (j + 1) * P],
                                              w2s[s][:, f * D:(f + 1) * D], start=(f == 0), stop=False)
                                pe.matmul(pY[j % 2][0:P, 0:D], C["ones"][0:1, 0:P], b2s[:, ds(e * D, D)],
                                          start=False, stop=True).then_inc(s_y, 1)

            @block.scalar
            def _(act):
                act.sem_inc(s_ha, 2)
                with act.Fori(0, NE // 2) as i:
                    for s in range(2):
                        e = i * 2 + s
                        act.wait_ge(s_bs, e + 2)
                        with act.Fori(0, Q) as q:
                            n = e * Q + q
                            for f in range(KF):
                                act.wait_ge(s_h, h.done(n * KF + f))
                                act.activation(hT[:, f * QN:f * QN + QA], pHa[f % 2][:, 0:QA], ACT.Gelu,
                                               bias=bc[s][:, f:f + 1])
                                act.activation(hT[:, f * QN + QA:(f + 1) * QN], pHb[f % 2][:, 0:QN - QA], ACT.Gelu,
                                               bias=bc[s][:, f:f + 1]).then_inc(s_ha, 1)

            @block.vector
            def _(v):
                v.sem_inc(s_bs, 1)
                v.sem_inc(s_yv, 2)
                v.wait_ge(s_row, 64)
                with v.Fori(0, NE // 2) as i:
                    for s in range(2):
                        e = i * 2 + s
                        v.wait_ge(s_bm, e + 1)
                        v.tensor_tensor(bc[s][:], pB[0][:, 0:KF], b1s[:, ds(e * KF, KF)], ALU.add).then_inc(s_bs, 1)
                        for c in range(KD):
                            v.tensor_scalar(w1s[s][:, c * FH:(c + 1) * FH], w1s[s][:, c * FH:(c + 1) * FH],
                                            gs[:, ds(e * KD + c, 1)], None, ALU.mult).then_inc(s_gs, 1)
                        with v.Fori(0, Q) as q:
                            for j in range(Q):
                                k = (e * Q + q) * Q + j
                                t = q * Q + j
                                v.wait_ge(s_y, y.done(k))
                                v.wait_ge(s_yv, yv.freed(k, 1))
                                v.scalar_tensor_tensor(X[:, ds(t * D, D)], pY[j % 2][0:P, 0:D],
                                                       gates[:, ds(t * NE + e, 1)], X[:, ds(t * D, D)], ALU.mult,
                                                       ALU.add).then_inc(s_yv, 1)
                v.wait_ge(s_yv, NE * NK + 2)


def ffn1(nc, C, X, rstd, nbias, dr):
    with ExitStack() as st:
        sb = lambda n, s, d=F32: st.enter_context(nc.sbuf_tensor(f"f1_{n}", s, d))
        gates, YT = sb("gates", [P, T * NE]), sb("YT", [128, KD * N])
        with ExitStack() as s2:
            sc = lambda n, s: s2.enter_context(nc.sbuf_tensor(f"f1_{n}", s, F32))
            Y, logits, gw, gb = sc("Y", [P, T * D]), sc("logits", [P, T * NE]), sc("gw", [128, KD * NE]), sc("gb", [1, NE])
            load_many(nc, [(gw[:].rearrange("p (c f) -> p c f", c=KD), dr["Wr"].rearrange("(c p) f -> p c f", p=128)),
                           (gb[:], dr["br"].unsqueeze(0))])
            row_stats(nc, X, rstd, nbias, 1e-5)
            project(nc, C, X, rstd, nbias, keep=Y, w=gw, F=NE, brow=gb[:], out=logits)
            gates1(nc, C, logits, gates)
            row_stats(nc, Y, rstd, nbias, 1e-5)
            project(nc, C, Y, rstd, nbias, keepT=YT)
        experts1(nc, C, YT, gates, dr["W1"].rearrange("e d f -> (e d) f"), dr["b1T"], dr["gT"], dr["bT"],
                 dr["W2"].rearrange("e f d -> (e f) d"), dr["b2"], X)


F2 = 264
S2 = NH * HD + NH


def edge_attention(nc, C, lew, ateT, EA):
    with Phase(nc, "eatt") as ph:
        s_in, s_z, s_bc, s_mm, s_ev = (ph.sem(n) for n in ("in", "z", "bc", "mm", "ev"))
        le = ph.sb("le", [HD, NH * EF])
        at = ph.sb("at", [HD, NH])
        ab = ph.sb("ab", [HD, NH * 128])
        pE = ph.ps("pE", 1)
        with nc.Block() as block:

            @block.sync
            def _(sp):
                sp.dma_start(le[:].rearrange("p (h f) -> p h f", h=NH), lew.rearrange("(h p) f -> p h f", p=HD)).then_inc(s_in, 16)
                sp.dma_start(at[:], ateT).then_inc(s_in, 16)

            @block.vector
            def _(v):
                v.wait_ge(s_in, 32)
                v.tensor_copy(ab[:].rearrange("p (h m) -> p h m", h=NH), over(at[:], [HD, NH, 128])).then_inc(s_bc, 1)
                v.wait_ge(s_mm, 1)
                v.tensor_copy(EA[:], pE[0][:, 0:NH * EF]).then_inc(s_ev, 1)
                v.wait_ge(s_ev, 1)

            @block.tensor
            def _(pe):
                pe.wait_ge(s_in, 32)
                pe.wait_ge(s_bc, 1)
                for h in range(NH):
                    last = pe.matmul(pE[0][:, h * EF:(h + 1) * EF], ab[:, h * 128:(h + 1) * 128],
                                     le[:, h * EF:(h + 1) * EF], start=True, stop=True)
                last.then_inc(s_mm, 1)


def gnn2_weights(nc, lw, lwT, asT, adT, W):
    with Phase(nc, "w2") as ph:
        s_in, s_z, s_mm, s_ev = (ph.sem(n) for n in ("in", "z", "mm", "ev"))
        nat = ph.sb("nat", [HD, NH * D])
        at = ph.sb("at", [HD, 2 * NH])
        pW = ph.ps("pW", KD)
        Wv = W[:].rearrange("p (c f) -> p c f", c=KD)
        with nc.Block() as block:

            @block.sync
            def _(sp):
                sp.dma_start(nat[:].rearrange("p (h d) -> p h d", h=NH), lw.rearrange("(h p) d -> p h d", p=HD)).then_inc(s_in, 16)
                sp.dma_start(at[:, 0:NH], asT).then_inc(s_in, 16)
                sp.dma_start(at[:, NH:2 * NH], adT).then_inc(s_in, 16)
                sp.dma_start(Wv[:, :, 0:D], lwT.rearrange("(c p) f -> p c f", p=128)).then_inc(s_in, 16)
                sp.wait_ge(s_in, 64)

            @block.tensor
            def _(pe):
                pe.wait_ge(s_in, 64)
                for c in range(KD):
                    for j in range(2 * NH):
                        h = j % NH
                        last = pe.matmul(pW[c][:, j:j + 1], nat[:, h * D + c * 128:h * D + (c + 1) * 128],
                                         at[:, j:j + 1], start=True, stop=True)
                    last.then_inc(s_mm, 1)

            @block.vector
            def _(v):
                v.wait_ge(s_mm, KD)
                v.wait_ge(s_in, 64)
                for c in range(KD):
                    v.tensor_copy(Wv[:, c, D:F2], pW[c][:, 0:2 * NH]).then_inc(s_ev, 1)
                v.wait_ge(s_ev, KD)


def gnn2_maxima(nc, C, hdr, blk_i, tscore, eat, U, smax):
    R = 8
    RP = 4
    with Phase(nc, "max2") as ph:
        s_cur, s_u, s_copy, s_msk, s_mm, s_red, s_max = (
            ph.sem(n) for n in ("cur", "u", "copy", "msk", "mm", "red", "max"))
        s_g = [ph.pool_dma_sem(f"g{i}") for i in range(R)]
        cur = ph.sb("cur", [128, R], I32)
        G = ph.ring("G", R, [128, NH])
        pen = ph.ring("pen", 4, [128, P])
        msk = ph.ring("msk", 4, [128, NH * P])
        top = ph.ring("top", 2, [P, NH])
        us8 = ph.sb("us8", [128, R * NH])
        pS = ph.ps("pS", RP)
        cu, us, ms, mm, rd, mx = Count(s_cur), Count(s_u, R), Count(s_msk, R), Count(s_mm, R), Count(s_red, R), Count(s_max, R)
        with nc.Block() as block:

            @block.gpsimd
            def _(pool):
                with pool.Fori(0, NT // R) as i:
                    for u in range(R):
                        k = i * R + u
                        pool.wait_ge(s_cur, cu.done(k))
                        pool.nop(nofuse=True)
                        pool.indirect_dma_start(out=G[u][:], out_offset=None, in_=tscore,
                                                in_offset=bass.IndirectOffsetOnAxis(ap=cur[:, u:u + 1], axis=0)
                                                ).then_inc(s_g[u], 16)

            @block.scalar
            def _(act):
                act.sem_inc(s_msk, R)

                for u in range(R):
                    act.activation(cur[:, u:u + 1], hdrx(hdr, u), ACT.Copy).then_inc(s_cur, 1)
                with act.Fori(0, NT // R) as i:
                    for u in range(R):
                        k = i * R + u
                        act.wait_ge(s_u, us.done(k))
                        act.wait_ge(s_mm, mm.freed(k, 4))
                        for h in range(NH):
                            last = act.activation(msk[u % 4][:, h * P:(h + 1) * P], pen[u % 4][:], ACT.Identity,
                                                  bias=us8[:, u * NH + h:u * NH + h + 1])
                        last.then_inc(s_msk, 1)
                        act.activation(cur[:, u:u + 1], hdrx(hdr, k + R), ACT.Copy).then_inc(s_cur, 1)

            @block.tensor
            def _(pe):
                pe.sem_inc(s_mm, R)
                with pe.Fori(0, NT // R) as i:
                    for u in range(R):
                        k = i * R + u
                        pe.wait_ge(s_msk, ms.done(k))
                        pe.wait_ge(s_red, rd.freed(k, RP))
                        for h in range(NH):
                            last = pe.transpose(pS[u % RP][0:P, h * 128:(h + 1) * 128], msk[u % 4][:, h * P:(h + 1) * P],
                                                C["ident"][:])
                        last.then_inc(s_mm, 1)

            @block.vector
            def _(v):
                v.sem_inc(s_u, R)
                v.sem_inc(s_red, R)
                v.sem_inc(s_max, R)

                def prepare(i, k, u):
                    v.wait_ge(s_msk, ms.freed(k, 4))
                    v.tensor_scalar(pen[u % 4][:], C["nodes"][:], hdr[:, ds(k * HB + DL1, 1)], -BIG,
                                    ALU.not_equal, ALU.mult)
                    v.wait_ge(s_g[u], i * 16 + 16)
                    v.tensor_tensor(us8[:, u * NH:(u + 1) * NH], G[u][:], eat[:, ds(k * NH, NH)],
                                    ALU.add).then_inc(s_u, 1)

                regs = [v.alloc_register(f"max2_block{u}") for u in range(R)]

                def fold(k, u, b):
                    v.wait_ge(s_mm, mm.done(k))
                    v.tensor_reduce(top[u % 2][:], pS[u % RP][0:P, :].rearrange("p (h e) -> p h e", h=NH), AX,
                                    ALU.max).then_inc(s_red, 1)
                    v.wait_ge(s_red, rd.done(k))
                    v.wait_ge(s_max, mx.freed(k, 1))
                    a = smax[:, ds(b * NH, NH)]
                    v.tensor_tensor(a, top[u % 2][:], a, ALU.max).then_inc(s_max, 1)

                def group(i, last):
                    blocks = blocks_of(v, regs, blk_i, i * R)
                    for u in range(R):
                        if u + LAG < R:
                            prepare(i, i * R + u + LAG, u + LAG)
                            if u + LAG == R - 1:
                                v.wait_ge(s_u, us.done(i * R + R - 1))
                                v.tensor_copy(U[:, ds(i * R * NH, R * NH)], us8[:]).then_inc(s_copy, 1)
                                v.wait_ge(s_copy, i + 1)
                        elif not last:
                            prepare(i + 1, i * R + u + LAG, u + LAG - R)
                        fold(i * R + u, u, blocks[u])

                for u in range(LAG):
                    prepare(0, u, u)
                with v.Fori(0, NT // R - 1) as i:
                    group(i, False)
                group(NT // R - 1, True)
                v.wait_ge(s_max, NT + R)


def hdrx(hdr, k):
    return hdr[:, ds(k * HB + SRC, 1)].bitcast(I32)


def gnn2_spread(nc, C, hdr, blk_i, sd, SD):
    R = 4
    G = 8
    TA, OA = 2, 3
    W = 2 * NH
    with Phase(nc, "spread2") as ph:
        s_oh, s_tr, s_ot, s_mm, s_sd = (ph.sem(n) for n in ("oh", "tr", "ot", "mm", "sd"))
        OH = ph.ring("OH", R, [128, P])
        OT = ph.ring("OT", R, [P, 128])
        pT, pD = ph.ps("pT", R), ph.ps("pD", 2)
        oh, tr, ot, mm = Count(s_oh), Count(s_tr, R), Count(s_ot, R), Count(s_mm, R)
        with nc.Block() as block:

            @block.vector
            def _(v):
                v.sem_inc(s_sd, 2)

                def prepare(k, u):
                    v.wait_ge(s_tr, tr.freed(k, R))
                    v.tensor_scalar(OH[u][:], C["nodes"][:], hdr[:, ds(k * HB + DL1, 1)], None, ALU.is_equal).then_inc(s_oh, 1)

                for u in range(OA):
                    prepare(u, u)
                with v.Fori(0, NT // G) as i:
                    for u in range(G):
                        k = i * G + u
                        prepare(k + OA, (u + OA) % R)
                        if u % R == R - 1:
                            v.wait_ge(s_mm, mm.done(k))
                            v.tensor_copy(SD[:, ds((k - (R - 1)) * W, R * W)], pD[u // R][:, 0:R * W]).then_inc(s_sd, 1)
                v.wait_ge(s_sd, NT // R + 2)
                v.wait_ge(s_oh, NT + OA)

            @block.tensor
            def _(pe):
                pe.sem_inc(s_tr, R)
                pe.sem_inc(s_mm, R)

                def transpose(k, u):
                    pe.wait_ge(s_oh, oh.done(k))
                    pe.wait_ge(s_ot, ot.freed(k, R))
                    pe.transpose(pT[u][0:P, 0:128], OH[u][:], C["ident"][:]).then_inc(s_tr, 1)

                regs = [pe.alloc_register(f"spread2_block{u}") for u in range(G)]
                for u in range(TA):
                    transpose(u, u)
                with pe.Fori(0, NT // G) as i:
                    blocks = blocks_of(pe, regs, blk_i, i * G)
                    for u in range(G):
                        k = i * G + u
                        transpose(k + TA, (u + TA) % R)
                        pe.wait_ge(s_ot, ot.done(k))
                        if u % R == 0:
                            pe.wait_ge(s_sd, i * 2 + 1 + u // R)
                        pe.matmul(pD[u // R][:, u % R * W:(u % R + 1) * W], OT[u % R][:], sd[:, ds(blocks[u] * W, W)],
                                  start=True, stop=True).then_inc(s_mm, 1)

            @block.scalar
            def _(act):
                act.sem_inc(s_ot, R)

                def copy(k, u):
                    act.wait_ge(s_tr, tr.done(k))
                    act.wait_ge(s_mm, mm.freed(k, R))
                    act.activation(OT[u][:], pT[u][0:P, 0:128], ACT.Copy).then_inc(s_ot, 1)

                with act.Fori(0, NT // G) as i:
                    for u in range(G):
                        copy(i * G + u, u % R)
                for u in range(TA):
                    copy(NT + u, (NT + u) % R)


def gnn2_weigh(nc, U, SD, ex):
    with Phase(nc, "weigh2") as ph:
        s_ch, s_v, s_e = ph.sem("ch"), ph.sem("v"), ph.sem("e")
        n = NT * NH
        u3 = U[:].rearrange("p (t h) -> p t h", h=NH)
        d3 = SD[:].rearrange("p (t h) -> p t h", h=2 * NH)
        x3 = ex[:, 0:n].rearrange("p (t h) -> p t h", h=NH)
        with nc.Block() as block:

            @block.vector
            def _(v):
                ch = Chain(v, s_ch)
                ch(v.tensor_tensor(x3, u3, d3[:, :, 0:NH], ALU.add))
                ch(v.scalar_tensor_tensor(x3, x3, 0.2, x3, ALU.mult, ALU.max))
                ch(v.tensor_tensor(x3, x3, d3[:, :, NH:2 * NH], ALU.subtract))
                ch(v.tensor_scalar(x3, x3, 0.0, None, ALU.min))
                ch(v.memset(ex[:, n:], 0.0))
                v.sem_inc(s_v, 1)

            @block.scalar
            def _(act):
                act.wait_ge(s_v, 1)
                act.activation(ex[:, 0:n], ex[:, 0:n], ACT.Exp).then_inc(s_e, 1)
                act.wait_ge(s_e, 1)


def gnn2_prepare(nc, tab, smax):
    with Phase(nc, "prep2") as ph:
        s = ph.sem("s")
        t3 = tab[:].rearrange("p (t f) -> p t f", f=F2)
        with nc.Block() as block:

            @block.vector
            def _(v):
                v.tensor_copy(smax[:].rearrange("p (t h) -> p t h", h=NH), t3[:, :, D:D + NH]).then_inc(s, 1)
                v.wait_ge(s, 1)


def gnn2_own(nc, tab, smax, sd, acc):
    with Phase(nc, "own2") as ph:
        s_ch, s_v, s_e, s_cp = ph.sem("ch"), ph.sem("v"), ph.sem("e"), ph.sem("cp")
        own = ph.sb("own", [P, T * NH])
        t3 = tab[:].rearrange("p (t f) -> p t f", f=F2)
        m3 = smax[:].rearrange("p (t h) -> p t h", h=NH)
        sd3 = sd[:].rearrange("p (t h) -> p t h", h=2 * NH)
        o3 = own[:].rearrange("p (t h) -> p t h", h=NH)
        a3 = acc[:].rearrange("p (t s) -> p t s", s=S2)
        with nc.Block() as block:

            @block.vector
            def _(v):
                ch = Chain(v, s_ch)
                ch(v.tensor_copy(sd3[:, :, 0:NH], t3[:, :, D + NH:F2]))
                ch(v.tensor_tensor(m3, m3, sd3[:, :, 0:NH], ALU.add))
                ch(v.scalar_tensor_tensor(sd3[:, :, NH:2 * NH], m3, 0.2, m3, ALU.mult, ALU.max))
                ch(v.tensor_tensor(o3, t3[:, :, D:D + NH], sd3[:, :, 0:NH], ALU.add))
                ch(v.scalar_tensor_tensor(o3, o3, 0.2, o3, ALU.mult, ALU.max))
                ch(v.tensor_tensor(o3, o3, sd3[:, :, NH:2 * NH], ALU.subtract))
                v.sem_inc(s_v, 1)
                v.wait_ge(s_e, 1)
                for h in range(NH):
                    ch(v.tensor_tensor(a3[:, :, h * HD:(h + 1) * HD], t3[:, :, h * HD:(h + 1) * HD],
                                       over(o3[:, :, h], [P, T, HD]), ALU.mult))
                ch(v.tensor_copy(a3[:, :, NH * HD:S2], o3))

            @block.scalar
            def _(act):
                act.wait_ge(s_v, 1)
                act.activation(own[:], own[:], ACT.Exp).then_inc(s_e, 1)


def gnn2_sum(nc, C, hdr, blk_i, table, ex, acc):
    R = 8
    RP = 4
    with Phase(nc, "sum2") as ph:
        s_cur, s_oh, s_w, s_mm, s_acc = (ph.sem(n) for n in ("cur", "oh", "w", "mm", "acc"))
        s_g = [ph.pool_dma_sem(f"g{i}") for i in range(R)]
        cur = ph.sb("cur", [128, R], I32)
        G = ph.ring("G", R, [128, D])
        OH = ph.ring("OH", RP, [128, P])
        Wt = ph.ring("Wt", RP, [128, S2])
        pS = ph.ps("pS", RP)
        cu, wt, mm, ac = Count(s_cur), Count(s_w, R), Count(s_mm, R), Count(s_acc, R)
        with nc.Block() as block:

            @block.gpsimd
            def _(pool):
                with pool.Fori(0, NT // R) as i:
                    for u in range(R):
                        k = i * R + u
                        pool.wait_ge(s_cur, cu.done(k))
                        pool.nop(nofuse=True)
                        pool.indirect_dma_start(out=G[u][:], out_offset=None, in_=table,
                                                in_offset=bass.IndirectOffsetOnAxis(ap=cur[:, u:u + 1], axis=0)
                                                ).then_inc(s_g[u], 16)

            @block.scalar
            def _(act):
                act.sem_inc(s_w, R)
                for u in range(R - 1):
                    act.activation(cur[:, u:u + 1], hdrx(hdr, u), ACT.Copy).then_inc(s_cur, 1)
                with act.Fori(0, NT // R) as i:
                    for u in range(R):
                        k = i * R + u
                        act.wait_ge(s_w, wt.freed(k, 1))
                        act.wait_ge(s_oh, k * 3 + R)
                        c = (u - 1) % R
                        act.activation(cur[:, c:c + 1], hdrx(hdr, k + R - 1), ACT.Copy).then_inc(s_cur, 1)
                        act.wait_ge(s_g[u], i * 16 + 16)
                        act.wait_ge(s_mm, mm.freed(k, RP))
                        for h in range(NH // 2):
                            last = act.activation(Wt[u % RP][:, h * HD:(h + 1) * HD], G[u][:, h * HD:(h + 1) * HD],
                                                  ACT.Copy, scale=ex[:, ds(k * NH + h, 1)])
                        last.then_inc(s_w, 1)

            @block.vector
            def _(v):
                v.sem_inc(s_acc, R)
                v.sem_inc(s_oh, R)

                def prepare(k, u, n):
                    v.wait_ge(s_mm, mm.freed(k, RP))
                    v.tensor_scalar(OH[u % RP][:], C["nodes"][:], hdr[:, ds(k * HB + DL1, 1)], None, ALU.is_equal).then_inc(s_oh, 1)
                    v.tensor_copy(Wt[u % RP][:, NH * HD:S2], ex[:, ds(k * NH, NH)]).then_inc(s_oh, 1)
                    h = NH // 2
                    v.wait_ge(s_g[u], n)
                    v.tensor_tensor(Wt[u % RP][:, h * HD:NH * HD].rearrange("p (h f) -> p h f", f=HD),
                                    G[u][:, h * HD:NH * HD].rearrange("p (h f) -> p h f", f=HD),
                                    over(ex[:, ds(k * NH + h, h)], [128, h, HD]), ALU.mult).then_inc(s_oh, 1)

                for u in range(LAG):
                    prepare(u, u, 16)

                regs = [v.alloc_register(f"sum2_block{u}") for u in range(R)]

                def group(i, last):
                    blocks = blocks_of(v, regs, blk_i, i * R)
                    for u in range(R):
                        k = i * R + u
                        if u + LAG < R:
                            prepare(k + LAG, u + LAG, i * 16 + 16)
                        elif not last:
                            prepare(k + LAG, u + LAG - R, i * 16 + 32)
                        v.wait_ge(s_mm, mm.done(k))
                        v.wait_ge(s_acc, ac.freed(k, 1))
                        a = acc[:, ds(blocks[u] * S2, S2)]
                        v.tensor_tensor(a, pS[u % RP][0:P, 0:S2], a, ALU.add).then_inc(s_acc, 1)

                with v.Fori(0, NT // R - 1) as i:
                    group(i, False)
                group(NT // R - 1, True)
                v.wait_ge(s_acc, NT + R)

            @block.tensor
            def _(pe):
                pe.sem_inc(s_mm, R)
                with pe.Fori(0, NT // R) as i:
                    for u in range(R):
                        k = i * R + u
                        pe.wait_ge(s_oh, k * 3 + 3 + R)
                        pe.wait_ge(s_w, wt.done(k))
                        pe.wait_ge(s_acc, ac.freed(k, RP))
                        pe.matmul(pS[u % RP][0:P, 0:S2], OH[u % RP][:], Wt[u % RP][:], start=True, stop=True).then_inc(s_mm, 1)


def gnn2_update(nc, acc, brow, X):
    with Phase(nc, "upd2") as ph:
        s_ch = ph.sem("ch")
        den = ph.sb("den", [P, T * NH])
        a3 = acc[:].rearrange("p (t s) -> p t s", s=S2)
        x3 = X[:].rearrange("p (t d) -> p t d", d=D)
        d3 = den[:].rearrange("p (t h) -> p t h", h=NH)
        with nc.Block() as block:

            @block.vector
            def _(v):
                ch = Chain(v, s_ch)
                ch(v.tensor_scalar(d3, a3[:, :, NH * HD:S2], 1e-12, None, ALU.add))
                ch(v.reciprocal(den[:], den[:]))
                for h in range(NH):
                    m = a3[:, :, h * HD:(h + 1) * HD]
                    ch(v.tensor_tensor(m, m, over(d3[:, :, h], [P, T, HD]), ALU.mult))
                ch(v.tensor_tensor(x3, x3, a3[:, :, 0:D], ALU.add))
                ch(v.tensor_tensor(x3, x3, brow[:].unsqueeze(1).to_broadcast([P, T, D]), ALU.add))


def gnn2(nc, C, hdr, blk_i, X, rstd, nbias, dr, sorted_rows, table, tscore):
    with ExitStack() as st:
        sb = lambda n, s: st.enter_context(nc.sbuf_tensor(f"g2_{n}", s, F32))
        tab, W, brow = sb("tab", [P, T * F2]), sb("W", [128, KD * F2]), sb("brow", [P, D])
        eat, U, SD = sb("eat", [128, NT * NH]), sb("U", [128, NT * NH]), sb("SD", [128, NT * 2 * NH])
        smax, sd, acc, ex = sb("smax", [P, T * NH]), sb("sd", [P, T * 2 * NH]), sb("acc", [P, T * S2]), sb("ex", [128, NTL * NH])
        gnn2_weights(nc, dr["lin_W"], dr["lin_WT"], dr["asT"], dr["adT"], W)
        row_stats(nc, X, rstd, nbias, 1e-5)
        project(nc, C, X, rstd, nbias, w=W, F=F2, out=tab)
        t3 = tab[:].rearrange("p (t f) -> p t f", f=F2)
        load_many(nc, [(table.rearrange("(t p) f -> p t f", p=P), t3[:, :, 0:D]),
                       (tscore.rearrange("(t p) f -> p t f", p=P), t3[:, :, D:D + NH]),
                       (brow[:], dr["bias"].unsqueeze(0).to_broadcast([P, D])),
                       (eat[:].rearrange("p (t h) -> p t h", h=NH),
                        sorted_rows.rearrange("(t p) c -> p t c", p=LANES)[:, :, EAT:EAT + NH])])
        gnn2_prepare(nc, tab, smax)
        gnn2_maxima(nc, C, hdr, blk_i, tscore, eat, U, smax)
        gnn2_own(nc, tab, smax, sd, acc)
        gnn2_spread(nc, C, hdr, blk_i, sd, SD)
        gnn2_weigh(nc, U, SD, ex)
        gnn2_sum(nc, C, hdr, blk_i, table, ex, acc)
        gnn2_update(nc, acc, brow, X)


def experts2(nc, C, YT, gates, wts, cols, bo, X):
    with Phase(nc, "exp2") as ph:
        s_row, s_ch, s_sq, s_dv, s_h, s_ha, s_y, s_yv = (ph.sem(n) for n in ("row", "ch", "sq", "dv", "h", "ha", "y", "yv"))
        s_ld = ph.sems_of("ld", 2)
        cs = {n: ph.sb(n, [128, NE * KD]) for n in cols}
        eps = 0.001
        bos = ph.sb("bo", [1, NE * D])
        ws = [ph.ring(f"w{l}", 2, [128, KD * D]) for l in range(3)]
        hid = [ph.sb(f"h{l}", [128, KD * QN]) for l in range(2)]
        pHa, pHb, pY = ph.ps("pHa", 2), ph.ps("pHb", 2), ph.ps("pY", 3)
        NK = Q * Q
        HS = 2 * KD
        h, ha, y, yv = Count(s_h), Count(s_ha, 2), Count(s_y, 2 * NK), Count(s_yv, 3)
        with nc.Block() as block:

            @block.sync
            def _(sp):
                for n in cols:
                    sp.dma_start(cs[n][:], cols[n]).then_inc(s_row, 16)
                sp.dma_start(bos[:], bo.rearrange("e d -> (e d)").unsqueeze(0)).then_inc(s_row, 16)
                with sp.Fori(0, NE // 2) as i:
                    for s in range(2):
                        e = i * 2 + s
                        sp.wait_ge(s_y, e * NK + NK)
                        for l in range(3):
                            sp.dma_start(ws[l][s][:].rearrange("p (c f) -> p c f", c=KD),
                                         wts[l][ds(e * D, D), :].rearrange("(c p) f -> p c f", p=128)).then_inc(s_ld[s], 16)

            @block.tensor
            def _(pe):
                pe.sem_inc(s_y, 2 * NK)
                pe.wait_ge(s_row, 16 * (len(cols) + 1))
                with pe.Fori(0, NE // 2) as i:
                    for s in range(2):
                        e = i * 2 + s
                        with pe.Fori(0, Q) as q:
                            n = e * Q + q
                            pe.wait_ge(s_ld[s], i * 48 + 48)
                            for l in range(2):
                                if l:
                                    pe.wait_ge(s_ha, ha.done(n * HS + KD - 1))
                                for f in range(KD):
                                    pe.wait_ge(s_ha, ha.freed(n * HS + l * KD + f, 2))
                                    for bank, a, m in ((pHa, 0, QA), (pHb, QA, QN - QA)):
                                        for c in range(KD):
                                            rhs = (YT[:, ds(q * QN + c * N + a, m)] if l == 0
                                                   else hid[0][:, c * QN + a:c * QN + a + m])
                                            last = pe.matmul(bank[f % 2][:, 0:m],
                                                             ws[l][s][:, c * D + f * 128:c * D + (f + 1) * 128], rhs,
                                                             start=(c == 0), stop=(c == KD - 1))
                                    last.then_inc(s_h, 1)
                            pe.wait_ge(s_ha, ha.done(n * HS + HS - 1))
                            for j in range(Q):
                                pe.wait_ge(s_yv, n * Q + j + 1 + 3 - (2 if j < 2 else 3))
                                for c in range(KD):
                                    pe.matmul(pY[j % 3][0:P, 0:D], hid[1][:, c * QN + j * P:c * QN + (j + 1) * P],
                                              ws[2][s][:, c * D:(c + 1) * D], start=(c == 0), stop=False)
                                pe.matmul(pY[j % 3][0:P, 0:D], C["ones"][0:1, 0:P], bos[:, ds(e * D, D)],
                                          start=False, stop=True).then_inc(s_y, 1)

            @block.scalar
            def _(act):
                act.wait_ge(s_dv, 1)
                for l in "12":
                    act.activation(cs["v" + l][:], cs["v" + l][:], ACT.Sqrt).then_inc(s_sq, 1)
                act.sem_inc(s_ha, 2)
                act.wait_ge(s_dv, 2)
                with act.Fori(0, NE // 2) as i:
                    for s in range(2):
                        e = i * 2 + s
                        with act.Fori(0, Q) as q:
                            n = e * Q + q
                            for l in range(2):
                                for f in range(KD):
                                    act.wait_ge(s_h, h.done(n * HS + l * KD + f))
                                    g, b = (cs[x + "12"[l]][:, ds(e * KD + f, 1)] for x in ("g", "b"))
                                    act.activation(hid[l][:, f * QN:f * QN + QA], pHa[f % 2][:, 0:QA], ACT.Relu,
                                                   bias=b, scale=g)
                                    act.activation(hid[l][:, f * QN + QA:(f + 1) * QN], pHb[f % 2][:, 0:QN - QA],
                                                   ACT.Relu, bias=b, scale=g).then_inc(s_ha, 1)

            @block.vector
            def _(v):
                ch = Chain(v, s_ch)
                v.wait_ge(s_row, 16 * (len(cols) + 1))
                for l in "12":
                    ch(v.tensor_scalar(cs["v" + l][:], cs["v" + l][:], eps, None, ALU.add))
                v.sem_inc(s_dv, 1)
                v.wait_ge(s_sq, 2)
                for l in "12":
                    ch(v.reciprocal(cs["v" + l][:], cs["v" + l][:]))
                    ch(v.tensor_tensor(cs["g" + l][:], cs["g" + l][:], cs["v" + l][:], ALU.mult))
                    ch(v.tensor_tensor(cs["b" + l][:], cs["b" + l][:], cs["m" + l][:], ALU.subtract))
                    ch(v.tensor_tensor(cs["b" + l][:], cs["b" + l][:], cs["g" + l][:], ALU.mult))
                    ch(v.tensor_tensor(cs["b" + l][:], cs["b" + l][:], cs["be" + l][:], ALU.add))
                v.sem_inc(s_dv, 1)
                v.sem_inc(s_yv, 3)
                with v.Fori(0, NE // 2) as i:
                    for s in range(2):
                        e = i * 2 + s
                        with v.Fori(0, Q) as q:
                            for j in range(Q):
                                k = (e * Q + q) * Q + j
                                t = q * Q + j
                                v.wait_ge(s_y, y.done(k))
                                v.wait_ge(s_yv, yv.freed(k, 1))
                                v.scalar_tensor_tensor(X[:, ds(t * D, D)], pY[j % 3][0:P, 0:D],
                                                       gates[:, ds(t * NE + e, 1)], X[:, ds(t * D, D)], ALU.mult,
                                                       ALU.add).then_inc(s_yv, 1)
                v.wait_ge(s_yv, NE * NK + 3)


def ffn2(nc, C, X, rstd, nbias, dr):
    with ExitStack() as st:
        sb = lambda n, s, d=F32: st.enter_context(nc.sbuf_tensor(f"f2_{n}", s, d))
        gates, YT = sb("gates", [P, T * NE]), sb("YT", [128, KD * N])
        with ExitStack() as s2:
            sc = lambda n, s: s2.enter_context(nc.sbuf_tensor(f"f2_{n}", s, F32))
            logits, gw, gb = sc("logits", [P, T * NE]), sc("gw", [128, KD * NE]), sc("gb", [1, NE])
            load_many(nc, [(gw[:].rearrange("p (c f) -> p c f", c=KD), dr["Wr"].rearrange("(c p) f -> p c f", p=128)),
                           (gb[:], dr["br"].unsqueeze(0))])
            row_stats(nc, X, rstd, nbias, 1e-5)
            project(nc, C, X, rstd, nbias, w=gw, F=NE, brow=gb[:], out=logits, keepT=YT)
            gates2(nc, logits, gates)
        cols = {n: dr[n + "T"] for n in ("b1", "g1", "be1", "m1", "v1", "b2", "g2", "be2", "m2", "v2")}
        experts2(nc, C, YT, gates, [dr[n].rearrange("e d f -> (e d) f") for n in ("W1", "W2", "Wo")], cols, dr["bo"], X)


R3 = 16
C3 = 64
INV3 = 1.0 / float(np.sqrt(np.float32(3.0)))


def normalise_by_axis(nc, src, rstd, nbias, out):
    with Phase(nc, "norm3") as ph:
        s_a = ph.sem("a")
        with nc.Block() as block:

            @block.scalar
            def _(act):
                with act.Fori(0, T // 5) as i:
                    for u in range(5):
                        k = i * 5 + u
                        act.activation(out[:, ds(k * D, C3)], src[:, ds(k * D, C3)], ACT.Identity,
                                       bias=nbias[:, ds(k, 1)], scale=rstd[:, ds(k, 1)]).then_inc(s_a, 1)
                        act.activation(out[:, ds(k * D + C3, 3 * C3)].rearrange("p (a c) -> p a c", a=3),
                                       src[:, ds(k * D + C3, 3 * C3)].rearrange("p (c a) -> p a c", a=3), ACT.Identity,
                                       bias=nbias[:, ds(k, 1)], scale=rstd[:, ds(k, 1)]).then_inc(s_a, 1)
                act.wait_ge(s_a, 2 * T)


def block_weights(nc, W, F, parts):
    with Phase(nc, "wblock") as ph:
        s_z, s_in = ph.sem("z"), ph.sem("in")
        with nc.Block() as block:

            @block.vector
            def _(v):
                v.memset(W[:], 0.0).then_inc(s_z, 1)

            @block.sync
            def _(sp):
                sp.wait_ge(s_z, 1)
                for col, w0, w1 in parts:
                    for b in range(4):
                        a = (b // 2) * F + col + b * C3
                        sp.dma_start(W[(b % 2) * C3:(b % 2 + 1) * C3, a:a + C3], w0 if b == 0 else w1).then_inc(s_in, 16)
                sp.wait_ge(s_in, 16 * 4 * len(parts))


def gnn3_sum(nc, C, hdr, blk_i, table, sorted_rows, dr, acc):
    B = 8
    H = B // 2
    GROUPS = NT // B
    with Phase(nc, "sum3") as ph:
        s_w, s_z, s_rbf, s_cur, s_oh, s_rt, s_re, s_h, s_he, s_tp, s_q0, s_q, s_msg, s_mm, s_acc = (
            ph.sem(n) for n in ("w", "z", "rbf", "cur", "oh", "rt", "re", "h", "he", "tp", "q0", "q", "msg", "mm",
                                "acc"))
        s_g = [ph.pool_dma_sem(f"g{i}") for i in range(B)]
        W1 = ph.sb("W1", [128, H * 128])
        Wm = [ph.sb(f"Wm{j}", [128, 128]) for j in range(2)]
        W4 = ph.sb("W4", [128, 4 * C3])
        rbf = ph.sb("rbf", [128, B * R3])
        rT = ph.sb("rT", [B * R3, 128])
        hs = [ph.sb(f"hs{j}", [2 * C3, H * 128]) for j in range(3)]
        cur = ph.sb("cur", [128, B], I32)
        G = ph.ring("G", B, [128, D])
        OH = ph.ring("OH", B, [128, P])
        dl = ph.sb("dl", [128, B])
        pq = ph.ring("pq", 2, [128, 2 * C3])
        t3 = ph.ring("t3", 2, [128, 3 * C3])
        qq = ph.ring("qq", B, [128, C3])
        ms = ph.ring("ms", 4, [128, D])
        pR, pH, pT, pS = ph.ps("pR"), ph.ps("pH"), ph.ps("pT", 4), ph.ps("pS", 2)
        STEPS = 5
        cu, mm, ac, tp, q0, msg = (Count(s_cur), Count(s_mm, B), Count(s_acc, B), Count(s_tp),
                                       Count(s_q0), Count(s_msg, B))
        rows = sorted_rows.rearrange("(t p) c -> p t c", p=LANES)

        def radial(i):
            return rows[:, ds(i * B, B), RBF:RBF + R3]

        with nc.Block() as block:

            @block.sync
            def _(sp):
                sp.wait_ge(s_z, 1)
                for t in range(B):
                    j, half = t % H, t // H
                    sp.dma_start(W1[t * R3:(t + 1) * R3, j * 128 + half * C3:j * 128 + (half + 1) * C3],
                                 dr["M1"]).then_inc(s_w, 16)
                for half in range(2):
                    r = slice(half * C3, (half + 1) * C3)
                    for j in range(2):
                        sp.dma_start(Wm[j][r, r], dr[f"M{j + 2}"]).then_inc(s_w, 16)
                    sp.dma_start(W4[r, :], dr["M4"]).then_inc(s_w, 16)
                sp.dma_start(rbf[:].rearrange("p (t c) -> p t c", t=B), radial(0)).then_inc(s_rbf, 16)
                with sp.Fori(0, GROUPS - 1) as i:
                    sp.wait_ge(s_rt, i + 1)
                    sp.dma_start(rbf[:].rearrange("p (t c) -> p t c", t=B), radial(i + 1)).then_inc(s_rbf, 16)

            @block.gpsimd
            def _(pool):
                pool.sem_inc(s_oh, 1)
                with pool.Fori(0, GROUPS) as i:
                    for u in range(B):
                        k = i * B + u
                        pool.wait_ge(s_cur, cu.done(k))
                        pool.nop(nofuse=True)
                        pool.indirect_dma_start(out=G[u][:], out_offset=None, in_=table,
                                                in_offset=bass.IndirectOffsetOnAxis(ap=cur[:, u:u + 1], axis=0)
                                                ).then_inc(s_g[u], 16)
                        if u == 0:
                            pool.wait_ge(s_oh, i * (B + 1) + 1)
                            pool.tensor_copy(dl[:], hdr[:, ds(i * B * HB, B * HB)].rearrange(
                                "p (t c) -> p t c", c=HB)[:, :, DL1]).then_inc(s_oh, 1)
                            pool.wait_ge(s_oh, i * (B + 1) + 2)
                        pool.wait_ge(s_mm, mm.freed(k, B))
                        pool.nop(nofuse=True)
                        pool.tensor_scalar(OH[u][:], C["nodes"][:], dl[:, u:u + 1], None,
                                           ALU.is_equal).then_inc(s_oh, 1)

            @block.scalar
            def _(act):
                def network(i):
                    act.wait_ge(s_rt, i + 1)
                    act.activation(rT[:], pR[0][:, 0:128], ACT.Copy).then_inc(s_re, 1)
                    for j in range(3):
                        act.wait_ge(s_h, i * 3 + j + 1)
                        act.activation(hs[j][:], pH[0][:], ACT.Silu).then_inc(s_he, 1)
                        yield

                def fetch(k, u):
                    act.wait_ge(s_msg, msg.freed(k, B))
                    act.activation(cur[:, u:u + 1], hdrx(hdr, k), ACT.Copy).then_inc(s_cur, 1)

                def first_part(k, u):
                    act.wait_ge(s_g[u], (k - u) * 2 + 16)
                    act.activation(qq[u][:], G[u][:, C3:2 * C3], ACT.Copy,
                                   scale=hdr[:, ds(k * HB + SH + 1, 1)]).then_inc(s_q0, 1)

                AHEAD = 2
                for u in range(B):
                    fetch(u, u)
                for _ in network(0):
                    pass
                for u in range(AHEAD):
                    first_part(u, u)

                def group(i, last):
                    steps = iter(()) if last else network(i + 1)
                    for u in range(B):
                        if u + AHEAD < B or not last:
                            first_part(i * B + u + AHEAD, (u + AHEAD) % B)
                        if u in (1, 2, 4):
                            next(steps, None)
                        if not last:
                            fetch(i * B + B + u, u)

                with act.Fori(0, GROUPS - 1) as i:
                    group(i, False)
                group(GROUPS - 1, True)

            @block.tensor
            def _(pe):
                def network(i):
                    pe.wait_ge(s_rbf, i * 16 + 16)
                    pe.transpose(pR[0][:, 0:128], rbf[:], C["ident"][:]).then_inc(s_rt, 1)
                    pe.wait_ge(s_re, i + 1)
                    for j in range(H):
                        last = pe.matmul(pH[0][:, j * 128:(j + 1) * 128], W1[:, j * 128:(j + 1) * 128], rT[:], start=True,
                                         stop=True)
                    last.then_inc(s_h, 1)
                    yield
                    for j in range(2):
                        pe.wait_ge(s_he, i * 3 + j + 1)
                        pe.matmul(pH[0][:], Wm[j][:], hs[j][:], start=True, stop=True).then_inc(s_h, 1)
                        yield

                def path_weights(k, u):
                    half, c = u // H, u % H
                    r = slice(half * C3, (half + 1) * C3)
                    pe.matmul(pT[u % 4][:, 0:4 * C3], hs[2][r, c * 128:(c + 1) * 128], W4[r, :], start=True,
                              stop=True).then_inc(s_tp, 1)

                def group(i, last):
                    steps = iter(()) if last else network(i + 1)
                    for u in range(B):
                        k = i * B + u
                        pe.wait_ge(s_msg, msg.done(k))
                        pe.wait_ge(s_oh, i * (B + 1) + 1 + 2 + u)
                        pe.wait_ge(s_acc, ac.freed(k, 2))
                        pe.matmul(pS[u % 2][0:P, 0:D], OH[u][:], ms[u % 4][:], start=True, stop=True).then_inc(s_mm, 1)
                        if u < 4:
                            path_weights(k + 4, u + 4)
                        if u in (0, 1, 3):
                            next(steps, None)
                        if u >= 4 and not last:
                            if u == 4:
                                pe.wait_ge(s_he, i * 3 + 6)
                            path_weights(k + 4, u - 4)

                pe.wait_ge(s_w, 16 * (B + 6))
                pe.sem_inc(s_mm, B)
                for _ in network(0):
                    pass
                pe.wait_ge(s_he, 3)
                for u in range(4):
                    path_weights(u, u)
                with pe.Fori(0, GROUPS - 1) as i:
                    group(i, False)
                group(GROUPS - 1, True)

            @block.vector
            def _(v):
                for w in [W1, *Wm]:
                    v.memset(w[:], 0.0)
                v.memset(acc[:], 0.0).then_inc(s_z, 1)
                v.wait_ge(s_z, 1)
                v.sem_inc(s_acc, B)
                v.sem_inc(s_msg, B)

                regs = [v.alloc_register(f"sum3_block{u}") for u in range(B)]

                def message(k, u):
                    x, q, p, w3, m = G[u], qq[u], pq[u % 2], t3[u % 2], ms[u % 4]
                    sh = [hdr[:, ds(k * HB + SH + a, 1)] for a in range(4)]
                    tw = [pT[u % 4][:, a * C3:(a + 1) * C3] for a in range(4)]
                    ax = [x[:, (a + 1) * C3:(a + 2) * C3] for a in range(3)]
                    base = k * STEPS
                    v.wait_ge(s_mm, mm.freed(k, 4))
                    v.wait_ge(s_msg, msg.freed(k, 2))
                    v.wait_ge(s_q0, q0.done(k))
                    v.scalar_tensor_tensor(q[:], ax[1], sh[2], q[:], ALU.mult, ALU.add).then_inc(s_q, 1)
                    v.wait_ge(s_tp, tp.done(k))
                    v.tensor_tensor(p[:].rearrange("p (a c) -> p a c", a=2),
                                    pT[u % 4][:, 0:2 * C3].rearrange("p (a c) -> p a c", a=2),
                                    x[:, 0:C3].unsqueeze(1).to_broadcast([128, 2, C3]), ALU.mult).then_inc(s_q, 1)
                    v.wait_ge(s_q, base + 1)
                    v.scalar_tensor_tensor(q[:], ax[2], sh[3], q[:], ALU.mult, ALU.add).then_inc(s_q, 1)
                    v.scalar_tensor_tensor(w3[:].rearrange("p (a c) -> p a c", a=3),
                                           x[:, C3:].rearrange("p (a c) -> p a c", a=3), sh[0],
                                           tw[2].unsqueeze(1).to_broadcast([128, 3, C3]), ALU.mult,
                                           ALU.mult).then_inc(s_q, 1)
                    v.wait_ge(s_q, base + 3)
                    v.scalar_tensor_tensor(q[:], q[:], INV3, tw[3], ALU.mult, ALU.mult).then_inc(s_q, 1)
                    v.wait_ge(s_q, base + 4)
                    for a in range(3):
                        v.scalar_tensor_tensor(m[:, (a + 1) * C3:(a + 2) * C3], p[:, C3:], sh[a + 1],
                                               w3[:, a * C3:(a + 1) * C3], ALU.mult, ALU.add)
                    v.wait_ge(s_q, base + 5)
                    v.scalar_tensor_tensor(m[:, 0:C3], p[:, 0:C3], sh[0], q[:], ALU.mult, ALU.add).then_inc(s_msg, 1)

                def add(k, u, b):
                    v.wait_ge(s_mm, mm.done(k))
                    v.wait_ge(s_acc, ac.freed(k, 1))
                    a = acc[:, ds(b * D, D)]
                    v.tensor_tensor(a, pS[u % 2][0:P, 0:D], a, ALU.add).then_inc(s_acc, 1)

                def group(i, last):
                    blocks = blocks_of(v, regs, blk_i, i * B)
                    for u in range(B):
                        if u < B - 1 or not last:
                            message(i * B + u + 1, (u + 1) % B)
                        add(i * B + u, u, blocks[u])

                message(0, 0)
                with v.Fori(0, GROUPS - 1) as i:
                    group(i, False)
                group(GROUPS - 1, True)
                v.wait_ge(s_acc, NT + B)


def gnn3_body(nc, A, B0, cw, dw, vv, tmp):
    with Phase(nc, "poly3") as ph:
        s_ch = ph.sem("ch")
        a3 = A[:].rearrange("p (t d) -> p t d", d=D)
        b3 = B0[:].rearrange("p (t d) -> p t d", d=D)
        v3 = vv[:].rearrange("p (t c) -> p t c", c=C3)
        t3 = tmp[:].rearrange("p (t c) -> p t c", c=C3)
        sh = [P, T, C3]
        row = lambda w, j: w[:, j * C3:(j + 1) * C3].unsqueeze(1).to_broadcast(sh)
        with nc.Block() as block:

            @block.vector
            def _(v):
                ch = Chain(v, s_ch)
                A0, O0 = a3[:, :, 0:C3], b3[:, :, 0:C3]
                ax = [a3[:, :, (a + 1) * C3:(a + 2) * C3] for a in range(3)]
                ch(v.tensor_tensor(v3, ax[0], ax[0], ALU.mult))
                for a in (1, 2):
                    ch(v.tensor_tensor(t3, ax[a], ax[a], ALU.mult))
                    ch(v.tensor_tensor(v3, v3, t3, ALU.add))
                ch(v.tensor_tensor(t3, A0, row(cw, 3), ALU.mult))
                ch(v.tensor_tensor(t3, t3, row(cw, 1), ALU.add))
                ch(v.tensor_tensor(t3, t3, A0, ALU.mult))
                ch(v.tensor_tensor(t3, t3, row(cw, 0), ALU.add))
                ch(v.tensor_tensor(O0, v3, row(cw, 4), ALU.mult))
                ch(v.tensor_tensor(t3, t3, O0, ALU.add))
                ch(v.tensor_tensor(t3, t3, A0, ALU.mult))
                ch(v.tensor_tensor(O0, v3, row(cw, 2), ALU.mult))
                ch(v.tensor_tensor(O0, t3, O0, ALU.add))
                ch(v.tensor_tensor(t3, A0, row(dw, 2), ALU.mult))
                ch(v.tensor_tensor(t3, t3, row(dw, 1), ALU.add))
                ch(v.tensor_tensor(t3, t3, A0, ALU.mult))
                ch(v.tensor_tensor(v3, v3, row(dw, 3), ALU.mult))
                ch(v.tensor_tensor(t3, t3, v3, ALU.add))
                ch(v.tensor_tensor(t3, t3, row(dw, 0), ALU.add))
                for a in range(3):
                    ch(v.tensor_tensor(b3[:, :, (a + 1) * C3:(a + 2) * C3], ax[a], t3, ALU.mult))


def gnn3_norm(nc, C, o, g0, be0, g1, X):
    with Phase(nc, "norm3b") as ph:
        s_ch, s_r, s_m, s_v, s_q = (ph.sem(n) for n in ("ch", "r", "m", "v", "q"))
        red = ph.sb("red", [P, 2 * C3])
        mean = ph.sb("mean", [P, C3])
        sc = ph.sb("sc", [P, 2 * C3])
        sq = ph.sb("sq", [P, T * D])
        pM, pV = ph.ps("pM"), ph.ps("pV")
        o3 = o[:].rearrange("p (t d) -> p t d", d=D)
        q3 = sq[:].rearrange("p (t d) -> p t d", d=D)
        x3 = X[:].rearrange("p (t d) -> p t d", d=D)
        sh = [P, T, C3]
        bc = lambda a: a.unsqueeze(1).to_broadcast(sh)
        with nc.Block() as block:

            @block.vector
            def _(v):
                ch = Chain(v, s_ch)
                v.tensor_reduce(red[:, 0:C3], o3[:, :, 0:C3].rearrange("p t c -> p c t"), AX, ALU.add).then_inc(s_r, 1)
                v.wait_ge(s_m, 1)
                ch(v.tensor_scalar(mean[:], pM[0][0:P, 0:C3], 1.0 / N, None, ALU.mult))
                ch(v.tensor_tensor(o3[:, :, 0:C3], o3[:, :, 0:C3], bc(mean[:]), ALU.subtract))
                ch(v.tensor_tensor(sq[:], o[:], o[:], ALU.mult))
                ch(v.tensor_reduce(red[:, 0:C3], q3[:, :, 0:C3].rearrange("p t c -> p c t"), AX, ALU.add))
                for a in (1, 2):
                    ch(v.tensor_tensor(q3[:, :, C3:2 * C3], q3[:, :, C3:2 * C3], q3[:, :, (a + 1) * C3:(a + 2) * C3], ALU.add))
                ch(v.tensor_reduce(red[:, C3:], q3[:, :, C3:2 * C3].rearrange("p t c -> p c t"), AX, ALU.add))
                v.sem_inc(s_r, 1)
                v.wait_ge(s_m, 2)
                ch(v.tensor_scalar(sc[:, 0:C3], pV[0][0:P, 0:C3], 1.0 / N, 1e-5, ALU.mult, ALU.add))
                ch(v.tensor_scalar(sc[:, C3:], pV[0][0:P, C3:2 * C3], 1.0 / (3 * N), 1e-5, ALU.mult, ALU.add))
                v.sem_inc(s_v, 1)
                v.wait_ge(s_q, 1)
                ch(v.reciprocal(sc[:], sc[:]))
                ch(v.tensor_tensor(sc[:, 0:C3], sc[:, 0:C3], g0[:], ALU.mult))
                ch(v.tensor_tensor(sc[:, C3:], sc[:, C3:], g1[:], ALU.mult))
                for b in range(4):
                    ob = o3[:, :, b * C3:(b + 1) * C3]
                    ch(v.tensor_tensor(ob, ob, bc(sc[:, 0:C3] if b == 0 else sc[:, C3:]), ALU.mult))
                    if b == 0:
                        ch(v.tensor_tensor(ob, ob, bc(be0[:]), ALU.add))
                        xb = x3[:, :, 0:C3]
                    else:
                        xb = x3[:, :, C3:].rearrange("p t (c a) -> p t a c", a=3)[:, :, b - 1, :]
                    ch(v.tensor_tensor(xb, xb, ob, ALU.add))

            @block.tensor
            def _(pe):
                pe.wait_ge(s_r, 1)
                pe.matmul(pM[0][0:P, 0:C3], C["ones"][0:P, 0:P], red[:, 0:C3], start=True, stop=True).then_inc(s_m, 1)
                pe.wait_ge(s_r, 2)
                pe.matmul(pV[0][0:P, 0:2 * C3], C["ones"][0:P, 0:P], red[:], start=True, stop=True).then_inc(s_m, 1)

            @block.scalar
            def _(act):
                act.wait_ge(s_v, 1)
                act.activation(sc[:], sc[:], ACT.Sqrt).then_inc(s_q, 1)


def gnn3(nc, C, hdr, blk_i, X, rstd, nbias, dr, sorted_rows, table):
    with ExitStack() as st:
        sb = lambda n, s: st.enter_context(nc.sbuf_tensor(f"g3_{n}", s, F32))
        acc, scc = sb("acc", [P, T * D]), sb("scc", [P, T * D])
        row_stats(nc, X, rstd, nbias, 1e-5)
        with ExitStack() as s2:
            sc = lambda n, s: s2.enter_context(nc.sbuf_tensor(f"g3_{n}", s, F32))
            Y, Wu = sc("Y", [P, T * D]), sc("Wu", [128, KD * D])
            normalise_by_axis(nc, X, rstd, nbias, Y)
            plain(nc, rstd, nbias)
            block_weights(nc, Wu, D, [(0, dr["W_up0"], dr["W_up1"])])
            project(nc, C, Y, rstd, nbias, w=Wu, F=D, out=acc)
            store_table(nc, acc, table, D)
            block_weights(nc, Wu, D, [(0, dr["Wsc0"], dr["Wsc1"])])
            project(nc, C, Y, rstd, nbias, w=Wu, F=D, out=scc)
        gnn3_sum(nc, C, hdr, blk_i, table, sorted_rows, dr, acc)
        with ExitStack() as s2:
            sc = lambda n, s: s2.enter_context(nc.sbuf_tensor(f"g3_{n}", s, F32))
            A, Wu = sc("A", [P, T * D]), sc("Wv", [128, KD * D])
            cw, dw = sc("cw", [P, 5 * C3]), sc("dw", [P, 4 * C3])
            vv, tmp = sc("vv", [P, T * C3]), sc("tmp", [P, T * C3])
            g0, be0, g1 = sc("g0", [P, C3]), sc("be0", [P, C3]), sc("g1", [P, C3])
            load_many(nc, [(cw[:], dr["Wc0T"].rearrange("j c -> (j c)").unsqueeze(0).to_broadcast([P, 5 * C3])),
                           (dw[:], dr["Wc1T"].rearrange("j c -> (j c)").unsqueeze(0).to_broadcast([P, 4 * C3]))]
                      + [(t[:], dr[n].unsqueeze(0).to_broadcast([P, C3]))
                         for t, n in ((g0, "gamma0"), (be0, "beta0"), (g1, "gamma1"))])
            block_weights(nc, Wu, D, [(0, dr["W_lin0"], dr["W_lin1"])])
            project(nc, C, acc, rstd, nbias, w=Wu, F=D, out=A)
            gnn3_body(nc, A, acc, cw, dw, vv, tmp)
            block_weights(nc, Wu, D, [(0, dr["WB0"], dr["WB1"])])
            project(nc, C, acc, rstd, nbias, w=Wu, F=D, add_to=scc)
            gnn3_norm(nc, C, scc, g0, be0, g1, X)


H3 = 8
G3 = 64
IN3 = H3 * G3
HP = H3 // 2


def ffn3_weights(nc, C, WxT, bxT, Wsl, bsl, temp, WS, bS):
    with Phase(nc, "w3") as ph:
        s_in, s_mm, s_ch, s_t = ph.sem("in"), ph.sem("mm"), ph.sem("ch"), ph.sem("t")
        wx = ph.sb("wx", [G3, H3 * D])
        bx = ph.sb("bx", [G3, H3])
        wl = ph.sb("wl", [G3, G3])
        bl = ph.sb("bl", [1, G3])
        tr = ph.sb("tr", [128, H3])
        pW, pB = ph.ps("pW", KD), ph.ps("pB")
        with nc.Block() as block:

            @block.sync
            def _(sp):
                sp.dma_start(wx[:].rearrange("p (h d) -> p h d", h=H3), WxT.rearrange("(h p) d -> p h d", p=G3)).then_inc(s_in, 16)
                sp.dma_start(bx[:], bxT).then_inc(s_in, 16)
                sp.dma_start(wl[:], Wsl).then_inc(s_in, 16)
                sp.dma_start(bl[:], bsl.unsqueeze(0)).then_inc(s_in, 16)
                sp.dma_start(tr[:], temp.unsqueeze(0).to_broadcast([128, H3])).then_inc(s_in, 16)

            @block.tensor
            def _(pe):
                pe.wait_ge(s_in, 80)
                for h in range(H3):
                    for c in range(KD):
                        pe.matmul(pW[c][:, h * G3:(h + 1) * G3], wx[:, h * D + c * 128:h * D + (c + 1) * 128], wl[:],
                                  start=True, stop=True)
                    pe.matmul(pB[0][0:1, h * G3:(h + 1) * G3], bx[:, h:h + 1], wl[:], start=True, stop=False)
                    last = pe.matmul(pB[0][0:1, h * G3:(h + 1) * G3], C["ones"][0:1, 0:1], bl[:], start=False, stop=True)
                last.then_inc(s_mm, 1)

            @block.vector
            def _(v):
                ch = Chain(v, s_ch)
                v.wait_ge(s_in, 80)
                ch(v.tensor_scalar(tr[:], tr[:], 0.1, 5.0, ALU.max, ALU.min))
                ch(v.reciprocal(tr[:], tr[:]))
                v.wait_ge(s_mm, 1)
                for c in range(KD):
                    ch(v.tensor_tensor(WS[:, c * IN3:(c + 1) * IN3].rearrange("p (h g) -> p h g", h=H3),
                                       pW[c][:, :].rearrange("p (h g) -> p h g", h=H3),
                                       over(tr[:], [128, H3, G3]), ALU.mult))
                ch(v.tensor_tensor(bS[:].rearrange("p (h g) -> p h g", h=H3),
                                   pB[0][0:1, :].rearrange("p (h g) -> p h g", h=H3),
                                   over(tr[0:1, :], [1, H3, G3]), ALU.mult))


def softmax3(nc, L, pairs):
    rows, runs = pairs
    with Phase(nc, "soft3") as ph:
        s_ch, s_v, s_e = ph.sem("ch"), ph.sem("v"), ph.sem("e")
        m = ph.sb("m", [rows, runs])
        l3 = L[:].rearrange("p (r g) -> p r g", g=G3)
        sh = [rows, runs, G3]
        with nc.Block() as block:

            @block.vector
            def _(v):
                ch = Chain(v, s_ch)
                ch(v.tensor_reduce(m[:], l3, AX, ALU.max))
                ch(v.tensor_tensor(l3, l3, over(m[:], sh), ALU.subtract))
                v.sem_inc(s_v, 1)
                v.wait_ge(s_e, 1)
                ch(v.tensor_reduce(m[:], l3, AX, ALU.add))
                ch(v.reciprocal(m[:], m[:]))
                ch(v.tensor_tensor(l3, l3, over(m[:], sh), ALU.mult))

            @block.scalar
            def _(act):
                act.wait_ge(s_v, 1)
                act.activation(L[:], L[:], ACT.Exp).then_inc(s_e, 1)


def ffn3_tokens(nc, C, SW, FX, tok):
    with Phase(nc, "tok3") as ph:
        s_z, s_w, s_mm, s_ch, s_all = ph.sem("z"), ph.sem("w"), ph.sem("mm"), ph.sem("ch"), ph.sem("all")
        R = 5
        wt = ph.ring("wt", R, [P, IN3])
        zero = ph.sb("zero", [1, 128])
        rn = ph.sb("rn", [128, HP])
        pS = ph.ps("pS", HP)
        w, mm = Count(s_w), Count(s_mm, R)
        with nc.Block() as block:

            @block.scalar
            def _(act):
                with act.Fori(0, T // R) as i:
                    for u in range(R):
                        k = i * R + u
                        act.wait_ge(s_mm, mm.freed(k, R))
                        act.activation(wt[u][:], SW[:, ds(k * IN3, IN3)], ACT.Copy).then_inc(s_w, 1)

            @block.tensor
            def _(pe):
                pe.sem_inc(s_mm, R)
                pe.wait_ge(s_z, 1)
                for p in range(HP):
                    pe.matmul(pS[p][:, 0:128], zero[:], zero[:], start=True, stop=False, skip_group_check=True)
                    pe.matmul(pS[p][:, 128:129], zero[:], zero[:, 0:1], start=False, stop=False, skip_group_check=True)
                with pe.Fori(0, T // R) as i:
                    for u in range(R):
                        k = i * R + u
                        pe.wait_ge(s_w, w.done(k))
                        for p in range(HP):
                            lhs = wt[u][:, p * 128:(p + 1) * 128]
                            pe.matmul(pS[p][:, 0:128], lhs, FX[:, ds(k * IN3 + p * 128, 128)], start=False, stop=False,
                                      skip_group_check=True)
                            last = pe.matmul(pS[p][:, 128:129], lhs, C["ones"][0:P, 0:1], start=False, stop=False,
                                             skip_group_check=True)
                        last.then_inc(s_mm, 1)
                for p in range(HP):
                    last = pe.matmul(pS[p][:, 0:129], zero[:], C["zeros"][0:1, 0:129], start=False, stop=True,
                                     skip_group_check=True)
                last.then_inc(s_all, 1)

            @block.vector
            def _(v):
                ch = Chain(v, s_ch)
                v.memset(zero[:], 0.0).then_inc(s_z, 1)
                v.wait_ge(s_all, 1)
                for p in range(HP):
                    ch(v.tensor_scalar(rn[:, p:p + 1], pS[p][:, 128:129], 1e-5, None, ALU.add))
                ch(v.reciprocal(rn[:], rn[:]))
                for p in range(HP):
                    for b in (0, 64):
                        ch(v.tensor_scalar(tok[b:b + 64, p * G3:(p + 1) * G3], pS[p][b:b + 64, b:b + 64],
                                           rn[b:b + 64, p:p + 1], None, ALU.mult))


def ffn3_attention(nc, C, tok, wq, wk, wv, wo, V):
    SCALE = float(G3) ** -0.5
    with Phase(nc, "att3") as ph:
        s_in, s_pe, s_ch, s_v, s_a = ph.sem("in"), ph.sem("pe"), ph.sem("ch"), ph.sem("v"), ph.sem("a")
        ws = [ph.sb(n, [G3, G3]) for n in ("wq", "wk", "wv")]
        wos = ph.sb("wo", [128, HP * D])
        tokT = ph.sb("tokT", [G3, HP * 128])
        qk = ph.ring("qk", 2, [G3, HP * 128])
        vs, osl = ph.sb("vs", [128, HP * G3]), ph.sb("os", [128, HP * G3])
        at = ph.sb("at", [128, HP * G3])
        bd, bdT = ph.sb("bd", [128, HP * 128]), ph.sb("bdT", [128, HP * 128])
        m = ph.sb("m", [128, HP])
        pA, pB, pV = ph.ps("pA", 1), ph.ps("pB", 3), ph.ps("pV", HP)
        a3 = at[:].rearrange("p (h g) -> p h g", h=HP)
        sh = [128, HP, G3]

        def blocks(dst, src):
            d3 = dst[:].rearrange("p (h g) -> p h g", h=HP)
            s3 = src[:].rearrange("p (h g) -> p h g", h=HP)
            for b in (0, 64):
                wide = (d3 if d3.shape[2] == 128 else s3)
                yield (d3[b:b + 64, :, b:b + 64] if wide is d3 else d3[b:b + 64],
                       s3[b:b + 64, :, b:b + 64] if wide is s3 else s3[b:b + 64])

        with nc.Block() as block:

            @block.sync
            def _(sp):
                for t, d in zip(ws, (wq, wk, wv)):
                    sp.dma_start(t[:], d).then_inc(s_in, 16)
                sp.dma_start(wos[:].rearrange("p (c d) -> p c d", c=HP), wo.rearrange("(c p) d -> p c d", p=128)).then_inc(s_in, 16)

            @block.tensor
            def _(pe):
                pe.wait_ge(s_in, 64)
                for p in range(HP):
                    last = pe.transpose(pA[0][0:G3, p * 128:(p + 1) * 128], tok[:, p * G3:(p + 1) * G3], C["ident"][:])
                last.then_inc(s_pe, 1)
                pe.wait_ge(s_v, 1)
                for j in range(2):
                    pe.matmul(pB[j][0:G3, :], ws[j][:], tokT[:], start=True, stop=True)
                for p in range(HP):
                    last = pe.matmul(pB[2][:, p * G3:(p + 1) * G3], tokT[:, p * 128:(p + 1) * 128], ws[2][:],
                                     start=True, stop=True)
                last.then_inc(s_pe, 1)
                pe.wait_ge(s_v, 2)
                for p in range(HP):
                    c = slice(p * 128, (p + 1) * 128)
                    last = pe.matmul(pA[0][:, c], qk[0][:, c], qk[1][:, c], start=True, stop=True)
                last.then_inc(s_pe, 1)
                pe.wait_ge(s_v, 4)
                for p in range(HP):
                    c = slice(p * 128, (p + 1) * 128)
                    last = pe.transpose(pB[0][:, c], bd[:, c], C["ident"][:])
                last.then_inc(s_pe, 1)
                pe.wait_ge(s_v, 5)
                for p in range(HP):
                    last = pe.matmul(pB[1][:, p * G3:(p + 1) * G3], bdT[:, p * 128:(p + 1) * 128],
                                     vs[:, p * G3:(p + 1) * G3], start=True, stop=True)
                last.then_inc(s_pe, 1)
                pe.wait_ge(s_v, 6)
                for p in range(HP):
                    c = slice(p * 128, (p + 1) * 128)
                    last = pe.transpose(pB[2][:, c], bd[:, c], C["ident"][:])
                last.then_inc(s_pe, 1)
                pe.wait_ge(s_v, 7)
                for p in range(HP):
                    last = pe.matmul(pV[p][:, 0:D], bdT[:, p * 128:(p + 1) * 128], wos[:, p * D:(p + 1) * D],
                                     start=True, stop=True)
                last.then_inc(s_pe, 1)

            @block.scalar
            def _(act):
                act.wait_ge(s_v, 3)
                act.activation(at[:], at[:], ACT.Exp, scale=SCALE).then_inc(s_a, 1)

            @block.vector
            def _(v):
                ch = Chain(v, s_ch)
                ch(v.memset(bd[:], 0.0))
                v.wait_ge(s_pe, 1)
                ch(v.tensor_copy(tokT[:], pA[0][0:G3, :]))
                v.sem_inc(s_v, 1)
                v.wait_ge(s_pe, 2)
                for j in range(2):
                    ch(v.tensor_copy(qk[j][:], pB[j][0:G3, :]))
                ch(v.tensor_copy(vs[:], pB[2][:, 0:HP * G3]))
                v.sem_inc(s_v, 1)
                v.wait_ge(s_pe, 3)
                for o, i in blocks(at, pA[0]):
                    ch(v.tensor_copy(o, i))
                ch(v.tensor_reduce(m[:], a3, AX, ALU.max))
                ch(v.tensor_tensor(a3, a3, over(m[:], sh), ALU.subtract))
                v.sem_inc(s_v, 1)
                v.wait_ge(s_a, 1)
                ch(v.tensor_reduce(m[:], a3, AX, ALU.add))
                ch(v.reciprocal(m[:], m[:]))
                ch(v.tensor_tensor(a3, a3, over(m[:], sh), ALU.mult))
                for o, i in blocks(bd, at):
                    ch(v.tensor_copy(o, i))
                v.sem_inc(s_v, 1)
                v.wait_ge(s_pe, 4)
                ch(v.tensor_copy(bdT[:], pB[0][:]))
                v.sem_inc(s_v, 1)
                v.wait_ge(s_pe, 5)
                ch(v.tensor_copy(osl[:], pB[1][:, 0:HP * G3]))
                for o, i in blocks(bd, osl):
                    ch(v.tensor_copy(o, i))
                v.sem_inc(s_v, 1)
                v.wait_ge(s_pe, 6)
                ch(v.tensor_copy(bdT[:], pB[2][:]))
                v.sem_inc(s_v, 1)
                v.wait_ge(s_pe, 7)
                for p in range(HP):
                    ch(v.tensor_copy(V[:, p * D:(p + 1) * D], pV[p][:, 0:D]))


def ffn3(nc, C, X, rstd, nbias, dr):
    with ExitStack() as st:
        sb = lambda n, s: st.enter_context(nc.sbuf_tensor(f"f3_{n}", s, F32))
        SW, V, bo = sb("SW", [P, T * IN3]), sb("V", [128, HP * D]), sb("bo", [1, D])
        row_stats(nc, X, rstd, nbias, 1e-5)
        with ExitStack() as s2:
            sc = lambda n, s: s2.enter_context(nc.sbuf_tensor(f"f3_{n}", s, F32))
            FX, WS, bS = sc("FX", [P, T * IN3]), sc("WS", [128, KD * IN3]), sc("bS", [1, IN3])
            WF, bF, tok = sc("WF", [128, KD * IN3]), sc("bF", [1, IN3]), sc("tok", [128, HP * G3])
            load_many(nc, [(WF[:].rearrange("p (c f) -> p c f", c=KD), dr["W_fx"].rearrange("(c p) f -> p c f", p=128)),
                           (bF[:], dr["b_fx"].unsqueeze(0)), (bo[:], dr["b_out"].unsqueeze(0))])
            ffn3_weights(nc, C, dr["W_xT"], dr["b_xT"], dr["W_slice"], dr["b_slice"], dr["temperature"], WS, bS)
            project(nc, C, X, rstd, nbias, w=WS, F=IN3, brow=bS[:], out=SW)
            project(nc, C, X, rstd, nbias, w=WF, F=IN3, brow=bF[:], out=FX)
            softmax3(nc, SW, (P, T * H3))
            ffn3_tokens(nc, C, SW, FX, tok)
            ffn3_attention(nc, C, tok, dr["W_q"], dr["W_k"], dr["W_v"], dr["W_out"], V)
        plain(nc, rstd, nbias)
        project(nc, C, SW, rstd, nbias, w=V, F=D, brow=bo[:], add_to=X, kd=HP)


def store_result(nc, X, out):
    with Phase(nc, "result") as ph:
        s = ph.sem("stored")
        with nc.Block() as block:

            @block.sync
            def _(sp):
                sp.dma_start(out.rearrange("(t p) d -> p t d", p=P),
                             X[:].rearrange("p (t d) -> p t d", d=D)).then_inc(s, 16)
                sp.wait_ge(s, 16)


def gnn0(nc, C, hdr, blk_i, X, rstd, nbias, dis, dr, table):
    with ExitStack() as st:
        W = st.enter_context(nc.sbuf_tensor("g0_W", [128, KD * F0], F32))
        tab = st.enter_context(nc.sbuf_tensor("g0_tab", [P, T * F0], F32))
        gnn0_weights(nc, dr["W_forward"], dr["W_reverse"], dr["attnT"], dr["W_forwardT"], dr["W_reverseT"], W)
        row_stats(nc, X, rstd, nbias, 1e-5)
        project(nc, C, X, rstd, nbias, w=W, F=F0, out=tab)
        store_table(nc, tab, table, F0)
    with ExitStack() as st:
        acc = st.enter_context(nc.sbuf_tensor("g0_acc", [P, T * S0], F32))
        with ExitStack() as s2:
            M = s2.enter_context(nc.sbuf_tensor("g0_M", [128, NTL * H0], F32))
            ex = s2.enter_context(nc.sbuf_tensor("g0_ex", [128, NTL * NH], F32))
            gnn0_messages(nc, table, hdr, M)
            gnn0_softmax(nc, hdr, M, ex)
            gnn0_sum(nc, C, hdr, blk_i, M, ex, acc)
        gnn0_update(nc, acc, X, dis)


def program(nc, dr, out):
    def layer(prefix):
        return {n[len(prefix):]: a for n, a in dr.items() if n.startswith(prefix)}

    Phase.opened = Phase.pool_dma_sems = 0
    sorted_rows = nc.dram_tensor("sorted_rows", [NT * LANES, ROW], F32).ap()
    table0 = nc.dram_tensor("table0", [N, F0], F32).ap()
    table = nc.dram_tensor("table", [N, D], F32).ap()
    tscore = nc.dram_tensor("tscore", [N, NH], F32).ap()
    buf = nc.dram_tensor("buf", [BUF, D], F32).ap()
    ybuf = nc.dram_tensor("ybuf", [NE * ES, D], F32).ap()
    with ExitStack() as st:
        def sb(name, shape, dt=F32):
            return st.enter_context(nc.sbuf_tensor(name, shape, dt))

        C = {"ident": sb("ident", [128, 128]), "tri": sb("tri", [128, 128]), "ones": sb("ones", [128, 128]),
             "nodes": sb("nodes", [128, P]), "row": sb("row", [128, NT]), "zeros": sb("zeros", [1, 129])}
        X, dis = sb("X", [P, T * D]), sb("dis", [P, T])
        rstd, nbias = sb("rstd", [P, T]), sb("nbias", [P, T])
        load_constants(nc, dr["x"], X, C)
        with ExitStack() as edges:
            hdr = edges.enter_context(nc.sbuf_tensor("hdr", [128, NTX * HB], F32))
            blk_i = edges.enter_context(nc.sbuf_tensor("blk_i", [1, NT], I32))
            with ExitStack() as s2:
                slots = s2.enter_context(nc.sbuf_tensor("slots", [P, ET], I32))
                loc1 = s2.enter_context(nc.sbuf_tensor("loc1", [P, ET], F32))
                EA = s2.enter_context(nc.sbuf_tensor("EA", [128, NH * EF], F32))
                edge_attention(nc, C, dr["L2_gnn_lin_edge_W"], dr["L2_gnn_att_edgeT"], EA)
                sort_edges(nc, C, dr["dst"], sorted_rows, slots, loc1, blk_i)
                scatter_edges(nc, dr["src"], dr["edge_attr_2"], dr["edge_weight"], dr["edge_attr_4"],
                              dr["edge_attr_16"], dr["edge_attr_32"], EA, slots, loc1, sorted_rows)
            load_headers(nc, sorted_rows, hdr)
            gnn0(nc, C, hdr, blk_i, X, rstd, nbias, dis, layer("L0_gnn_"), table0)
            ffn0(nc, C, X, rstd, nbias, layer("L0_ffn_"), buf, ybuf)
            gnn1(nc, C, hdr, blk_i, X, dis, rstd, nbias, layer("L1_gnn_"), table)
            ffn1(nc, C, X, rstd, nbias, layer("L1_ffn_"))
            gnn2(nc, C, hdr, blk_i, X, rstd, nbias, layer("L2_gnn_"), sorted_rows, table, tscore)
            ffn2(nc, C, X, rstd, nbias, layer("L2_ffn_"))
            gnn3(nc, C, hdr, blk_i, X, rstd, nbias, layer("L3_gnn_"), sorted_rows, table)
        ffn3(nc, C, X, rstd, nbias, layer("L3_ffn_"))
        store_result(nc, X, out)


def columns(a):
    e, f = a.shape
    return a.reshape(e, f // 128, 128).transpose(2, 0, 1).reshape(128, -1)


def kernel(**inputs):
    import concourse.bacc as bacc
    from concourse.bass_utils import run_bass_kernel_spmd

    a = {n: np.asarray(v) for n, v in inputs.items()}
    g0 = {"W_forward": a["L0_gnn_W_forward"], "W_reverse": a["L0_gnn_W_reverse"],
          "W_forwardT": a["L0_gnn_W_forward"].T, "W_reverseT": a["L0_gnn_W_reverse"].T,
          "attnT": a["L0_gnn_attn_forward"][0].T}
    f0 = {n: a["L0_ffn_" + n] for n in ("gate_w", "gate_b", "w1", "w2", "b2")} | {"b1T": columns(a["L0_ffn_b1"])}
    g1 = {n: a["L1_gnn_" + n] for n in ("ln6_g", "ln6_b", "ln7_g", "ln7_b", "b6", "b7", "bp")} | {
        n: a["L1_gnn_" + n].T for n in ("W6", "W7", "Wp")}
    f1 = {n: a["L1_ffn_" + n] for n in ("Wr", "br", "W1", "W2", "b2")} | {
        "b1T": columns(a["L1_ffn_b1"]), "gT": columns(a["L1_ffn_ln_g"]), "bT": columns(a["L1_ffn_ln_b"])}
    g2 = {"lin_W": a["L2_gnn_lin_W"], "lin_WT": a["L2_gnn_lin_W"].T, "asT": a["L2_gnn_att_src"].T,
          "adT": a["L2_gnn_att_dst"].T, "bias": a["L2_gnn_bias"], "lin_edge_W": a["L2_gnn_lin_edge_W"],
          "att_edgeT": a["L2_gnn_att_edge"].T}
    f2 = {n: a["L2_ffn_" + n] for n in ("Wr", "br", "W1", "W2", "Wo", "bo")} | {
        n + "T": columns(a["L2_ffn_" + n]) for n in ("b1", "g1", "be1", "m1", "v1", "b2", "g2", "be2", "m2", "v2")}
    g3 = {n: a["L3_gnn_" + n] for n in ("W_up0", "W_up1", "M1", "M2", "M3", "M4", "W_lin0", "W_lin1", "Wsc0", "Wsc1",
                                        "WB0", "WB1", "gamma0", "beta0", "gamma1")} | {
        n + "T": a["L3_gnn_" + n].T for n in ("Wc0", "Wc1")}
    f3 = {n: a["L3_ffn_" + n] for n in ("W_fx", "b_fx", "W_slice", "b_slice", "W_q", "W_k", "W_v", "W_out", "b_out")} | {
        "W_xT": a["L3_ffn_W_x"].T, "b_xT": a["L3_ffn_b_x"].reshape(H3, G3).T,
        "temperature": a["L3_ffn_temperature"].reshape(H3)}
    laid = {n: a[n] for n in ("x", "src", "dst", "edge_attr_16", "edge_attr_2", "edge_attr_32", "edge_attr_4", "edge_weight")}
    for prefix, d in (("L0_gnn_", g0), ("L0_ffn_", f0), ("L1_gnn_", g1), ("L1_ffn_", f1),
                      ("L2_gnn_", g2), ("L2_ffn_", f2), ("L3_gnn_", g3), ("L3_ffn_", f3)):
        laid |= {prefix + n: v for n, v in d.items()}
    laid = {n: np.ascontiguousarray(v) for n, v in laid.items()}

    nc = bacc.Bacc("TRN2", target_bir_lowering=False, num_devices=1)
    dr = {n: nc.dram_tensor(f"in_{n}", v.shape, mybir.dt.from_np(v.dtype), kind="ExternalInput").ap()
          for n, v in laid.items()}
    out = nc.dram_tensor("out_x", (N, D), F32, kind="ExternalOutput").ap()
    program(nc, dr, out)
    r = run_bass_kernel_spmd(nc, [{f"in_{n}": v for n, v in laid.items()}], core_ids=[0])
    return r.results[0]["out_x"]
```

```python
from contextlib import ExitStack

import concourse.bass as bass
import numpy as np
from concourse import mybir

F32 = mybir.dt.float32
I32 = mybir.dt.int32
ALU = mybir.AluOpType
ACT = mybir.ActivationFunctionType
AX = mybir.AxisListType.X
ds = bass.ds

N = 3125
D = 256
T = 25
P = N // T
KD = D // 128
E = 53125
ET = E // P
LANES = 128
NT = 440
LAG = 2
NTL = NT + LAG
NTX = NT + 8
SRC, DL1, DIR, WGT, VALID = 0, 1, 2, 4, 5
HB = 10
SH, EAT, RBF = 6, 10, 16
ROW = 32
EF = 32
BIG = 1.0e30
ROUND = 12582912.0
NH = 4
HD = 64

assert E // LANES + T <= NT and P * T == N and ET * P == E and NT % 8 == 0


POOL_DMA_SEM_BASE = 100
SEM_BASE = 170


class Phase:

    opened = 0
    pool_dma_sems = 0

    def __init__(self, nc, name):
        Phase.opened += 1
        self.nc, self.name, self.stack = nc, f"{name}_{Phase.opened}", ExitStack()
        self.sems = 0

    def __enter__(self):
        self.stack.__enter__()
        return self

    def __exit__(self, *what):
        if what[0] is None:
            self.nc.all_engine_barrier(sems_to_clear=range(SEM_BASE, SEM_BASE + self.sems))
        self.stack.__exit__(*what)
        return False

    def sem(self, name):
        self.sems += 1
        return self.stack.enter_context(
            self.nc.semaphore(f"{self.name}_{name}", num=SEM_BASE + self.sems - 1))

    def sems_of(self, name, n):
        return [self.sem(f"{name}{i}") for i in range(n)]

    def pool_dma_sem(self, name):
        Phase.pool_dma_sems += 1
        return self.stack.enter_context(
            self.nc.semaphore(f"{self.name}_{name}", num=POOL_DMA_SEM_BASE + Phase.pool_dma_sems - 1))

    def sb(self, name, shape, dt=F32):
        return self.stack.enter_context(self.nc.sbuf_tensor(f"{self.name}_{name}", shape, dt))

    def ring(self, name, n, shape, dt=F32):
        return [self.sb(f"{name}{i}", shape, dt) for i in range(n)]

    def ps(self, name, n=1):
        return [self.stack.enter_context(self.nc.psum_tensor(f"{self.name}_{name}{i}", [128, 512], F32))
                for i in range(n)]


class Count:

    def __init__(self, sem, ahead=0):
        self.sem, self.ahead = sem, ahead

    def done(self, k):
        return k + 1 + self.ahead

    def freed(self, k, ring):
        return k + 1 - ring + self.ahead


class Chain:

    def __init__(self, eng, sem):
        self.eng, self.sem, self.n = eng, sem, 0

    def __call__(self, ins):
        self.n += 1
        ins.then_inc(self.sem, 1)
        self.eng.wait_ge(self.sem, self.n)

    def restart(self):
        self.eng.sem_clear(self.sem)
        self.n = 0


def blocks_of(eng, regs, table, k, top=T - 1):
    eng.load(regs, table[0:1, ds(k, len(regs))])
    return [eng.snap(r, min_val=0, max_val=top) for r in regs]


def over(ap, shape):
    return ap.unsqueeze(2).to_broadcast(shape)


def load_constants(nc, x, X, C):
    with Phase(nc, "setup") as ph:
        s_x, s_zero, s_made = ph.sem("x"), ph.sem("zero"), ph.sem("made")
        with nc.Block() as block:

            @block.sync
            def _(sp):
                sp.dma_start(X[:].rearrange("p (t d) -> p t d", d=D),
                             x.rearrange("(t p) d -> p t d", p=P)).then_inc(s_x, 16)
                sp.wait_ge(s_x, 16)

            @block.gpsimd
            def _(pool):
                pool.memset(C["ident"][:], 0.0).then_inc(s_zero, 1)
                pool.memset(C["tri"][:], 1.0).then_inc(s_zero, 1)
                pool.memset(C["ones"][:], 1.0).then_inc(s_zero, 1)
                pool.wait_ge(s_zero, 3)
                pool.affine_select(out=C["ident"][:], in_=C["ident"][:], compare_op=ALU.not_equal, fill=1.0,
                                   base=0, pattern=[[-1, 128]], channel_multiplier=1).then_inc(s_made, 1)
                pool.affine_select(out=C["tri"][:], in_=C["tri"][:], compare_op=ALU.is_gt, fill=0.0,
                                   base=0, pattern=[[1, 128]], channel_multiplier=-1).then_inc(s_made, 1)
                pool.iota(C["nodes"][:], [[1, P]], base=1, channel_multiplier=0,
                          allow_small_or_imprecise_dtypes=True).then_inc(s_made, 1)
                pool.iota(C["row"][:], [[1, NT]], base=0, channel_multiplier=0,
                          allow_small_or_imprecise_dtypes=True).then_inc(s_made, 1)
                pool.wait_ge(s_made, 4)


def sort_edges(nc, C, dst, sorted_rows, slots, loc1, blk_i):
    with Phase(nc, "rank") as ph:
        s_dst, s_fill, s_ch = ph.sem("dst"), ph.sem("fill"), ph.sem("ch")
        s_zero, s_tot, s_pref = ph.sem("zero"), ph.sem("tot"), ph.sem("pref")
        dst_i = ph.sb("dst_i", [P, ET], I32)
        dstf = ph.sb("dstf", [P, ET])
        blk = ph.sb("blk", [P, ET])
        eq = ph.sb("eq", [P, ET])
        cum = ph.sb("cum", [P, ET])
        slotf = ph.sb("slotf", [P, ET])
        zeros = ph.sb("zeros", [128, NT * ROW // 8])
        tot = ph.sb("tot", [P, T])
        tiles = ph.sb("tiles", [P, T])
        ends = ph.sb("ends", [P, T])
        base = ph.sb("base", [P, T])
        which = ph.sb("which", [1, NT])
        over_end = ph.sb("over_end", [T, NT])
        ps_pref, ps_all, ps_end, ps_which = ph.ps("pref"), ph.ps("all"), ph.ps("end"), ph.ps("which")
        zrows = sorted_rows.rearrange("(p r) c -> p (r c)", p=128)
        with nc.Block() as block:

            @block.sync
            def _(sp):
                sp.dma_start(dst_i[:], dst.rearrange("(p t) -> p t", p=P)).then_inc(s_dst, 16)
                sp.wait_ge(s_zero, 1)
                n = NT * ROW // 8
                for q in range(8):
                    sp.dma_start(zrows[:, q * n:(q + 1) * n], zeros[:]).then_inc(s_fill, 16)
                sp.wait_ge(s_fill, 8 * 16)

            @block.gpsimd
            def _(pool):
                pool.memset(zeros[:], 0.0).then_inc(s_zero, 1)

            @block.tensor
            def _(pe):
                pe.wait_ge(s_tot, 1)
                pe.matmul(ps_pref[0][0:P, 0:T], C["tri"][0:P, 0:P], tot[:], start=True, stop=True).then_inc(s_pref, 1)
                pe.matmul(ps_all[0][0:P, 0:T], C["ones"][0:P, 0:P], tot[:], start=True, stop=True).then_inc(s_pref, 1)
                pe.wait_ge(s_tot, 2)
                pe.matmul(ps_end[0][0:T, 0:1], ends[0:1, :], C["ones"][0:1, 0:1], start=True, stop=True).then_inc(s_pref, 1)
                pe.wait_ge(s_tot, 3)
                pe.matmul(ps_which[0][0:1, 0:NT], C["ones"][0:T, 0:1], over_end[:], start=True, stop=True).then_inc(s_pref, 1)

            @block.vector
            def _(v):
                ch = Chain(v, s_ch)
                v.wait_ge(s_dst, 16)
                ch(v.tensor_copy(dstf[:], dst_i[:]))
                ch(v.tensor_scalar(blk[:], dstf[:], float((P - 1) // 2), 1.0 / P, ALU.subtract, ALU.mult))
                ch(v.tensor_scalar(blk[:], blk[:], ROUND, ROUND, ALU.add, ALU.subtract))
                ch(v.scalar_tensor_tensor(loc1[:], blk[:], -float(P), dstf[:], ALU.mult, ALU.add))
                ch(v.tensor_scalar(loc1[:], loc1[:], 1.0, None, ALU.add))
                ch(v.memset(slotf[:], -1.0))
                with v.Fori(0, T) as b:
                    ch.restart()
                    ch(v.tensor_scalar(eq[:], blk[:], C["row"][0:P, ds(b, 1)], None, ALU.is_equal))
                    ch(v.tensor_reduce(tot[:, ds(b, 1)], eq[:], AX, ALU.add))
                v.sem_inc(s_tot, 1)
                ch.restart()
                v.wait_ge(s_pref, 2)
                ch(v.tensor_scalar(tiles[:], ps_all[0][0:P, 0:T], 1.0 / LANES, (LANES - 1) / 2.0 / LANES,
                                   ALU.mult, ALU.add))
                ch(v.tensor_scalar(tiles[:], tiles[:], ROUND, ROUND, ALU.add, ALU.subtract))
                ch(v.tensor_tensor_scan(ends[:], C["ones"][0:P, 0:1].to_broadcast([P, T]), tiles[:], 0.0,
                                        ALU.mult, ALU.add))
                v.sem_inc(s_tot, 1)
                ch(v.tensor_tensor(base[:], ends[:], tiles[:], ALU.subtract))
                ch(v.scalar_tensor_tensor(base[:], base[:], float(LANES), ps_pref[0][0:P, 0:T], ALU.mult, ALU.add))
                v.wait_ge(s_pref, 3)
                with v.Fori(0, T) as b:
                    ch.restart()
                    ch(v.tensor_scalar(eq[:], blk[:], C["row"][0:P, ds(b, 1)], None, ALU.is_equal))
                    ch(v.tensor_tensor_scan(cum[:], C["ones"][0:P, 0:1].to_broadcast([P, ET]), eq[:], 0.0, ALU.mult, ALU.add))
                    ch(v.scalar_tensor_tensor(cum[:], cum[:], base[:, ds(b, 1)], eq[:], ALU.add, ALU.mult))
                    ch(v.tensor_tensor(slotf[:], slotf[:], cum[:], ALU.add))
                ch.restart()
                ch(v.tensor_scalar(over_end[:], C["row"][0:T, 0:NT], ps_end[0][0:T, 0:1], None, ALU.is_ge))
                v.sem_inc(s_tot, 1)
                v.wait_ge(s_pref, 4)
                ch(v.tensor_scalar(which[:], ps_which[0][0:1, 0:NT], float(T - 1), None, ALU.min))
                ch(v.tensor_copy(blk_i[:], which[:]))
                ch(v.tensor_copy(slots[:], slotf[:]))


def scatter_edges(nc, src, attr2, weight, attr4, attr16, attr32, edge_att, slots, loc1, sorted_rows, hdr):
    CH = 25
    NCH = ET // CH
    assert NCH % 2 == 1
    with Phase(nc, "scatter") as ph:
        s_in, s_used, s_init = ph.sem("in"), ph.sem("used"), ph.sem("init")
        s_sent = [ph.pool_dma_sem(f"sent{j}") for j in range(2)]
        s_out, s_prod = ph.sem("out"), ph.sem("prod")
        pays = ph.ring("pay", 2, [P, CH * ROW])
        st_src = ph.sb("src", [P, CH], I32)
        st2 = ph.sb("st2", [P, CH * 2])
        stw = ph.sb("stw", [P, CH])
        st4 = ph.sb("st4", [P, CH * 4])
        st16 = ph.sb("st16", [P, CH * 16])
        st32 = ph.sb("st32", [P, CH * EF])
        sls = ph.ring("sl", 2, [P, CH], I32)
        prod = ph.sb("prod", [P, CH * NH * EF])

        def field(j, a, n):
            return pays[j][:].rearrange("p (c w) -> p c w", w=ROW)[:, :, a:a + n]

        def chunks(eng, chunk):
            with eng.Fori(0, NCH // 2) as i:
                chunk(i * 2, 0)
                chunk(i * 2 + 1, 1)
            chunk(NCH - 1, 0)

        def parts(t, n):
            return t[:].rearrange("p (c w) -> p c w", w=n)

        with nc.Block() as block:

            @block.sync
            def _(sp):
                sp.wait_ge(s_init, 1)
                sp.sem_inc(s_used, 8)
                with sp.Fori(0, NCH) as c:
                    sp.wait_ge(s_used, c * 8 + 8)
                    for t, a, n in ((st_src, src, 1), (st2, attr2, 2), (stw, weight, 1), (st4, attr4, 4),
                                    (st16, attr16, 16), (st32, attr32, EF)):
                        rows = (a.rearrange("(p t) -> p t", p=P) if n == 1
                                else a.rearrange("(p t) w -> p (t w)", p=P))
                        sp.dma_start(t[:], rows[:, ds(c * (CH * n), CH * n)]).then_inc(s_in, 16)

            @block.vector
            def _(v):
                v.memset(hdr[:, NT * HB:NTX * HB], 0.0)
                for j in range(2):
                    v.memset(pays[j][:], 0.0).then_inc(s_init, 1)
                v.wait_ge(s_init, 2)
                for j in range(2):
                    v.memset(field(j, VALID, 1), 1.0).then_inc(s_init, 1)
                v.wait_ge(s_init, 4)
                p4 = prod[:].rearrange("p (c h f) -> p c h f", h=NH, f=EF)

                def chunk(c, j):
                    v.wait_ge(s_in, c * 96 + 96)
                    v.wait_ge(s_out, c + 1)
                    v.tensor_copy(field(j, SRC, 1).bitcast(I32), parts(st_src, 1)).then_inc(s_used, 1)
                    v.tensor_copy(field(j, DIR, 2), parts(st2, 2)).then_inc(s_used, 1)
                    v.tensor_copy(field(j, WGT, 1), parts(stw, 1)).then_inc(s_used, 1)
                    v.wait_ge(s_used, c * 8 + 8)
                    for h in range(NH):
                        last = v.tensor_tensor(p4[:, :, h, :], parts(st32, EF),
                                               edge_att[0:P, h * EF:(h + 1) * EF].unsqueeze(1).to_broadcast([P, CH, EF]),
                                               ALU.mult)
                    last.then_inc(s_prod, 1)
                    v.wait_ge(s_prod, c + 1)
                    v.tensor_reduce(field(j, EAT, NH), p4, AX, ALU.add).then_inc(s_used, 1)
                    v.tensor_copy(field(j, DL1, 1), loc1[:, ds(c * CH, CH)].unsqueeze(2)).then_inc(s_used, 1)
                    v.tensor_copy(sls[j][:], slots[:, ds(c * CH, CH)]).then_inc(s_used, 1)

                chunks(v, chunk)

            @block.scalar
            def _(act):
                act.wait_ge(s_init, 4)

                def chunk(c, j):
                    act.wait_ge(s_in, c * 96 + 96)
                    act.wait_ge(s_out, c + 1)
                    act.activation(field(j, RBF, 16), parts(st16, 16), ACT.Copy).then_inc(s_used, 1)
                    act.activation(field(j, SH, 4), parts(st4, 4), ACT.Copy).then_inc(s_used, 1)

                chunks(act, chunk)

            @block.gpsimd
            def _(pool):
                pool.sem_inc(s_out, 2)

                def send(c, j):
                    pool.wait_ge(s_used, c * 8 + 16)
                    pool.nop(nofuse=True)
                    for t in range(CH):
                        pool.indirect_dma_start(
                            out=sorted_rows, out_offset=bass.IndirectOffsetOnAxis(ap=sls[j][:, t:t + 1], axis=0),
                            in_=pays[j][:, t * ROW:(t + 1) * ROW], in_offset=None).then_inc(s_sent[j], 16)

                def sent(j, n):
                    pool.wait_ge(s_sent[j], n * (16 * CH))
                    pool.sem_inc(s_out, 1)

                send(0, 0)
                with pool.Fori(0, (NCH - 1) // 2) as i:
                    send(i * 2 + 1, 1)
                    sent(0, i + 1)
                    send(i * 2 + 2, 0)
                    sent(1, i + 1)
                sent(0, (NCH + 1) // 2)


def header_words(sorted_rows, hdr):
    rows = sorted_rows.rearrange("(t p) c -> p t c", p=LANES)
    return hdr[:].rearrange("p (t c) -> p t c", c=HB)[:, 0:NT, :], rows[:, :, 0:HB]


def row_stats(nc, src, rstd, nbias, eps):
    with Phase(nc, "stats") as ph:
        s_st, s_ch, s_var, s_sq = ph.sem("st"), ph.sem("ch"), ph.sem("var"), ph.sem("sq")
        st = ph.sb("st", [P, T * 6])
        mean = ph.sb("mean", [P, T])
        dif = ph.sb("dif", [P, T])
        var = ph.sb("var", [P, T])
        s6 = st[:].rearrange("p (t s) -> p t s", s=6)
        with nc.Block() as block:

            @block.vector
            def _(v):
                ch = Chain(v, s_ch)
                with v.Fori(0, T // 5) as i:
                    for u in range(5):
                        v.bn_stats(st[:, ds(i * 30 + u * 6, 6)], src[:, ds(i * (5 * D) + u * D, D)]).then_inc(s_st, 1)
                v.wait_ge(s_st, T)
                ch(v.tensor_tensor(mean[:], s6[:, :, 1], s6[:, :, 4], ALU.add))
                ch(v.tensor_tensor(dif[:], s6[:, :, 1], s6[:, :, 4], ALU.subtract))
                ch(v.tensor_tensor(var[:], s6[:, :, 2], s6[:, :, 5], ALU.add))
                ch(v.tensor_scalar(var[:], var[:], 1.0 / D, eps, ALU.mult, ALU.add))
                ch(v.tensor_tensor(dif[:], dif[:], dif[:], ALU.mult))
                v.scalar_tensor_tensor(var[:], dif[:], 0.25, var[:], ALU.mult, ALU.add).then_inc(s_var, 1)
                v.wait_ge(s_sq, 1)
                ch(v.reciprocal(rstd[:], var[:]))
                ch(v.scalar_tensor_tensor(nbias[:], mean[:], -0.5, rstd[:], ALU.mult, ALU.mult))

            @block.scalar
            def _(act):
                act.wait_ge(s_var, 1)
                act.activation(var[:], var[:], ACT.Sqrt).then_inc(s_sq, 1)


def project(nc, C, src, rstd, nbias, gain=None, keep=None, keepT=None, w=None, F=0, brow=None, out=None,
            scale=None, add_to=None, kd=KD, also=(), store=(), pieces=1):
    U = 5
    with Phase(nc, "project") as ph:
        s_norm, s_aff, s_tr, s_ev, s_mm, s_res = (ph.sem(n) for n in ("norm", "aff", "tr", "ev", "mm", "res"))
        s_keep = ph.sem("keep")
        xt = ph.ring("xt", U, [P, kd * 128])
        xT = ph.ring("xT", U, [128, kd * P])
        pT = ph.ps("pT", 3)
        pO = ph.ps("pO", U) if w is not None else None
        spread = brow is not None and add_to is None
        assert not (spread and scale is not None)
        s_b = ph.sem("b")
        bias = ph.sb("bias", [P, F]) if spread else None
        norm = Count(s_norm, 0)
        tr = Count(s_tr, U)
        nev = (w is not None) + (keepT is not None)
        mm = Count(s_mm, U)
        res = Count(s_res, U)

        def slot(u):
            return pT[u % 3][:, 0:kd * P]

        s_also = ph.sem("also")
        with nc.Block() as block:

            @block.sync
            def _(sp):
                for dst, source in also:
                    sp.dma_start(dst, source).then_inc(s_also, 16)
                if store:
                    with sp.Fori(0, T // U) as i:
                        sp.wait_ge(s_res, i * U + 2 * U)
                        for table, a in store:
                            sp.dma_start(table.rearrange("(t p) f -> p t f", p=P)[:, ds(i * U, U), :],
                                         out[:, ds(i * (U * F), U * F)].rearrange("p (t f) -> p t f", f=F)
                                         [:, :, a:a + table.shape[1]]).then_inc(s_also, 16)
                if also or store:
                    sp.wait_ge(s_also, 16 * (len(also) + len(store) * (T // U)))

            @block.scalar
            def _(act):
                with act.Fori(0, T // U) as i:
                    for u in range(U):
                        k = i * U + u
                        act.wait_ge(s_tr, tr.freed(k, U))
                        act.activation(xt[u][:], src[:, ds(k * (kd * 128), kd * 128)], ACT.Identity, bias=nbias[:, ds(k, 1)],
                                       scale=rstd[:, ds(k, 1)]).then_inc(s_norm, 1)
                        if keep is not None:
                            act.activation(keep[:, ds(k * D, D)], src[:, ds(k * D, D)], ACT.Identity,
                                           bias=nbias[:, ds(k, 1)], scale=rstd[:, ds(k, 1)]).then_inc(s_keep, 1)
                if keep is not None:
                    act.wait_ge(s_keep, T)

            @block.tensor
            def _(pe):
                pe.sem_inc(s_tr, U)
                if w is not None:
                    pe.sem_inc(s_mm, U)
                if spread:
                    pe.matmul(pO[U - 1][0:P, 0:F], C["ones"][0:1, 0:P], brow, start=True, stop=True).then_inc(s_b, 1)

                def turn(k, u):
                    if gain is None:
                        pe.wait_ge(s_norm, norm.done(k))
                    else:
                        pe.wait_ge(s_aff, k * 2 + 2)
                    pe.wait_ge(s_ev, (k + U - (2 if u < 2 else 3)) * nev + nev)
                    for c in range(kd):
                        last = pe.transpose(slot(u)[:, c * P:(c + 1) * P], xt[u][:, c * 128:(c + 1) * 128],
                                            C["ident"][0:P, 0:P])
                    last.then_inc(s_tr, 1)

                def product(k, u):
                    pe.wait_ge(s_ev, k * nev + nev * (U + 1))
                    pe.wait_ge(s_res, res.freed(k, U))
                    for c in range(kd):
                        last = pe.matmul(pO[u][0:P, 0:F], xT[u][:, c * P:(c + 1) * P], w[:, c * F:(c + 1) * F],
                                         start=(c == 0), stop=(c == kd - 1 and (spread or brow is None)))
                    if brow is not None and not spread:
                        last = pe.matmul(pO[u][0:P, 0:F], C["ones"][0:1, 0:P], brow, start=False, stop=True)
                    last.then_inc(s_mm, 1)

                def group(i, last):
                    for u in range(U):
                        if not last or u + LAG < U:
                            turn(i * U + u + LAG, (u + LAG) % U)
                        if w is not None:
                            product(i * U + u, u)

                for u in range(LAG):
                    turn(u, u)
                with pe.Fori(0, T // U - 1) as i:
                    group(i, False)
                group(T // U - 1, True)

            @block.vector
            def _(v):
                v.sem_inc(s_ev, U * nev)
                if spread:
                    v.wait_ge(s_b, 1)
                    v.tensor_copy(bias[:], pO[U - 1][0:P, 0:F]).then_inc(s_b, 1)
                    v.wait_ge(s_b, 2)
                v.sem_inc(s_res, U)

                def affine(k, u):
                    if gain is not None:
                        v.wait_ge(s_norm, norm.done(k))
                        v.tensor_tensor(xt[u][:], xt[u][:], gain[0][:], ALU.mult).then_inc(s_aff, 1)
                        v.wait_ge(s_aff, k * 2 + 1)
                        v.tensor_tensor(xt[u][:], xt[u][:], gain[1][:], ALU.add).then_inc(s_aff, 1)

                def turned(k, u):
                    v.wait_ge(s_tr, tr.done(k))
                    if w is not None:
                        v.wait_ge(s_mm, mm.freed(k, U))
                        v.tensor_copy(xT[u][:], slot(u)).then_inc(s_ev, 1)
                    if keepT is not None:
                        v.tensor_copy(keepT[:].rearrange("p (c n) -> p c n", c=kd)[:, :, ds(k * P, P)],
                                      slot(u).rearrange("p (c n) -> p c n", c=kd)).then_inc(s_ev, 1)

                def result(k, u):
                    v.wait_ge(s_mm, mm.done(k))
                    if add_to is not None:
                        v.tensor_tensor(add_to[:, ds(k * F, F)], add_to[:, ds(k * F, F)], pO[u][0:P, 0:F],
                                        ALU.add).then_inc(s_res, 1)
                    elif spread:
                        if pieces == 1:
                            o, a, b = out[:, ds(k * F, F)], pO[u][0:P, 0:F], bias[:]
                        else:
                            wide, c = F + pieces, F // pieces
                            o = out[:, ds(k * wide, wide)].rearrange("p (h c) -> p h c", h=pieces)[:, :, 0:c]
                            a = pO[u][0:P, 0:F].rearrange("p (h c) -> p h c", h=pieces)
                            b = bias[:].rearrange("p (h c) -> p h c", h=pieces)
                        v.tensor_tensor(o, a, b, ALU.add).then_inc(s_res, 1)
                    elif scale is not None:
                        v.tensor_scalar(out[:, ds(k * F, F)], pO[u][0:P, 0:F], scale[:, ds(k, 1)], None,
                                        ALU.mult).then_inc(s_res, 1)
                    else:
                        v.tensor_copy(out[:, ds(k * F, F)], pO[u][0:P, 0:F]).then_inc(s_res, 1)

                def group(i, last):
                    for u in range(U):
                        if not last or u + LAG + 1 < U:
                            affine(i * U + u + LAG + 1, (u + LAG + 1) % U)
                        if not last or u + LAG < U:
                            turned(i * U + u + LAG, (u + LAG) % U)
                        if w is not None:
                            result(i * U + u, u)

                for u in range(LAG + 1):
                    affine(u, u)
                for u in range(LAG):
                    turned(u, u)
                with v.Fori(0, T // U - 1) as i:
                    group(i, False)
                group(T // U - 1, True)


def store_table(nc, res, table, F):
    with Phase(nc, "table") as ph:
        s = ph.sem("stored")
        with nc.Block() as block:

            @block.sync
            def _(sp):
                sp.dma_start(table.rearrange("(t p) f -> p t f", p=P),
                             res[:].rearrange("p (t f) -> p t f", f=F)).then_inc(s, 16)
                sp.wait_ge(s, 16)


def load_many(nc, pairs, zero=None):
    with Phase(nc, "load") as ph:
        s, s_z = ph.sem("in"), ph.sem("zero")
        with nc.Block() as block:

            @block.vector
            def _(v):
                if zero is not None:
                    v.memset(zero, 0.0).then_inc(s_z, 1)
                    v.wait_ge(s_z, 1)

            @block.sync
            def _(sp):
                for dst, src in pairs:
                    sp.dma_start(dst, src).then_inc(s, 16)
                sp.wait_ge(s, 16 * len(pairs))


F0 = 136
H0 = 68
A0 = 65
S0 = NH * A0 + 1


def gnn0_weights(nc, wf, wr, attnT, wfT, wrT, W):
    with Phase(nc, "w0") as ph:
        s_in, s_mm, s_ev = ph.sem("in"), ph.sem("mm"), ph.sem("ev")
        nat = ph.ring("nat", 2, [HD, D])
        at = ph.sb("at", [HD, NH])
        pW = ph.ps("pW", 4)
        Wv = W[:].rearrange("p (c f) -> p c f", c=KD)
        with nc.Block() as block:

            @block.sync
            def _(sp):
                sp.dma_start(nat[0][:], wf).then_inc(s_in, 16)
                sp.dma_start(nat[1][:], wr).then_inc(s_in, 16)
                sp.dma_start(at[:], attnT).then_inc(s_in, 16)
                sp.dma_start(Wv[:, :, 0:HD], wfT.rearrange("(c p) f -> p c f", p=128)).then_inc(s_in, 16)
                sp.dma_start(Wv[:, :, H0:H0 + HD], wrT.rearrange("(c p) f -> p c f", p=128)).then_inc(s_in, 16)
                sp.wait_ge(s_in, 80)

            @block.tensor
            def _(pe):
                pe.wait_ge(s_in, 80)
                for j in range(2):
                    for c in range(KD):
                        pe.matmul(pW[j * 2 + c][:, 0:NH], nat[j][:, c * 128:(c + 1) * 128], at[:], start=True,
                                  stop=True).then_inc(s_mm, 1)

            @block.vector
            def _(v):
                v.wait_ge(s_mm, 4)
                v.wait_ge(s_in, 80)
                for j in range(2):
                    for c in range(KD):
                        v.tensor_copy(Wv[:, c, j * H0 + HD:(j + 1) * H0],
                                      pW[j * 2 + c][:, 0:NH]).then_inc(s_ev, 1)
                v.wait_ge(s_ev, 4)


def gnn0_messages(nc, table, hdr, M):
    R = 8
    with Phase(nc, "msg0") as ph:
        s_cur, s_msg, s_tmp, s_init = ph.sem("cur"), ph.sem("msg"), ph.sem("tmp"), ph.sem("init")
        s_g = [ph.pool_dma_sem(f"g{i}") for i in range(R)]
        cur = ph.sb("cur", [128, R], I32)
        G = ph.ring("G", R, [128, F0])
        tmp = ph.ring("tmp", 2, [128, H0])
        cu, msg, tm = Count(s_cur), Count(s_msg, R), Count(s_tmp)
        with nc.Block() as block:

            @block.scalar
            def _(act):
                with act.Fori(0, NT // R) as i:
                    for u in range(R):
                        k = i * R + u
                        act.wait_ge(s_msg, msg.freed(k, R))
                        act.activation(cur[:, u:u + 1], hdr[:, ds(k * HB + SRC, 1)].bitcast(I32), ACT.Copy).then_inc(s_cur, 1)

            @block.gpsimd
            def _(pool):
                with pool.Fori(0, NT // R) as i:
                    for u in range(R):
                        k = i * R + u
                        pool.wait_ge(s_cur, cu.done(k))
                        pool.nop(nofuse=True)
                        pool.indirect_dma_start(out=G[u][:], out_offset=None, in_=table,
                                                in_offset=bass.IndirectOffsetOnAxis(ap=cur[:, u:u + 1], axis=0)
                                                ).then_inc(s_g[u], 16)

            @block.vector
            def _(v):
                v.memset(M[:, NT * H0:NTL * H0], 0.0).then_inc(s_init, 1)
                v.sem_inc(s_msg, R)
                with v.Fori(0, NT // R) as i:
                    for u in range(R):
                        k = i * R + u
                        v.wait_ge(s_g[u], i * 16 + 16)
                        v.wait_ge(s_msg, msg.freed(k, 2))
                        v.tensor_scalar(tmp[u % 2][:], G[u][:, H0:F0], hdr[:, ds(k * HB + DIR + 1, 1)], None,
                                        ALU.mult).then_inc(s_tmp, 1)
                        v.wait_ge(s_tmp, tm.done(k))
                        v.scalar_tensor_tensor(M[:, ds(k * H0, H0)], G[u][:, 0:H0], hdr[:, ds(k * HB + DIR, 1)],
                                               tmp[u % 2][:], ALU.mult, ALU.add).then_inc(s_msg, 1)
                v.wait_ge(s_msg, NT + R)


def gnn0_softmax(nc, hdr, M, ex):
    with Phase(nc, "soft0") as ph:
        s_ch, s_mx, s_all, s_ex, s_low = ph.sem("ch"), ph.sem("mx"), ph.sem("all"), ph.sem("ex"), ph.sem("low")
        low = ph.sb("low", [128, NTL])
        mx = ph.sb("mx", [128, NH])
        am = ph.sb("am", [128, NH])
        M3 = M[:].rearrange("p (t f) -> p t f", f=H0)
        sc = M3[:, :, HD:H0]
        e3 = ex[:].rearrange("p (t h) -> p t h", h=NH)
        h3 = hdr[:].rearrange("p (t c) -> p t c", c=HB)
        with nc.Block() as block:

            @block.vector
            def _(v):
                ch = Chain(v, s_ch)
                ch(v.scalar_tensor_tensor(e3, sc, 0.2, sc, ALU.mult, ALU.max))
                ch(v.tensor_scalar(low[:], h3[:, 0:NTL, VALID], 1.0, BIG, ALU.subtract, ALU.mult))
                ch(v.tensor_tensor(e3, e3, over(low[:], [128, NTL, NH]), ALU.add))
                v.tensor_reduce(mx[:], ex[:].rearrange("p (t h) -> p h t", h=NH), AX, ALU.max).then_inc(s_mx, 1)
                ch(v.memset(M3[:, :, HD:HD + 1], 1.0))
                v.wait_ge(s_all, 1)
                ch(v.tensor_tensor(e3, e3, am[:].unsqueeze(1).to_broadcast([128, NTL, NH]), ALU.subtract))
                v.sem_inc(s_low, 1)

            @block.gpsimd
            def _(pool):
                pool.wait_ge(s_mx, 1)
                pool.partition_all_reduce(am[:], mx[:], 128, bass.bass_isa.ReduceOp.max).then_inc(s_all, 1)

            @block.scalar
            def _(act):
                act.wait_ge(s_low, 1)
                act.activation(ex[:], ex[:], ACT.Exp).then_inc(s_ex, 1)
                act.wait_ge(s_ex, 1)


def gnn0_sum(nc, C, hdr, blk_i, M, ex, acc):
    R = 4
    G = 8
    with Phase(nc, "sum0") as ph:
        s_oh, s_mm, s_acc, s_z, s_w = ph.sem("oh"), ph.sem("mm"), ph.sem("acc"), ph.sem("z"), ph.sem("w")
        OH = ph.ring("OH", R, [128, P])
        Wt = ph.ring("Wt", R, [128, S0])
        pS = ph.ps("pS", R)
        mm, ac = Count(s_mm, R), Count(s_acc, R)
        with nc.Block() as block:

            @block.vector
            def _(v):
                v.memset(acc[:], 0.0).then_inc(s_z, 1)
                v.wait_ge(s_z, 1)
                v.sem_inc(s_acc, R)

                def prepare(k, u):
                    v.wait_ge(s_mm, mm.freed(k, R))
                    v.tensor_scalar(OH[u][:], C["nodes"][:], hdr[:, ds(k * HB + DL1, 1)], None, ALU.is_equal).then_inc(s_oh, 1)
                    v.tensor_scalar(Wt[u][:, 0:A0], M[:, ds(k * H0, A0)], ex[:, ds(k * NH, 1)], None,
                                    ALU.mult).then_inc(s_oh, 1)

                for u in range(LAG):
                    prepare(u, u)
                regs = [v.alloc_register(f"sum0_block{u}") for u in range(G)]
                with v.Fori(0, NT // G) as i:
                    blocks = blocks_of(v, regs, blk_i, i * G)
                    for u in range(G):
                        k = i * G + u
                        prepare(k + LAG, (u + LAG) % R)
                        v.wait_ge(s_mm, mm.done(k))
                        v.wait_ge(s_acc, ac.freed(k, 1))
                        a = acc[:, ds(blocks[u] * S0, S0)]
                        v.tensor_tensor(a, pS[u % R][0:P, 0:S0], a, ALU.add).then_inc(s_acc, 1)
                v.wait_ge(s_acc, NT + R)
                v.wait_ge(s_oh, 2 * NTL)

            @block.scalar
            def _(act):
                with act.Fori(0, NT // G) as i:
                    for u in range(G):
                        k = i * G + u
                        act.wait_ge(s_mm, mm.freed(k, R))
                        act.activation(Wt[u % R][:, S0 - 1:S0], hdr[:, ds(k * HB + WGT, 1)], ACT.Copy)
                        for h in range(1, NH):
                            last = act.activation(Wt[u % R][:, h * A0:(h + 1) * A0], M[:, ds(k * H0, A0)], ACT.Copy,
                                                  scale=ex[:, ds(k * NH + h, 1)])
                        last.then_inc(s_w, 1)

            @block.tensor
            def _(pe):
                pe.sem_inc(s_mm, R)
                with pe.Fori(0, NT // R) as i:
                    for u in range(R):
                        k = i * R + u
                        pe.wait_ge(s_oh, k * 2 + 2)
                        pe.wait_ge(s_w, k + 1)
                        pe.wait_ge(s_acc, ac.freed(k, R))
                        pe.matmul(pS[u][0:P, 0:S0], OH[u][:], Wt[u][:], start=True, stop=True).then_inc(s_mm, 1)


def gnn0_update(nc, acc, X, dis):
    with Phase(nc, "upd0") as ph:
        s_ch, s_d, s_sq = ph.sem("ch"), ph.sem("d"), ph.sem("sq")
        den = ph.sb("den", [P, T * NH])
        deg = ph.sb("deg", [P, T])
        pos = ph.sb("pos", [P, T])
        a3 = acc[:].rearrange("p (t s) -> p t s", s=S0)
        x3 = X[:].rearrange("p (t d) -> p t d", d=D)
        with nc.Block() as block:

            @block.vector
            def _(v):
                ch = Chain(v, s_ch)
                ch(v.tensor_scalar(deg[:], a3[:, :, S0 - 1], 1.0, None, ALU.add))
                ch(v.tensor_scalar(pos[:], deg[:], 0.0, None, ALU.is_gt))
                ch(v.tensor_tensor(deg[:], deg[:], pos[:], ALU.mult))
                ch(v.tensor_tensor(deg[:], deg[:], pos[:], ALU.subtract))
                v.tensor_scalar(deg[:], deg[:], 1.0, None, ALU.add).then_inc(s_d, 1)
                d3 = den[:].rearrange("p (t h) -> p t h", h=NH)
                for h in range(NH):
                    ch(v.tensor_scalar(d3[:, :, h], a3[:, :, h * A0 + HD], 1e-10, None, ALU.add))
                ch(v.reciprocal(den[:], den[:]))
                for h in range(NH):
                    m = a3[:, :, h * A0:h * A0 + HD]
                    ch(v.tensor_tensor(m, m, over(d3[:, :, h], [P, T, HD]), ALU.mult))
                    xh = x3[:, :, h * HD:(h + 1) * HD]
                    ch(v.tensor_tensor(xh, xh, m, ALU.add))
                v.wait_ge(s_sq, 1)
                ch(v.reciprocal(deg[:], deg[:]))
                ch(v.tensor_tensor(dis[:], deg[:], pos[:], ALU.mult))

            @block.scalar
            def _(act):
                act.wait_ge(s_d, 1)
                act.activation(deg[:], deg[:], ACT.Sqrt).then_inc(s_sq, 1)


def normalise(nc, src, rstd, nbias, out):
    with Phase(nc, "norm") as ph:
        s_a, s_v = ph.sem("a"), ph.sem("v")
        with nc.Block() as block:

            @block.vector
            def _(v):
                with v.Fori(0, T // 5) as i:
                    for u in range(3, 5):
                        k = i * 5 + u
                        v.tensor_scalar(out[:, ds(k * D, D)], src[:, ds(k * D, D)], rstd[:, ds(k, 1)], nbias[:, ds(k, 1)],
                                        ALU.mult, ALU.add).then_inc(s_v, 1)
                v.wait_ge(s_v, 2 * T // 5)

            @block.scalar
            def _(act):
                with act.Fori(0, T // 5) as i:
                    for u in range(3):
                        k = i * 5 + u
                        act.activation(out[:, ds(k * D, D)], src[:, ds(k * D, D)], ACT.Identity,
                                       bias=nbias[:, ds(k, 1)], scale=rstd[:, ds(k, 1)]).then_inc(s_a, 1)
                act.wait_ge(s_a, 3 * T // 5)


def weighted_neighbour_sum(nc, C, hdr, blk_i, table, acc):
    R = 8
    RP = 4
    with Phase(nc, "conv") as ph:
        s_cur, s_oh, s_mm, s_acc = ph.sem("cur"), ph.sem("oh"), ph.sem("mm"), ph.sem("acc")
        s_g = [ph.pool_dma_sem(f"g{i}") for i in range(R)]
        cur = ph.sb("cur", [128, R], I32)
        G = ph.ring("G", R, [128, D])
        OH = ph.ring("OH", RP, [128, P])
        pS = ph.ps("pS", RP)
        cu, mm, ac = Count(s_cur), Count(s_mm, R), Count(s_acc, R)
        with nc.Block() as block:

            @block.scalar
            def _(act):
                with act.Fori(0, NT // R) as i:
                    for u in range(R):
                        k = i * R + u
                        act.wait_ge(s_mm, mm.freed(k, R))
                        act.activation(cur[:, u:u + 1], hdr[:, ds(k * HB + SRC, 1)].bitcast(I32), ACT.Copy).then_inc(s_cur, 1)

            @block.gpsimd
            def _(pool):
                with pool.Fori(0, NT // R) as i:
                    for u in range(R):
                        k = i * R + u
                        pool.wait_ge(s_cur, cu.done(k))
                        pool.nop(nofuse=True)
                        pool.indirect_dma_start(out=G[u][:], out_offset=None, in_=table,
                                                in_offset=bass.IndirectOffsetOnAxis(ap=cur[:, u:u + 1], axis=0)
                                                ).then_inc(s_g[u], 16)

            @block.vector
            def _(v):
                v.sem_inc(s_acc, R)

                def prepare(k, u):
                    v.wait_ge(s_mm, mm.freed(k, RP))
                    v.tensor_scalar(OH[u][:], C["nodes"][:], hdr[:, ds(k * HB + DL1, 1)],
                                    hdr[:, ds(k * HB + WGT, 1)], ALU.is_equal, ALU.mult).then_inc(s_oh, 1)

                for u in range(LAG):
                    prepare(u, u)
                regs = [v.alloc_register(f"{ph.name}_block{u}") for u in range(R)]
                with v.Fori(0, NT // R) as i:
                    blocks = blocks_of(v, regs, blk_i, i * R)
                    for u in range(R):
                        k = i * R + u
                        prepare(k + LAG, (u + LAG) % RP)
                        v.wait_ge(s_mm, mm.done(k))
                        v.wait_ge(s_acc, ac.freed(k, 1))
                        a = acc[:, ds(blocks[u] * D, D)]
                        v.tensor_tensor(a, pS[u % RP][0:P, 0:D], a, ALU.add).then_inc(s_acc, 1)
                v.wait_ge(s_acc, NT + R)
                v.wait_ge(s_oh, NTL)

            @block.tensor
            def _(pe):
                pe.sem_inc(s_mm, R)
                with pe.Fori(0, NT // R) as i:
                    for u in range(R):
                        k = i * R + u
                        pe.wait_ge(s_oh, k + 1)
                        pe.wait_ge(s_g[u], i * 16 + 16)
                        pe.wait_ge(s_acc, ac.freed(k, RP))
                        pe.matmul(pS[u % RP][0:P, 0:D], OH[u % RP][:], G[u][:], start=True, stop=True).then_inc(s_mm, 1)


def conv_update(nc, acc, dis, brow, Y):
    with Phase(nc, "convup") as ph:
        s_ch = ph.sem("ch")
        a3 = acc[:].rearrange("p (t d) -> p t d", d=D)
        y3 = Y[:].rearrange("p (t d) -> p t d", d=D)
        with nc.Block() as block:

            @block.vector
            def _(v):
                ch = Chain(v, s_ch)
                ch(v.tensor_tensor(a3, a3, over(dis[:], [P, T, D]), ALU.mult))
                ch(v.tensor_tensor(a3, a3, brow[:].unsqueeze(1).to_broadcast([P, T, D]), ALU.add))
                ch(v.scalar_tensor_tensor(y3, a3, 0.0, y3, ALU.max, ALU.add))


def gnn1(nc, C, hdr, blk_i, X, dis, rstd, nbias, dr, table):
    with ExitStack() as st:
        sb = lambda n, s: st.enter_context(nc.sbuf_tensor(f"g1_{n}", s, F32))
        Y, acc = sb("Y", [P, T * D]), sb("acc", [P, T * D])
        rows = {n: sb(n, [P, D]) for n in ("ln6_g", "ln6_b", "ln7_g", "ln7_b", "b6", "b7")}
        bp = sb("bp", [1, D])
        Ws = {n: sb(n, [128, KD * D]) for n in ("W6", "W7", "Wp")}
        load_many(nc, [(rows[n][:], dr[n].unsqueeze(0).to_broadcast([P, D])) for n in rows]
                  + [(bp[:], dr["bp"].unsqueeze(0))]
                  + [(Ws[n][:].rearrange("p (c f) -> p c f", c=KD), dr[n].rearrange("(c p) f -> p c f", p=128)) for n in Ws])
        row_stats(nc, X, rstd, nbias, 1e-5)
        normalise(nc, X, rstd, nbias, Y)
        for j in "67":
            row_stats(nc, Y, rstd, nbias, 1e-5)
            project(nc, C, Y, rstd, nbias, gain=(rows[f"ln{j}_g"], rows[f"ln{j}_b"]), w=Ws[f"W{j}"], F=D, out=acc, scale=dis,
                    store=[(table, 0)])
            weighted_neighbour_sum(nc, C, hdr, blk_i, table, acc)
            conv_update(nc, acc, dis, rows[f"b{j}"], Y)
        plain(nc, rstd, nbias)
        project(nc, C, Y, rstd, nbias, w=Ws["Wp"], F=D, brow=bp[:], add_to=X)


def plain(nc, rstd, nbias):
    with Phase(nc, "plain") as ph:
        s = ph.sem("s")
        with nc.Block() as block:

            @block.vector
            def _(v):
                v.memset(rstd[:], 1.0).then_inc(s, 1)
                v.memset(nbias[:], 0.0).then_inc(s, 1)
                v.wait_ge(s, 2)


NE = 8
FH = 1024
KF = FH // 128
CAP = 489
ER = 123
EJ = 4
ES = ER * EJ
Q = 5
QN = Q * P
QA = 3 * P
BUF = NE * ES + N
NTT = (2 * N + NE * 127) // 128
NTT_X = NTT + 8
assert NTT % 4 == 0 and NTT_X <= NT
assert CAP == -(-5 * N // (4 * NE)) and CAP <= ES and ER <= 128


def softmax_parts(ch, v, l3, m, shape):
    ch(v.tensor_reduce(m[:], l3, AX, ALU.max))
    ch(v.tensor_tensor(l3, l3, over(m[:], shape), ALU.subtract))


def first_of(ch, v, out3, p3, m, tmp3, iota3, ix, shape):
    ch(v.tensor_tensor(out3, p3, over(m[:], shape), ALU.is_equal))
    ch(v.scalar_tensor_tensor(tmp3, iota3, -float(NE), out3, ALU.add, ALU.mult))
    ch(v.tensor_reduce(ix[:], tmp3, AX, ALU.min))
    ch(v.tensor_scalar(ix[:], ix[:], float(NE), None, ALU.add))
    ch(v.tensor_tensor(out3, iota3, over(ix[:], shape), ALU.is_equal))


def route0(nc, C, logits, gslot, sslot, gate):
    sh = [P, T, NE]
    with Phase(nc, "route0") as ph:
        s_ch, s_a, s_b, s_oh, s_pf, s_io = (ph.sem(n) for n in ("ch", "a", "b", "oh", "pf", "io"))
        m, s, ix = ph.sb("m", [P, T]), ph.sb("s", [P, T]), ph.sb("ix", [P, T])
        oh, tmp = ph.sb("oh", [P, T * NE]), ph.sb("tmp", [P, T * NE])
        before, pos, kept = ph.sb("before", [P, T * NE]), ph.sb("pos", [P, T]), ph.sb("kept", [P, T])
        trash = ph.sb("trash", [P, T])
        pP, pA = ph.ps("pP"), ph.ps("pA")
        v3 = lambda t: t[:].rearrange("p (t e) -> p t e", e=NE)
        with nc.Block() as block:

            @block.gpsimd
            def _(pool):
                pool.iota(trash[:], [[P, T]], base=NE * ES, channel_multiplier=1,
                          allow_small_or_imprecise_dtypes=True).then_inc(s_io, 1)

            @block.scalar
            def _(act):
                act.wait_ge(s_a, 1)
                act.activation(logits[:], logits[:], ACT.Exp).then_inc(s_b, 1)

            @block.tensor
            def _(pe):
                pe.wait_ge(s_oh, 1)
                pe.matmul(pP[0][0:P, 0:T * NE], C["tri"][0:P, 0:P], oh[:], start=True, stop=True).then_inc(s_pf, 1)
                pe.matmul(pA[0][0:P, 0:T * NE], C["ones"][0:P, 0:P], oh[:], start=True, stop=True).then_inc(s_pf, 1)

            @block.vector
            def _(v):
                ch = Chain(v, s_ch)
                io3 = C["row"][0:P, 0:NE].unsqueeze(1).to_broadcast(sh)
                softmax_parts(ch, v, v3(logits), m, sh)
                v.sem_inc(s_a, 1)
                v.wait_ge(s_b, 1)
                ch(v.tensor_reduce(s[:], v3(logits), AX, ALU.add))
                ch(v.reciprocal(s[:], s[:]))
                ch(v.tensor_tensor(v3(logits), v3(logits), over(s[:], sh), ALU.mult))
                ch(v.tensor_reduce(m[:], v3(logits), AX, ALU.max))
                first_of(ch, v, v3(oh), v3(logits), m, v3(tmp), io3, ix, sh)
                v.sem_inc(s_oh, 1)
                v.wait_ge(s_pf, 2)
                ch(v.tensor_copy(tmp[:], pA[0][0:P, 0:T * NE]))
                for e in range(NE):
                    ch(v.tensor_tensor_scan(v3(before)[:, :, e], C["ones"][0:P, 0:1].to_broadcast([P, T]),
                                            v3(tmp)[:, :, e], 0.0, ALU.mult, ALU.add))
                ch(v.tensor_tensor(before[:], before[:], tmp[:], ALU.subtract))
                ch(v.tensor_tensor(before[:], before[:], pP[0][0:P, 0:T * NE], ALU.add))
                ch(v.tensor_tensor(before[:], before[:], oh[:], ALU.mult))
                ch(v.tensor_reduce(pos[:], v3(before), AX, ALU.add))
                ch(v.tensor_scalar(kept[:], pos[:], float(CAP), None, ALU.is_lt))
                ch(v.tensor_tensor(gate[:], m[:], kept[:], ALU.mult))
                ch(v.tensor_scalar(pos[:], pos[:], float(CAP - 1), None, ALU.min))
                ch(v.scalar_tensor_tensor(pos[:], ix[:], float(ES), pos[:], ALU.mult, ALU.add))
                ch(v.tensor_copy(gslot[:], pos[:]))
                v.wait_ge(s_io, 1)
                ch(v.tensor_tensor(pos[:], pos[:], trash[:], ALU.subtract))
                ch(v.tensor_tensor(pos[:], pos[:], kept[:], ALU.mult))
                ch(v.tensor_tensor(pos[:], pos[:], trash[:], ALU.add))
                ch(v.tensor_copy(sslot[:], pos[:]))


def dispatch0(nc, Y, sslot, buf):
    with Phase(nc, "disp0") as ph:
        s_s = ph.pool_dma_sem("s")
        with nc.Block() as block:

            @block.gpsimd
            def _(pool):
                for t in range(T):
                    pool.indirect_dma_start(out=buf, out_offset=bass.IndirectOffsetOnAxis(ap=sslot[:, t:t + 1], axis=0),
                                            in_=Y[:, t * D:(t + 1) * D], in_offset=None).then_inc(s_s, 16)
                pool.wait_ge(s_s, 16 * T)


def experts0(nc, C, w1, b1T, w2, b2, buf, ybuf):
    with Phase(nc, "exp0") as ph:
        s_row, s_tr, s_bt, s_h, s_ha, s_y, s_yv = (ph.sem(n) for n in ("row", "tr", "bt", "h", "ha", "y", "yv"))
        s_st, s_free = ph.pool_dma_sem("st"), ph.sem("free")
        s_ld = ph.sems_of("ld", 2)
        b1s, b2s = ph.sb("b1", [128, NE * KF]), ph.sb("b2", [1, NE * D])
        w1s, w2s = ph.ring("w1", 2, [128, KD * FH]), ph.ring("w2", 2, [128, KF * D])
        bufs = ph.ring("buf", 2, [ER, EJ * D])
        bT = ph.sb("bT", [128, KD * ES])
        hT = ph.sb("hT", [128, KF * ES])
        ys = ph.ring("y", 2, [ER, EJ * D])
        pT, pH, pY = ph.ps("pT", 2), ph.ps("pH", 2), ph.ps("pY", 2)
        tr, bt, h, ha, y, yv = Count(s_tr, EJ), Count(s_bt, EJ), Count(s_h), Count(s_ha, 2), Count(s_y, 2 * EJ), Count(s_yv, EJ)
        with nc.Block() as block:

            @block.sync
            def _(sp):
                sp.dma_start(b1s[:], b1T).then_inc(s_row, 16)
                sp.dma_start(b2s[:], b2.rearrange("e d -> (e d)").unsqueeze(0)).then_inc(s_row, 16)
                with sp.Fori(0, NE // 2) as i:
                    for s in range(2):
                        e = i * 2 + s
                        sp.wait_ge(s_y, e * EJ + EJ)
                        sp.dma_start(w1s[s][:].rearrange("p (c f) -> p c f", c=KD),
                                     w1[ds(e * D, D), :].rearrange("(c p) f -> p c f", p=128)).then_inc(s_ld[s], 16)
                        sp.dma_start(w2s[s][:].rearrange("p (c d) -> p c d", c=KF),
                                     w2[ds(e * FH, FH), :].rearrange("(c p) d -> p c d", p=128)).then_inc(s_ld[s], 16)
                        sp.dma_start(bufs[s][:].rearrange("p (j d) -> p j d", j=EJ),
                                     buf[ds(e * ES, ES), :].rearrange("(j p) d -> p j d", p=ER)).then_inc(s_ld[s], 16)

            @block.tensor
            def _(pe):
                pe.sem_inc(s_tr, EJ)
                pe.sem_inc(s_y, 2 * EJ)
                pe.wait_ge(s_row, 32)
                with pe.Fori(0, NE // 2) as i:
                    for s in range(2):
                        e = i * 2 + s
                        pe.wait_ge(s_ld[s], i * 48 + 48)
                        for j in range(EJ):
                            k = e * EJ + j
                            pe.wait_ge(s_bt, bt.freed(k, 2))
                            for c in range(KD):
                                last = pe.transpose(pT[j % 2][:, c * ER:(c + 1) * ER],
                                                    bufs[s][:, j * D + c * 128:j * D + (c + 1) * 128],
                                                    C["ident"][0:ER, 0:ER])
                            last.then_inc(s_tr, 1)
                        pe.wait_ge(s_bt, bt.done(e * EJ + EJ - 1))
                        for f in range(KF):
                            k = e * KF + f
                            pe.wait_ge(s_ha, ha.freed(k, 2))
                            for c in range(KD):
                                last = pe.matmul(pH[f % 2][:, 0:ES], w1s[s][:, c * FH + f * 128:c * FH + (f + 1) * 128],
                                                 bT[:, c * ES:(c + 1) * ES], start=(c == 0), stop=(c == KD - 1))
                            last.then_inc(s_h, 1)
                        pe.wait_ge(s_ha, ha.done(e * KF + KF - 1))
                        for j in range(EJ):
                            k = e * EJ + j
                            pe.wait_ge(s_yv, yv.freed(k, 2))
                            for f in range(KF):
                                pe.matmul(pY[j % 2][0:ER, 0:D], hT[:, f * ES + j * ER:f * ES + (j + 1) * ER],
                                          w2s[s][:, f * D:(f + 1) * D], start=(f == 0), stop=False)
                            pe.matmul(pY[j % 2][0:ER, 0:D], C["ones"][0:1, 0:ER], b2s[:, ds(e * D, D)], start=False,
                                      stop=True).then_inc(s_y, 1)

            @block.scalar
            def _(act):
                act.sem_inc(s_ha, 2)
                act.wait_ge(s_row, 32)
                with act.Fori(0, NE // 2) as i:
                    for s in range(2):
                        e = i * 2 + s
                        for f in range(KF):
                            act.wait_ge(s_h, h.done(e * KF + f))
                            act.activation(hT[:, f * ES:(f + 1) * ES], pH[f % 2][:, 0:ES], ACT.Relu,
                                           bias=b1s[:, ds(e * KF + f, 1)]).then_inc(s_ha, 1)

            @block.vector
            def _(v):
                v.sem_inc(s_bt, EJ)
                v.sem_inc(s_yv, EJ)
                b3 = bT[:].rearrange("p (c n) -> p c n", c=KD)
                with v.Fori(0, NE // 2) as i:
                    for s in range(2):
                        e = i * 2 + s
                        for j in range(EJ):
                            v.wait_ge(s_tr, tr.done(e * EJ + j))
                            v.tensor_copy(b3[:, :, j * ER:(j + 1) * ER],
                                          pT[j % 2][:, 0:KD * ER].rearrange("p (c n) -> p c n", c=KD)).then_inc(s_bt, 1)
                        v.wait_ge(s_free, e + 1)
                        for j in range(EJ):
                            v.wait_ge(s_y, e * EJ + j + 1 + 2 * EJ)
                            v.tensor_copy(ys[s][:, j * D:(j + 1) * D], pY[j % 2][0:ER, 0:D]).then_inc(s_yv, 1)

            @block.gpsimd
            def _(pool):
                pool.sem_inc(s_free, 2)
                with pool.Fori(0, NE // 2) as i:
                    for s in range(2):
                        e = i * 2 + s
                        pool.wait_ge(s_yv, yv.done(e * EJ + EJ - 1))
                        pool.dma_start(ybuf[ds(e * ES, ES), :].rearrange("(j p) d -> p j d", p=ER),
                                       ys[s][:].rearrange("p (j d) -> p j d", j=EJ)).then_inc(s_st, 16)
                        pool.wait_ge(s_st, e * 16 + 16)
                        pool.sem_inc(s_free, 1)


def combine0(nc, ybuf, gslot, gate, X):
    U = 5
    with Phase(nc, "comb0") as ph:
        s_ch = ph.sem("ch")
        s_g = [ph.pool_dma_sem(f"g{i}") for i in range(T // U)]
        YG = ph.sb("YG", [P, T * D])
        mask = ph.ring("mask", 3, [P, U * D], I32)
        val = ph.ring("val", 3, [P, U * D])
        yt = ph.sb("yt", [P, U * D])
        with nc.Block() as block:

            @block.gpsimd
            def _(pool):
                for t in range(T):
                    pool.indirect_dma_start(out=YG[:, t * D:(t + 1) * D], out_offset=None, in_=ybuf,
                                            in_offset=bass.IndirectOffsetOnAxis(ap=gslot[:, t:t + 1], axis=0)
                                            ).then_inc(s_g[t // U], 16)

            @block.vector
            def _(v):
                ch = Chain(v, s_ch)
                for j, x in enumerate((0.0, 10000.0, -10000.0)):
                    ch(v.memset(val[j][:], x))
                for i in range(T // U):
                    v.wait_ge(s_g[i], 16 * U)
                    y, a = yt[:], slice(i * U * D, (i + 1) * U * D)
                    ch(v.tensor_tensor(y.rearrange("p (t d) -> p t d", d=D),
                                       YG[:, a].rearrange("p (t d) -> p t d", d=D),
                                       over(gate[:, i * U:(i + 1) * U], [P, U, D]), ALU.mult))
                    ch(v.tensor_tensor(mask[0][:], y, y, ALU.not_equal))
                    ch(v.tensor_scalar(mask[1][:], y, 3.4028234e38, None, ALU.is_gt))
                    ch(v.tensor_scalar(mask[2][:], y, -3.4028234e38, None, ALU.is_lt))
                    for j in range(3):
                        ch(v.copy_predicated(y, mask[j][:], val[j][:]))
                    ch(v.tensor_tensor(X[:, a], X[:, a], y, ALU.add))


def ffn0(nc, C, X, rstd, nbias, dr, buf, ybuf):
    with ExitStack() as st:
        sb = lambda n, s, d=F32: st.enter_context(nc.sbuf_tensor(f"f0_{n}", s, d))
        gslot, sslot, gate = sb("gslot", [P, T], I32), sb("sslot", [P, T], I32), sb("gate", [P, T])
        with ExitStack() as s2:
            sc = lambda n, s: s2.enter_context(nc.sbuf_tensor(f"f0_{n}", s, F32))
            Y, logits, gw, gb = sc("Y", [P, T * D]), sc("logits", [P, T * NE]), sc("gw", [128, KD * NE]), sc("gb", [1, NE])
            zeros = sc("zeros", [ER, D])
            load_many(nc, [(gw[:].rearrange("p (c f) -> p c f", c=KD), dr["gate_w"].rearrange("(c p) f -> p c f", p=128)),
                           (gb[:], dr["gate_b"].unsqueeze(0))], zero=zeros[:])
            row_stats(nc, X, rstd, nbias, 1e-5)
            project(nc, C, X, rstd, nbias, keep=Y, w=gw, F=NE, brow=gb[:], out=logits,
                    also=[(buf[0:NE * ES, :].rearrange("(p r) d -> p r d", p=ER),
                           zeros[:].unsqueeze(1).to_broadcast([ER, NE * EJ, D]))])
            route0(nc, C, logits, gslot, sslot, gate)
            dispatch0(nc, Y, sslot, buf)
        experts0(nc, C, dr["w1"].rearrange("e d f -> (e d) f"), dr["b1T"], dr["w2"].rearrange("e f d -> (e f) d"),
                 dr["b2"], buf, ybuf)
        combine0(nc, ybuf, gslot, gate, X)


def expert_weights(w1, w2, W1s, W2s, first, second):
    pairs = [(W1s[:, e * KD * FH:(e + 1) * KD * FH].rearrange("p (c f) -> p c f", c=KD),
              w1[e * D:(e + 1) * D, :].rearrange("(c p) f -> p c f", p=128)) for e in first]
    return pairs + [(W2s[:, e * KF * D:(e + 1) * KF * D].rearrange("p (c d) -> p c d", c=KF),
                     w2[e * FH:(e + 1) * FH, :].rearrange("(c p) d -> p c d", p=128)) for e in second]


def route1(nc, C, logits, weights, gate, slot, tokens, expert_i):
    sh = [P, T, NE]
    with Phase(nc, "route1") as ph:
        s_ch, s_a, s_b, s_oh, s_pf, s_io, s_ld, s_hot, s_map = (
            ph.sem(n) for n in ("ch", "a", "b", "oh", "pf", "io", "ld", "hot", "map"))
        m, s, ix = ph.sb("m", [P, T]), ph.sb("s", [P, T]), [ph.sb(f"ix{j}", [P, T]) for j in range(2)]
        o = [ph.sb(f"o{j}", [P, T * NE]) for j in range(2)]
        tmp, rest, both, before = (ph.sb(n, [P, T * NE]) for n in ("tmp", "rest", "both", "before"))
        end, first = ph.sb("end", [P, NE]), ph.sb("first", [P, NE])
        node = ph.sb("node", [P, T])
        pos, hi = ph.sb("pos", [P, T]), ph.sb("hi", [P, T])
        tiles = ph.sb("tiles", [1, NTT_X])
        lows, highs = ph.ring("lows", 2, [P, 128]), ph.ring("highs", 2, [P, NTT])
        pP, pA, pM = ph.ps("pP"), ph.ps("pA"), ph.ps("pM")
        v3 = lambda t: t[:].rearrange("p (t e) -> p t e", e=NE)
        hot, mp = Count(s_hot), Count(s_map, 2)
        with nc.Block() as block:

            @block.sync
            def _(sp):
                for dst, source in weights:
                    sp.dma_start(dst, source).then_inc(s_ld, 16)
                sp.wait_ge(s_ld, 16 * len(weights))

            @block.gpsimd
            def _(pool):
                pool.iota(node[:], [[P, T]], base=0, channel_multiplier=1,
                          allow_small_or_imprecise_dtypes=True).then_inc(s_io, 1)

            @block.scalar
            def _(act):
                act.wait_ge(s_a, 1)
                act.activation(logits[:], logits[:], ACT.Exp).then_inc(s_b, 1)

            @block.tensor
            def _(pe):
                pe.wait_ge(s_oh, 1)
                pe.matmul(pP[0][0:P, 0:T * NE], C["tri"][0:P, 0:P], both[:], start=True, stop=True).then_inc(s_pf, 1)
                pe.matmul(pA[0][0:P, 0:T * NE], C["ones"][0:P, 0:P], both[:], start=True, stop=True).then_inc(s_pf, 1)
                pe.sem_inc(s_map, 2)
                for k in range(2 * T):
                    pe.wait_ge(s_hot, hot.done(k))
                    pe.matmul(pM[0][:, 0:NTT], lows[k % 2][:], highs[k % 2][:], start=(k == 0),
                              stop=(k == 2 * T - 1)).then_inc(s_map, 1)

            @block.vector
            def _(v):
                ch = Chain(v, s_ch)
                io3 = C["row"][0:P, 0:NE].unsqueeze(1).to_broadcast(sh)
                g = [gate[:, j * T:(j + 1) * T] for j in range(2)]
                softmax_parts(ch, v, v3(logits), m, sh)
                v.sem_inc(s_a, 1)
                v.wait_ge(s_b, 1)
                ch(v.tensor_reduce(s[:], v3(logits), AX, ALU.add))
                ch(v.reciprocal(s[:], s[:]))
                ch(v.tensor_tensor(v3(logits), v3(logits), over(s[:], sh), ALU.mult))
                ch(v.tensor_reduce(g[0], v3(logits), AX, ALU.max))
                first_of(ch, v, v3(o[0]), v3(logits), g[0], v3(tmp), io3, ix[0], sh)
                ch(v.scalar_tensor_tensor(v3(rest), v3(o[0]), -2.0, v3(logits), ALU.mult, ALU.add))
                ch(v.tensor_reduce(g[1], v3(rest), AX, ALU.max))
                first_of(ch, v, v3(o[1]), v3(rest), g[1], v3(tmp), io3, ix[1], sh)
                ch(v.tensor_tensor(both[:], o[0][:], o[1][:], ALU.add))
                v.sem_inc(s_oh, 1)
                ch(v.tensor_tensor(s[:], g[0], g[1], ALU.add))
                ch(v.reciprocal(s[:], s[:]))
                for j in range(2):
                    ch(v.tensor_tensor(g[j], g[j], s[:], ALU.mult))
                v.wait_ge(s_pf, 2)
                ch(v.tensor_copy(tmp[:], pA[0][0:P, 0:T * NE]))
                for e in range(NE):
                    ch(v.tensor_tensor_scan(v3(before)[:, :, e], C["ones"][0:P, 0:1].to_broadcast([P, T]),
                                            v3(tmp)[:, :, e], 0.0, ALU.mult, ALU.add))
                ch(v.tensor_scalar(first[:], v3(before)[:, T - 1, :], 127.0 - 63.5, 1.0 / 128, ALU.add, ALU.mult))
                ch(v.tensor_scalar(first[:], first[:], ROUND, ROUND, ALU.add, ALU.subtract))
                ch(v.tensor_tensor_scan(end[:], C["ones"][0:P, 0:1].to_broadcast([P, NE]), first[:], 0.0, ALU.mult,
                                        ALU.add))
                ch(v.tensor_tensor(first[:], end[:], first[:], ALU.subtract))
                ch(v.tensor_tensor(before[:], before[:], tmp[:], ALU.subtract))
                ch(v.tensor_tensor(before[:], before[:], pP[0][0:P, 0:T * NE], ALU.add))
                ch(v.memset(tiles[:], 0.0))
                for e in range(NE - 1):
                    ch(v.scalar_tensor_tensor(tiles[:], C["row"][0:1, 0:NTT_X], end[0:1, e:e + 1], tiles[:],
                                              ALU.is_ge, ALU.add))
                ch(v.tensor_copy(expert_i[:], tiles[:]))
                v.wait_ge(s_io, 1)
                for j in range(2):
                    ch(v.tensor_tensor(tmp[:], before[:], o[j][:], ALU.mult))
                    ch(v.tensor_reduce(pos[:], v3(tmp), AX, ALU.add))
                    ch(v.tensor_tensor(v3(tmp), v3(o[j]), first[:].unsqueeze(1).to_broadcast(sh), ALU.mult))
                    ch(v.tensor_reduce(hi[:], v3(tmp), AX, ALU.add))
                    ch(v.tensor_scalar(m[:], pos[:], -63.5, 1.0 / 128, ALU.add, ALU.mult))
                    ch(v.tensor_scalar(m[:], m[:], ROUND, ROUND, ALU.add, ALU.subtract))
                    ch(v.tensor_tensor(hi[:], hi[:], m[:], ALU.add))
                    ch(v.scalar_tensor_tensor(pos[:], m[:], -128.0, pos[:], ALU.mult, ALU.add))
                    ch(v.scalar_tensor_tensor(m[:], hi[:], 128.0, pos[:], ALU.mult, ALU.add))
                    ch(v.tensor_copy(slot[:, j * T:(j + 1) * T], m[:]))
                    for t in range(T):
                        k = j * T + t
                        v.wait_ge(s_map, mp.freed(k, 2))
                        v.tensor_scalar(lows[k % 2][:], C["row"][0:P, 0:128], pos[:, t:t + 1], None, ALU.is_equal)
                        v.tensor_scalar(highs[k % 2][:], C["row"][0:P, 0:NTT], hi[:, t:t + 1], node[:, t:t + 1],
                                        ALU.is_equal, ALU.mult).then_inc(s_hot, 1)
                    v.wait_ge(s_hot, T * (j + 1))
                v.wait_ge(s_map, mp.done(2 * T - 1))
                ch(v.tensor_copy(tokens[:], pM[0][:, 0:NTT]))


def gates2(nc, logits, gates):
    sh = [P, T, NE]
    with Phase(nc, "gate2") as ph:
        s_ch, s_a, s_b = ph.sem("ch"), ph.sem("a"), ph.sem("b")
        m, s = ph.sb("m", [P, T]), ph.sb("s", [P, T])
        v3 = lambda t: t[:].rearrange("p (t e) -> p t e", e=NE)
        with nc.Block() as block:

            @block.scalar
            def _(act):
                act.wait_ge(s_a, 1)
                act.activation(logits[:], logits[:], ACT.Exp).then_inc(s_b, 1)

            @block.vector
            def _(v):
                ch = Chain(v, s_ch)
                softmax_parts(ch, v, v3(logits), m, sh)
                v.sem_inc(s_a, 1)
                v.wait_ge(s_b, 1)
                ch(v.tensor_reduce(s[:], v3(logits), AX, ALU.add))
                ch(v.reciprocal(s[:], s[:]))
                ch(v.tensor_tensor(v3(gates), v3(logits), over(s[:], sh), ALU.mult))


def experts1(nc, C, table, tokens, expert_i, W1s, W2s, b1T, gT, bT, b2, ybuf):
    U = 4
    HB2 = FH // 512
    with Phase(nc, "exp1") as ph:
        s_row, s_cur, s_yt, s_yc, s_h, s_hc, s_ht, s_ga, s_o, s_oc = (
            ph.sem(n) for n in ("row", "cur", "yt", "yc", "h", "hc", "ht", "ga", "o", "oc"))
        s_st = ph.sems_of("st", U)
        s_g = [ph.pool_dma_sem(f"g{i}") for i in range(U)]
        b1s, b2s = ph.sb("b1", [128, NE * KF]), ph.sb("b2", [1, NE * D])
        gs, lbs = ph.sb("gs", [128, NE * KD]), ph.sb("lbs", [128, NE * KD])
        cur = ph.sb("cur", [128, U], I32)
        G = ph.ring("G", U, [128, D])
        yT = ph.ring("yT", 2, [128, KD * 128])
        hs, hT = ph.sb("h", [128, FH]), ph.sb("hT", [128, FH])
        ys = ph.ring("y", U, [128, D])
        pT, pH, pG, pO = ph.ps("pT"), ph.ps("pH", HB2), ph.ps("pG", HB2), ph.ps("pO", 2)
        yt, yc, h, hc, ht, ga, o, oc = (Count(s_yt, U), Count(s_yc), Count(s_h), Count(s_hc), Count(s_ht),
                                        Count(s_ga), Count(s_o, 2), Count(s_oc, 2))
        STEPS = NTT // U
        out = ybuf.rearrange("(k p) d -> p k d", p=128)
        with nc.Block() as block:

            @block.sync
            def _(sp):
                sp.dma_start(b1s[:], b1T).then_inc(s_row, 16)
                sp.dma_start(b2s[:], b2.rearrange("e d -> (e d)").unsqueeze(0)).then_inc(s_row, 16)
                sp.dma_start(gs[:], gT).then_inc(s_row, 16)
                sp.dma_start(lbs[:], bT).then_inc(s_row, 16)
                with sp.Fori(0, STEPS) as i:
                    for u in range(U):
                        k = i * U + u
                        sp.wait_ge(s_oc, oc.done(k))
                        sp.dma_start(out[:, ds(k, 1), :], ys[u][:].unsqueeze(1)).then_inc(s_st[u], 16)
                for u in range(U):
                    sp.wait_ge(s_st[u], (STEPS + 1) * 16)

            @block.gpsimd
            def _(pool):
                with pool.Fori(0, STEPS) as i:
                    for u in range(U):
                        pool.wait_ge(s_cur, i * U + u + 1)
                        pool.nop(nofuse=True)
                        pool.indirect_dma_start(out=G[u][:], out_offset=None, in_=table,
                                                in_offset=bass.IndirectOffsetOnAxis(ap=cur[:, u:u + 1], axis=0)
                                                ).then_inc(s_g[u], 16)

            @block.scalar
            def _(act):
                act.wait_ge(s_row, 64)
                regs = [act.alloc_register(f"exp1_act{u}") for u in range(U)]

                def fetch(k, u):
                    act.wait_ge(s_yt, yt.freed(k, U))
                    act.activation(cur[:, u:u + 1], tokens[:, ds(k, 1)], ACT.Copy).then_inc(s_cur, 1)

                def halves(k):
                    act.wait_ge(s_h, h.done(k))
                    act.activation(hs[:, FH // 2:], pH[1][:], ACT.Copy).then_inc(s_hc, 1)

                def hidden(k, e):
                    act.wait_ge(s_ht, ht.done(k))
                    for f in range(KF):
                        last = act.activation(hT[:, f * 128:(f + 1) * 128], pG[f // 4][:, f % 4 * 128:(f % 4 + 1) * 128],
                                              ACT.Gelu, bias=b1s[:, ds(e * KF + f, 1)])
                    last.then_inc(s_ga, 1)

                def step(i, last):
                    experts = blocks_of(act, regs, expert_i, i * U, NE - 1)
                    for u in range(U):
                        k = i * U + u
                        halves(k)
                        hidden(k, experts[u])
                        if not last:
                            fetch(k + U, u)

                for u in range(U):
                    fetch(u, u)
                with act.Fori(0, STEPS - 1) as i:
                    step(i, False)
                step(STEPS - 1, True)

            @block.tensor
            def _(pe):
                pe.sem_inc(s_yt, U)
                pe.sem_inc(s_o, 2)
                pe.wait_ge(s_row, 64)
                regs = [pe.alloc_register(f"exp1_pe{u}") for u in range(U + 2)]

                def turn(k, u, n, first=False):
                    pe.wait_ge(s_g[u], n)
                    if not first:
                        pe.wait_ge(s_yc, k)
                    for c in range(KD):
                        last = pe.transpose(pT[0][:, c * 128:(c + 1) * 128], G[u][:, c * 128:(c + 1) * 128], C["ident"][:])
                    last.then_inc(s_yt, 1)

                def first_layer(k, u, e):
                    pe.wait_ge(s_yc, yc.done(k))
                    for b in range(HB2):
                        for c in range(KD):
                            last = pe.matmul(pH[b][:], yT[u % 2][:, c * 128:(c + 1) * 128],
                                             W1s[:, ds(e * (KD * FH) + (c * FH + b * 512), 512)], start=(c == 0),
                                             stop=(c == KD - 1))
                    last.then_inc(s_h, 1)

                def turn_hidden(k):
                    pe.wait_ge(s_hc, k * 2 + 2)
                    for f in range(KF):
                        last = pe.transpose(pG[f // 4][:, f % 4 * 128:(f % 4 + 1) * 128], hs[:, f * 128:(f + 1) * 128],
                                            C["ident"][:])
                    last.then_inc(s_ht, 1)

                def second_layer(k, u, e):
                    pe.wait_ge(s_ga, ga.done(k))
                    pe.wait_ge(s_oc, oc.freed(k, 2))
                    for f in range(KF):
                        pe.matmul(pO[u % 2][:, 0:D], hT[:, f * 128:(f + 1) * 128],
                                  W2s[:, ds(e * (KF * D) + f * D, D)], start=(f == 0), stop=False)
                    pe.matmul(pO[u % 2][:, 0:D], C["ones"][0:1, :], b2s[:, ds(e * D, D)], start=False,
                              stop=True).then_inc(s_o, 1)

                def step(i, last):
                    experts = blocks_of(pe, regs, expert_i, i * U, NE - 1)
                    for u in range(U):
                        k = i * U + u
                        if not last or u + 1 < U:
                            first_layer(k + 1, u + 1, experts[u + 1])
                        if not last or u + 2 < U:
                            turn(k + 2, (u + 2) % U, i * 16 + 16 * ((u + 2) // U) + 16)
                        second_layer(k, u, experts[u])
                        if not last or u + 1 < U:
                            turn_hidden(k + 1)

                turn(0, 0, 16, first=True)
                e0 = blocks_of(pe, regs[:1], expert_i, 0, NE - 1)[0]
                first_layer(0, 0, e0)
                turn(1, 1, 16)
                turn_hidden(0)
                with pe.Fori(0, STEPS - 1) as i:
                    step(i, False)
                step(STEPS - 1, True)

            @block.vector
            def _(v):
                v.sem_inc(s_oc, 2)
                for u in range(U):
                    v.sem_inc(s_st[u], 16)
                v.wait_ge(s_row, 64)
                regs = [v.alloc_register(f"exp1_dve{u}") for u in range(U + 2)]

                def turned(k, u, e):
                    v.wait_ge(s_yt, yt.done(k))
                    for c in range(KD):
                        last = v.tensor_scalar(yT[u % 2][:, c * 128:(c + 1) * 128], pT[0][:, c * 128:(c + 1) * 128],
                                               gs[:, ds(e * KD + c, 1)], lbs[:, ds(e * KD + c, 1)], ALU.mult, ALU.add)
                    last.then_inc(s_yc, 1)

                def halves(k):
                    v.wait_ge(s_h, h.done(k))
                    v.tensor_copy(hs[:, 0:FH // 2], pH[0][:]).then_inc(s_hc, 1)

                def result(k, u, n):
                    v.wait_ge(s_o, o.done(k))
                    v.wait_ge(s_st[u], n)
                    v.tensor_copy(ys[u][:], pO[u % 2][:, 0:D]).then_inc(s_oc, 1)

                def step(i, last):
                    experts = blocks_of(v, regs, expert_i, i * U, NE - 1)
                    for u in range(U):
                        k = i * U + u
                        if not last or u + 1 < U:
                            halves(k + 1)
                        if not last or u + 2 < U:
                            turned(k + 2, u + 2, experts[u + 2])
                        result(k, u, i * 16 + 16)

                e01 = blocks_of(v, regs[:2], expert_i, 0, NE - 1)
                turned(0, 0, e01[0])
                halves(0)
                turned(1, 1, e01[1])
                with v.Fori(0, STEPS - 1) as i:
                    step(i, False)
                step(STEPS - 1, True)


def combine1(nc, ybuf, slot, gate, X):
    J = 5
    with Phase(nc, "comb1") as ph:
        s_x = ph.sem("x")
        s_g = [ph.pool_dma_sem(f"g{i}") for i in range(T // J)]
        YG = ph.sb("YG", [P, 2 * T * D])
        with nc.Block() as block:

            @block.gpsimd
            def _(pool):
                for t in range(T):
                    for j in range(2):
                        pool.indirect_dma_start(out=YG[:, (2 * t + j) * D:(2 * t + j + 1) * D], out_offset=None, in_=ybuf,
                                                in_offset=bass.IndirectOffsetOnAxis(
                                                    ap=slot[:, j * T + t:j * T + t + 1], axis=0)).then_inc(s_g[t // J], 16)

            @block.vector
            def _(v):
                for g in range(T // J):
                    v.wait_ge(s_g[g], 2 * J * 16)
                    for j in range(2):
                        if j:
                            v.wait_ge(s_x, J * (2 * g + 1))
                        for t in range(g * J, (g + 1) * J):
                            x = X[:, t * D:(t + 1) * D]
                            v.scalar_tensor_tensor(x, YG[:, (2 * t + j) * D:(2 * t + j + 1) * D],
                                                   gate[:, j * T + t:j * T + t + 1], x, ALU.mult,
                                                   ALU.add).then_inc(s_x, 1)


def ffn1(nc, C, X, rstd, nbias, dr, table, ybuf):
    with ExitStack() as st:
        sb = lambda n, s, d=F32: st.enter_context(nc.sbuf_tensor(f"f1_{n}", s, d))
        gate, slot = sb("gate", [P, 2 * T]), sb("slot", [P, 2 * T], I32)
        with ExitStack() as s2:
            sc = lambda n, s, d=F32: s2.enter_context(nc.sbuf_tensor(f"f1_{n}", s, d))
            tokens, expert_i = sc("tokens", [128, NTT]), sc("expert", [1, NTT_X], I32)
            logits, gw, gb = sc("logits", [P, T * NE]), sc("gw", [128, KD * NE]), sc("gb", [1, NE])
            W1s, W2s = sc("W1", [128, NE * KD * FH]), sc("W2", [128, NE * KF * D])
            half = NE // 2
            Y = W2s[0:P, NE * KF * D - T * D:]
            assert T * D <= (NE - half) * KF * D
            w1, w2 = dr["W1"].rearrange("e d f -> (e d) f"), dr["W2"].rearrange("e f d -> (e f) d")
            load_many(nc, [(gw[:].rearrange("p (c f) -> p c f", c=KD), dr["Wr"].rearrange("(c p) f -> p c f", p=128)),
                           (gb[:], dr["br"].unsqueeze(0))])
            row_stats(nc, X, rstd, nbias, 1e-5)
            project(nc, C, X, rstd, nbias, keep=Y, w=gw, F=NE, brow=gb[:], out=logits,
                    also=expert_weights(w1, w2, W1s, W2s, range(NE), range(half)))
            row_stats(nc, Y, rstd, nbias, 1e-5)
            normalise(nc, Y, rstd, nbias, Y)
            store_table(nc, Y, table, D)
            route1(nc, C, logits, expert_weights(w1, w2, W1s, W2s, (), range(half, NE)), gate, slot, tokens,
                   expert_i)
            experts1(nc, C, table, tokens, expert_i, W1s, W2s, dr["b1T"], dr["gT"], dr["bT"], dr["b2"], ybuf)
        combine1(nc, ybuf, slot, gate, X)


F2 = 264
S2 = NH * HD + NH


def edge_attention(nc, C, lew, ateT, EA):
    with Phase(nc, "eatt") as ph:
        s_in, s_bc, s_mm, s_ev = (ph.sem(n) for n in ("in", "bc", "mm", "ev"))
        le = ph.sb("le", [HD, NH * EF])
        at = ph.sb("at", [HD, NH])
        ab = ph.sb("ab", [HD, NH * 128])
        pE = ph.ps("pE", 1)
        with nc.Block() as block:

            @block.sync
            def _(sp):
                sp.dma_start(le[:].rearrange("p (h f) -> p h f", h=NH), lew.rearrange("(h p) f -> p h f", p=HD)).then_inc(s_in, 16)
                sp.dma_start(at[:], ateT).then_inc(s_in, 16)

            @block.vector
            def _(v):
                v.wait_ge(s_in, 32)
                v.tensor_copy(ab[:].rearrange("p (h m) -> p h m", h=NH), over(at[:], [HD, NH, 128])).then_inc(s_bc, 1)
                v.wait_ge(s_mm, 1)
                v.tensor_copy(EA[:], pE[0][:, 0:NH * EF]).then_inc(s_ev, 1)
                v.wait_ge(s_ev, 1)

            @block.tensor
            def _(pe):
                pe.wait_ge(s_in, 32)
                pe.wait_ge(s_bc, 1)
                for h in range(NH):
                    last = pe.matmul(pE[0][:, h * EF:(h + 1) * EF], ab[:, h * 128:(h + 1) * 128],
                                     le[:, h * EF:(h + 1) * EF], start=True, stop=True)
                last.then_inc(s_mm, 1)


def gnn2_weights(nc, lw, lwT, asT, adT, W):
    with Phase(nc, "w2") as ph:
        s_in, s_mm, s_ev = (ph.sem(n) for n in ("in", "mm", "ev"))
        nat = ph.sb("nat", [HD, NH * D])
        at = ph.sb("at", [HD, 2 * NH])
        pW = ph.ps("pW", KD)
        Wv = W[:].rearrange("p (c f) -> p c f", c=KD)
        with nc.Block() as block:

            @block.sync
            def _(sp):
                sp.dma_start(nat[:].rearrange("p (h d) -> p h d", h=NH), lw.rearrange("(h p) d -> p h d", p=HD)).then_inc(s_in, 16)
                sp.dma_start(at[:, 0:NH], asT).then_inc(s_in, 16)
                sp.dma_start(at[:, NH:2 * NH], adT).then_inc(s_in, 16)
                sp.dma_start(Wv[:, :, 0:D], lwT.rearrange("(c p) f -> p c f", p=128)).then_inc(s_in, 16)
                sp.wait_ge(s_in, 64)

            @block.tensor
            def _(pe):
                pe.wait_ge(s_in, 64)
                for c in range(KD):
                    for j in range(2 * NH):
                        h = j % NH
                        last = pe.matmul(pW[c][:, j:j + 1], nat[:, h * D + c * 128:h * D + (c + 1) * 128],
                                         at[:, j:j + 1], start=True, stop=True)
                    last.then_inc(s_mm, 1)

            @block.vector
            def _(v):
                v.wait_ge(s_mm, KD)
                v.wait_ge(s_in, 64)
                for c in range(KD):
                    v.tensor_copy(Wv[:, c, D:F2], pW[c][:, 0:2 * NH]).then_inc(s_ev, 1)
                v.wait_ge(s_ev, KD)


def gnn2_maxima(nc, C, hdr, blk_i, tscore, sorted_rows, eat, U, smax):
    R = 8
    RP = 4
    AHEAD = 3
    with Phase(nc, "max2") as ph:
        s_eat, s_cur, s_u, s_copy, s_msk, s_msk2, s_mm, s_red, s_max = (
            ph.sem(n) for n in ("eat", "cur", "u", "copy", "msk", "msk2", "mm", "red", "max"))
        s_g = [ph.pool_dma_sem(f"g{i}") for i in range(R)]
        cur = ph.sb("cur", [128, R], I32)
        G = ph.ring("G", R, [128, NH])
        pen = ph.ring("pen", 4, [128, P])
        msk = ph.ring("msk", 4, [128, NH * P])
        top = ph.ring("top", 2, [P, NH])
        us8 = ph.sb("us8", [128, R * NH])
        pS = ph.ps("pS", RP)
        cu, us, ms, mm, rd, mx = Count(s_cur), Count(s_u, R), Count(s_msk, R), Count(s_mm, R), Count(s_red, R), Count(s_max, R)
        with nc.Block() as block:

            @block.sync
            def _(sp):
                sp.sem_inc(s_eat, 16)
                with sp.Fori(0, NT // R) as i:
                    sp.wait_ge(s_eat, i * 16 + 16)
                    sp.dma_start(eat[:, ds(i * R * NH, R * NH)].rearrange("p (t h) -> p t h", h=NH),
                                 sorted_rows.rearrange("(t p) c -> p t c", p=LANES)[:, ds(i * R, R), EAT:EAT + NH]
                                 ).then_inc(s_eat, 16)

            @block.gpsimd
            def _(pool):
                with pool.Fori(0, NT // R) as i:
                    for u in range(R):
                        k = i * R + u
                        pool.wait_ge(s_cur, cu.done(k))
                        pool.nop(nofuse=True)
                        pool.indirect_dma_start(out=G[u][:], out_offset=None, in_=tscore,
                                                in_offset=bass.IndirectOffsetOnAxis(ap=cur[:, u:u + 1], axis=0)
                                                ).then_inc(s_g[u], 16)

            @block.scalar
            def _(act):
                act.sem_inc(s_msk, R)

                for u in range(R):
                    act.activation(cur[:, u:u + 1], hdrx(hdr, u), ACT.Copy).then_inc(s_cur, 1)
                with act.Fori(0, NT // R) as i:
                    for u in range(R):
                        k = i * R + u
                        act.wait_ge(s_u, us.done(k))
                        act.wait_ge(s_mm, mm.freed(k, 4))
                        for h in range(NH - 1):
                            last = act.activation(msk[u % 4][:, h * P:(h + 1) * P], pen[u % 4][:], ACT.Identity,
                                                  bias=us8[:, u * NH + h:u * NH + h + 1])
                        last.then_inc(s_msk, 1)
                        act.activation(cur[:, u:u + 1], hdrx(hdr, k + R), ACT.Copy).then_inc(s_cur, 1)

            @block.tensor
            def _(pe):
                pe.sem_inc(s_mm, R)
                with pe.Fori(0, NT // R) as i:
                    for u in range(R):
                        k = i * R + u
                        pe.wait_ge(s_msk, ms.done(k))
                        pe.wait_ge(s_msk2, k + 1)
                        pe.wait_ge(s_red, rd.freed(k, RP))
                        for h in range(NH):
                            last = pe.transpose(pS[u % RP][0:P, h * 128:(h + 1) * 128], msk[u % 4][:, h * P:(h + 1) * P],
                                                C["ident"][:])
                        last.then_inc(s_mm, 1)

            @block.vector
            def _(v):
                v.sem_inc(s_u, R)
                v.sem_inc(s_red, R)
                v.sem_inc(s_max, R)

                def prepare(i, k, u):
                    if u == 0:
                        v.wait_ge(s_eat, i * 16 + 32)
                    v.wait_ge(s_msk, ms.freed(k, 4))
                    v.tensor_scalar(pen[u % 4][:], C["nodes"][:], hdr[:, ds(k * HB + DL1, 1)], -BIG,
                                    ALU.not_equal, ALU.mult)
                    v.wait_ge(s_g[u], i * 16 + 16)
                    v.tensor_tensor(us8[:, u * NH:(u + 1) * NH], G[u][:], eat[:, ds(k * NH, NH)],
                                    ALU.add).then_inc(s_u, 1)

                regs = [v.alloc_register(f"max2_block{u}") for u in range(R)]

                def last_head(k, u):
                    v.wait_ge(s_u, us.done(k))
                    v.wait_ge(s_mm, mm.freed(k, 4))
                    h = NH - 1
                    v.tensor_scalar(msk[u % 4][:, h * P:(h + 1) * P], pen[u % 4][:], us8[:, u * NH + h:u * NH + h + 1],
                                    None, ALU.add).then_inc(s_msk2, 1)

                def largest(k, u):
                    v.wait_ge(s_mm, mm.done(k))
                    v.tensor_reduce(top[u % 2][:], pS[u % RP][0:P, :].rearrange("p (h e) -> p h e", h=NH), AX,
                                    ALU.max).then_inc(s_red, 1)

                def fold(k, u, b):
                    v.wait_ge(s_red, rd.done(k))
                    v.wait_ge(s_max, mx.freed(k, 1))
                    a = smax[:, ds(b * NH, NH)]
                    v.tensor_tensor(a, top[u % 2][:], a, ALU.max).then_inc(s_max, 1)

                def group(i, last):
                    blocks = blocks_of(v, regs, blk_i, i * R)
                    for u in range(R):
                        if u + AHEAD < R:
                            prepare(i, i * R + u + AHEAD, u + AHEAD)
                            if u + AHEAD == R - 1:
                                v.wait_ge(s_u, us.done(i * R + R - 1))
                                v.tensor_copy(U[:, ds(i * R * NH, R * NH)], us8[:]).then_inc(s_copy, 1)
                                v.wait_ge(s_copy, i + 1)
                        elif not last:
                            prepare(i + 1, i * R + u + AHEAD, u + AHEAD - R)
                        largest(i * R + u, u)
                        if u + AHEAD < R or not last:
                            last_head(i * R + u + AHEAD, (u + AHEAD) % R)
                        fold(i * R + u, u, blocks[u])

                for u in range(AHEAD):
                    prepare(0, u, u)
                    last_head(u, u)
                with v.Fori(0, NT // R - 1) as i:
                    group(i, False)
                group(NT // R - 1, True)
                v.wait_ge(s_max, NT + R)


def hdrx(hdr, k):
    return hdr[:, ds(k * HB + SRC, 1)].bitcast(I32)


def gnn2_spread(nc, C, hdr, blk_i, sd, SD):
    R = 4
    PAIRS = NT // 2
    TA, OA = 2, 3
    W = 2 * NH
    with Phase(nc, "spread2") as ph:
        s_oh, s_tr, s_ot, s_mm, s_sd = (ph.sem(n) for n in ("oh", "tr", "ot", "mm", "sd"))
        OH = ph.ring("OH", R, [128, 2 * P])
        OT = ph.ring("OT", R, [P, 2 * 128])
        pT, pD = ph.ps("pT", R), ph.ps("pD", 2)
        oh, tr, ot, mm = Count(s_oh), Count(s_tr, R), Count(s_ot, R), Count(s_mm, R)
        with nc.Block() as block:

            @block.vector
            def _(v):
                v.sem_inc(s_sd, 2)

                def prepare(m, w):
                    v.wait_ge(s_tr, tr.freed(m, R))
                    for j in range(2):
                        last = v.tensor_scalar(OH[w][:, j * P:(j + 1) * P], C["nodes"][:],
                                               hdr[:, ds((m * 2 + j) * HB + DL1, 1)], None, ALU.is_equal)
                    last.then_inc(s_oh, 1)

                for w in range(OA):
                    prepare(w, w)
                with v.Fori(0, PAIRS // R) as i:
                    for w in range(R):
                        m = i * R + w
                        prepare(m + OA, (w + OA) % R)
                        if w % 2 == 1:
                            v.wait_ge(s_mm, mm.done(m))
                            v.tensor_copy(SD[:, ds((m - 1) * 2 * W, 4 * W)], pD[w // 2][:, 0:4 * W]).then_inc(s_sd, 1)
                v.wait_ge(s_sd, PAIRS // 2 + 2)
                v.wait_ge(s_oh, PAIRS + OA)

            @block.tensor
            def _(pe):
                pe.sem_inc(s_tr, R)
                pe.sem_inc(s_mm, R)

                def transpose(m, w):
                    pe.wait_ge(s_oh, oh.done(m))
                    pe.wait_ge(s_ot, ot.freed(m, R))
                    for j in range(2):
                        last = pe.transpose(pT[w][0:P, j * 128:(j + 1) * 128], OH[w][:, j * P:(j + 1) * P], C["ident"][:])
                    last.then_inc(s_tr, 1)

                regs = [pe.alloc_register(f"spread2_block{u}") for u in range(2 * R)]
                for w in range(TA):
                    transpose(w, w)
                with pe.Fori(0, PAIRS // R) as i:
                    blocks = blocks_of(pe, regs, blk_i, i * (2 * R))
                    for w in range(R):
                        m = i * R + w
                        transpose(m + TA, (w + TA) % R)
                        pe.wait_ge(s_ot, ot.done(m))
                        if w % 2 == 0:
                            pe.wait_ge(s_sd, i * 2 + 1 + w // 2)
                        for j in range(2):
                            c = (w % 2 * 2 + j) * W
                            last = pe.matmul(pD[w // 2][:, c:c + W], OT[w][:, j * 128:(j + 1) * 128],
                                             sd[:, ds(blocks[w * 2 + j] * W, W)], start=True, stop=True)
                        last.then_inc(s_mm, 1)

            @block.scalar
            def _(act):
                act.sem_inc(s_ot, R)

                def copy(m, w):
                    act.wait_ge(s_tr, tr.done(m))
                    act.wait_ge(s_mm, mm.freed(m, R))
                    act.activation(OT[w][:], pT[w][0:P, 0:256], ACT.Copy).then_inc(s_ot, 1)

                with act.Fori(0, PAIRS // R) as i:
                    for w in range(R):
                        copy(i * R + w, w)
                for w in range(TA):
                    copy(PAIRS + w, (PAIRS + w) % R)


def gnn2_weigh(nc, U, SD, ex):
    with Phase(nc, "weigh2") as ph:
        s_ch, s_v, s_e = ph.sem("ch"), ph.sem("v"), ph.sem("e")
        n = NT * NH
        u3 = U[:].rearrange("p (t h) -> p t h", h=NH)
        d3 = SD[:].rearrange("p (t h) -> p t h", h=2 * NH)
        x3 = ex[:, 0:n].rearrange("p (t h) -> p t h", h=NH)
        with nc.Block() as block:

            @block.vector
            def _(v):
                ch = Chain(v, s_ch)
                ch(v.tensor_tensor(x3, u3, d3[:, :, 0:NH], ALU.add))
                ch(v.scalar_tensor_tensor(x3, x3, 0.2, x3, ALU.mult, ALU.max))
                ch(v.tensor_tensor(x3, x3, d3[:, :, NH:2 * NH], ALU.subtract))
                ch(v.tensor_scalar(x3, x3, 0.0, None, ALU.min))
                ch(v.memset(ex[:, n:], 0.0))
                v.sem_inc(s_v, 1)

            @block.scalar
            def _(act):
                act.wait_ge(s_v, 1)
                act.activation(ex[:, 0:n], ex[:, 0:n], ACT.Exp).then_inc(s_e, 1)
                act.wait_ge(s_e, 1)


def gnn2_prepare(nc, tab, smax):
    with Phase(nc, "prep2") as ph:
        s = ph.sem("s")
        t3 = tab[:].rearrange("p (t f) -> p t f", f=F2)
        with nc.Block() as block:

            @block.vector
            def _(v):
                v.tensor_copy(smax[:].rearrange("p (t h) -> p t h", h=NH), t3[:, :, D:D + NH]).then_inc(s, 1)
                v.wait_ge(s, 1)


def gnn2_own(nc, tab, smax, sd, acc):
    with Phase(nc, "own2") as ph:
        s_ch, s_v, s_e = ph.sem("ch"), ph.sem("v"), ph.sem("e")
        own = ph.sb("own", [P, T * NH])
        t3 = tab[:].rearrange("p (t f) -> p t f", f=F2)
        m3 = smax[:].rearrange("p (t h) -> p t h", h=NH)
        sd3 = sd[:].rearrange("p (t h) -> p t h", h=2 * NH)
        o3 = own[:].rearrange("p (t h) -> p t h", h=NH)
        a3 = acc[:].rearrange("p (t s) -> p t s", s=S2)
        with nc.Block() as block:

            @block.vector
            def _(v):
                ch = Chain(v, s_ch)
                ch(v.tensor_copy(sd3[:, :, 0:NH], t3[:, :, D + NH:F2]))
                ch(v.tensor_tensor(m3, m3, sd3[:, :, 0:NH], ALU.add))
                ch(v.scalar_tensor_tensor(sd3[:, :, NH:2 * NH], m3, 0.2, m3, ALU.mult, ALU.max))
                ch(v.tensor_tensor(o3, t3[:, :, D:D + NH], sd3[:, :, 0:NH], ALU.add))
                ch(v.scalar_tensor_tensor(o3, o3, 0.2, o3, ALU.mult, ALU.max))
                ch(v.tensor_tensor(o3, o3, sd3[:, :, NH:2 * NH], ALU.subtract))
                v.sem_inc(s_v, 1)
                v.wait_ge(s_e, 1)
                for h in range(NH):
                    ch(v.tensor_tensor(a3[:, :, h * HD:(h + 1) * HD], t3[:, :, h * HD:(h + 1) * HD],
                                       over(o3[:, :, h], [P, T, HD]), ALU.mult))
                ch(v.tensor_copy(a3[:, :, NH * HD:S2], o3))

            @block.scalar
            def _(act):
                act.wait_ge(s_v, 1)
                act.activation(own[:], own[:], ACT.Exp).then_inc(s_e, 1)


def gnn2_sum(nc, C, hdr, blk_i, table, ex, acc):
    R = 8
    RP = 4
    with Phase(nc, "sum2") as ph:
        s_cur, s_oh, s_w, s_mm, s_acc = (ph.sem(n) for n in ("cur", "oh", "w", "mm", "acc"))
        s_g = [ph.pool_dma_sem(f"g{i}") for i in range(R)]
        cur = ph.sb("cur", [128, R], I32)
        G = ph.ring("G", R, [128, D])
        OH = ph.ring("OH", RP, [128, P])
        Wt = ph.ring("Wt", RP, [128, S2])
        pS = ph.ps("pS", RP)
        cu, wt, mm, ac = Count(s_cur), Count(s_w, R), Count(s_mm, R), Count(s_acc, R)
        with nc.Block() as block:

            @block.gpsimd
            def _(pool):
                with pool.Fori(0, NT // R) as i:
                    for u in range(R):
                        k = i * R + u
                        pool.wait_ge(s_cur, cu.done(k))
                        pool.nop(nofuse=True)
                        pool.indirect_dma_start(out=G[u][:], out_offset=None, in_=table,
                                                in_offset=bass.IndirectOffsetOnAxis(ap=cur[:, u:u + 1], axis=0)
                                                ).then_inc(s_g[u], 16)

            @block.scalar
            def _(act):
                act.sem_inc(s_w, R)
                for u in range(R - 1):
                    act.activation(cur[:, u:u + 1], hdrx(hdr, u), ACT.Copy).then_inc(s_cur, 1)
                with act.Fori(0, NT // R) as i:
                    for u in range(R):
                        k = i * R + u
                        act.wait_ge(s_w, wt.freed(k, 1))
                        act.wait_ge(s_oh, k * 3 + R)
                        c = (u - 1) % R
                        act.activation(cur[:, c:c + 1], hdrx(hdr, k + R - 1), ACT.Copy).then_inc(s_cur, 1)
                        act.wait_ge(s_g[u], i * 16 + 16)
                        act.wait_ge(s_mm, mm.freed(k, RP))
                        for h in range(NH // 2):
                            last = act.activation(Wt[u % RP][:, h * HD:(h + 1) * HD], G[u][:, h * HD:(h + 1) * HD],
                                                  ACT.Copy, scale=ex[:, ds(k * NH + h, 1)])
                        last.then_inc(s_w, 1)

            @block.vector
            def _(v):
                v.sem_inc(s_acc, R)
                v.sem_inc(s_oh, R)

                def prepare(k, u, n):
                    v.wait_ge(s_mm, mm.freed(k, RP))
                    v.tensor_scalar(OH[u % RP][:], C["nodes"][:], hdr[:, ds(k * HB + DL1, 1)], None, ALU.is_equal).then_inc(s_oh, 1)
                    v.tensor_copy(Wt[u % RP][:, NH * HD:S2], ex[:, ds(k * NH, NH)]).then_inc(s_oh, 1)
                    h = NH // 2
                    v.wait_ge(s_g[u], n)
                    v.tensor_tensor(Wt[u % RP][:, h * HD:NH * HD].rearrange("p (h f) -> p h f", f=HD),
                                    G[u][:, h * HD:NH * HD].rearrange("p (h f) -> p h f", f=HD),
                                    over(ex[:, ds(k * NH + h, h)], [128, h, HD]), ALU.mult).then_inc(s_oh, 1)

                for u in range(LAG):
                    prepare(u, u, 16)

                regs = [v.alloc_register(f"sum2_block{u}") for u in range(R)]

                def group(i, last):
                    blocks = blocks_of(v, regs, blk_i, i * R)
                    for u in range(R):
                        k = i * R + u
                        if u + LAG < R:
                            prepare(k + LAG, u + LAG, i * 16 + 16)
                        elif not last:
                            prepare(k + LAG, u + LAG - R, i * 16 + 32)
                        v.wait_ge(s_mm, mm.done(k))
                        v.wait_ge(s_acc, ac.freed(k, 1))
                        a = acc[:, ds(blocks[u] * S2, S2)]
                        v.tensor_tensor(a, pS[u % RP][0:P, 0:S2], a, ALU.add).then_inc(s_acc, 1)

                with v.Fori(0, NT // R - 1) as i:
                    group(i, False)
                group(NT // R - 1, True)
                v.wait_ge(s_acc, NT + R)

            @block.tensor
            def _(pe):
                pe.sem_inc(s_mm, R)
                with pe.Fori(0, NT // R) as i:
                    for u in range(R):
                        k = i * R + u
                        pe.wait_ge(s_oh, k * 3 + 3 + R)
                        pe.wait_ge(s_w, wt.done(k))
                        pe.wait_ge(s_acc, ac.freed(k, RP))
                        pe.matmul(pS[u % RP][0:P, 0:S2], OH[u % RP][:], Wt[u % RP][:], start=True, stop=True).then_inc(s_mm, 1)


def gnn2_update(nc, acc, brow, X):
    with Phase(nc, "upd2") as ph:
        s_ch = ph.sem("ch")
        den = ph.sb("den", [P, T * NH])
        a3 = acc[:].rearrange("p (t s) -> p t s", s=S2)
        x3 = X[:].rearrange("p (t d) -> p t d", d=D)
        d3 = den[:].rearrange("p (t h) -> p t h", h=NH)
        with nc.Block() as block:

            @block.vector
            def _(v):
                ch = Chain(v, s_ch)
                ch(v.tensor_scalar(d3, a3[:, :, NH * HD:S2], 1e-12, None, ALU.add))
                ch(v.reciprocal(den[:], den[:]))
                for h in range(NH):
                    m = a3[:, :, h * HD:(h + 1) * HD]
                    ch(v.tensor_tensor(m, m, over(d3[:, :, h], [P, T, HD]), ALU.mult))
                ch(v.tensor_tensor(x3, x3, a3[:, :, 0:D], ALU.add))
                ch(v.tensor_tensor(x3, x3, brow[:].unsqueeze(1).to_broadcast([P, T, D]), ALU.add))


def gnn2(nc, C, hdr, blk_i, X, rstd, nbias, dr, sorted_rows, table, tscore):
    with ExitStack() as st:
        sb = lambda n, s: st.enter_context(nc.sbuf_tensor(f"g2_{n}", s, F32))
        tab, W, brow = sb("tab", [P, T * F2]), sb("W", [128, KD * F2]), sb("brow", [P, D])
        eat, U, SD = sb("eat", [128, NT * NH]), sb("U", [128, NT * NH]), sb("SD", [128, NT * 2 * NH])
        smax, sd, acc, ex = sb("smax", [P, T * NH]), sb("sd", [P, T * 2 * NH]), sb("acc", [P, T * S2]), sb("ex", [128, NTL * NH])
        gnn2_weights(nc, dr["lin_W"], dr["lin_WT"], dr["asT"], dr["adT"], W)
        row_stats(nc, X, rstd, nbias, 1e-5)
        project(nc, C, X, rstd, nbias, w=W, F=F2, out=tab, store=[(table, 0), (tscore, D)],
                also=[(brow[:], dr["bias"].unsqueeze(0).to_broadcast([P, D]))])
        gnn2_prepare(nc, tab, smax)
        gnn2_maxima(nc, C, hdr, blk_i, tscore, sorted_rows, eat, U, smax)
        gnn2_own(nc, tab, smax, sd, acc)
        gnn2_spread(nc, C, hdr, blk_i, sd, SD)
        gnn2_weigh(nc, U, SD, ex)
        gnn2_sum(nc, C, hdr, blk_i, table, ex, acc)
        gnn2_update(nc, acc, brow, X)


def experts2(nc, C, YT, gates, wts, cols, bo, X):
    with Phase(nc, "exp2") as ph:
        s_row, s_ch, s_sq, s_dv, s_h, s_ha, s_y, s_yv = (ph.sem(n) for n in ("row", "ch", "sq", "dv", "h", "ha", "y", "yv"))
        s_gt, s_gc = ph.sem("gt"), ph.sem("gc")
        s_ld = ph.sems_of("ld", 2)
        cs = {n: ph.sb(n, [128, NE * KD]) for n in cols}
        eps = 0.001
        bos = ph.sb("bo", [NE, D])
        gT = ph.ring("gT", 2, [NE, P])
        ws = [ph.ring(f"w{l}", 2, [128, KD * D]) for l in range(3)]
        hid = [ph.sb(f"h{l}", [128, KD * QN]) for l in range(2)]
        pHa, pHb, pY = ph.ps("pHa", 2), ph.ps("pHb", 2), ph.ps("pY", 3)
        NK = Q * Q
        HS = 2 * KD
        h, ha, y, yv = Count(s_h), Count(s_ha, 2), Count(s_y, 2 * NK), Count(s_yv, 3)
        with nc.Block() as block:

            @block.sync
            def _(sp):
                for n in cols:
                    sp.dma_start(cs[n][:], cols[n]).then_inc(s_row, 16)
                sp.dma_start(bos[:], bo).then_inc(s_row, 16)
                with sp.Fori(0, NE // 2) as i:
                    for s in range(2):
                        e = i * 2 + s
                        sp.wait_ge(s_y, e * NK + NK)
                        for l in range(3):
                            sp.dma_start(ws[l][s][:].rearrange("p (c f) -> p c f", c=KD),
                                         wts[l][ds(e * D, D), :].rearrange("(c p) f -> p c f", p=128)).then_inc(s_ld[s], 16)

            @block.tensor
            def _(pe):
                pe.sem_inc(s_y, 2 * NK)
                pe.wait_ge(s_row, 16 * (len(cols) + 1))

                def layer(l, s, q, m):
                    if l:
                        pe.wait_ge(s_ha, ha.done(m - 1))
                    for f in range(KD):
                        pe.wait_ge(s_ha, ha.freed(m + f, 2))
                        for bank, a, w in ((pHa, 0, QA), (pHb, QA, QN - QA)):
                            for c in range(KD):
                                rhs = (YT[:, ds(q * QN + c * N + a, w)] if l == 0
                                       else hid[0][:, c * QN + a:c * QN + a + w])
                                last = pe.matmul(bank[f % 2][:, 0:w],
                                                 ws[l][s][:, c * D + f * 128:c * D + (f + 1) * 128], rhs,
                                                 start=(c == 0), stop=(c == KD - 1))
                        last.then_inc(s_h, 1)

                def results(s, n):
                    for j in range(Q):
                        pe.wait_ge(s_yv, n * Q + j + 1 + 3 - (2 if j < 2 else 3))
                        if j == 0:
                            pe.wait_ge(s_ha, ha.done(n * HS + HS - 1))
                        for c in range(KD):
                            last = pe.matmul(pY[j % 3][0:P, 0:D], hid[1][:, c * QN + j * P:c * QN + (j + 1) * P],
                                             ws[2][s][:, c * D:(c + 1) * D], start=(c == 0), stop=(c == KD - 1))
                        last.then_inc(s_y, 1)

                def expert(i, s, last):
                    e = i * 2 + s
                    with pe.Fori(0, Q - 1) as q:
                        n = e * Q + q
                        pe.nop(nofuse=True)
                        layer(1, s, q, n * HS + KD)
                        layer(0, s, q + 1, n * HS + 2 * KD)
                        results(s, n)
                    n = e * Q + Q - 1
                    layer(1, s, Q - 1, n * HS + KD)
                    if not last:
                        pe.wait_ge(s_ld[1 - s], (i + s) * 48 + 48)
                        layer(0, 1 - s, 0, n * HS + 2 * KD)
                    results(s, n)

                pe.wait_ge(s_ld[0], 48)
                layer(0, 0, 0, 0)
                with pe.Fori(0, NE // 2 - 1) as i:
                    expert(i, 0, False)
                    expert(i, 1, False)
                expert(NE // 2 - 1, 0, False)
                expert(NE // 2 - 1, 1, True)
                pe.wait_ge(s_yv, NE * NK + 3)
                for t in range(T):
                    k = NE * NK + t
                    pe.wait_ge(s_yv, k - 1 + 3)
                    pe.transpose(pHa[t % 2][0:NE, 0:P], gates[:, t * NE:(t + 1) * NE], C["ident"][0:P, 0:P]).then_inc(s_gt, 1)
                    pe.wait_ge(s_gc, t + 1)
                    pe.matmul(pY[t % 2][0:P, 0:D], gT[t % 2][:], bos[:], start=True, stop=True).then_inc(s_y, 1)

            @block.scalar
            def _(act):
                act.wait_ge(s_dv, 1)
                for l in "12":
                    act.activation(cs["v" + l][:], cs["v" + l][:], ACT.Sqrt).then_inc(s_sq, 1)
                act.sem_inc(s_ha, 2)
                act.wait_ge(s_dv, 2)

                def piece(l, e, f, m):
                    act.wait_ge(s_h, h.done(m))
                    g, b = (cs[x + "12"[l]][:, ds(e * KD + f, 1)] for x in ("g", "b"))
                    act.activation(hid[l][:, f * QN:f * QN + QA], pHa[f % 2][:, 0:QA], ACT.Relu, bias=b, scale=g)
                    act.activation(hid[l][:, f * QN + QA:(f + 1) * QN], pHb[f % 2][:, 0:QN - QA],
                                   ACT.Relu, bias=b, scale=g).then_inc(s_ha, 1)

                def group(e, n, after):
                    for l, x in ((1, e), (0, after)):
                        if x is not None:
                            for f in range(KD):
                                piece(l, x, f, n * HS + (2 - l) * KD + f)

                for f in range(KD):
                    piece(0, 0, f, f)
                with act.Fori(0, NE - 1) as e:
                    with act.Fori(0, Q - 1) as q:
                        group(e, e * Q + q, e)
                    group(e, e * Q + Q - 1, e + 1)
                e = NE - 1
                with act.Fori(0, Q - 1) as q:
                    group(e, q + e * Q, e)
                group(e, e * Q + Q - 1, None)
                for t in range(T):
                    act.wait_ge(s_gt, t + 1)
                    act.wait_ge(s_y, 2 * NK + NE * NK + t - 1)
                    act.activation(gT[t % 2][:], pHa[t % 2][0:NE, 0:P], ACT.Copy).then_inc(s_gc, 1)

            @block.vector
            def _(v):
                ch = Chain(v, s_ch)
                v.wait_ge(s_row, 16 * (len(cols) + 1))
                for l in "12":
                    ch(v.tensor_scalar(cs["v" + l][:], cs["v" + l][:], eps, None, ALU.add))
                v.sem_inc(s_dv, 1)
                v.wait_ge(s_sq, 2)
                for l in "12":
                    ch(v.reciprocal(cs["v" + l][:], cs["v" + l][:]))
                    ch(v.tensor_tensor(cs["g" + l][:], cs["g" + l][:], cs["v" + l][:], ALU.mult))
                    ch(v.tensor_tensor(cs["b" + l][:], cs["b" + l][:], cs["m" + l][:], ALU.subtract))
                    ch(v.tensor_tensor(cs["b" + l][:], cs["b" + l][:], cs["g" + l][:], ALU.mult))
                    ch(v.tensor_tensor(cs["b" + l][:], cs["b" + l][:], cs["be" + l][:], ALU.add))
                v.sem_inc(s_dv, 1)
                v.sem_inc(s_yv, 3)
                with v.Fori(0, NE // 2) as i:
                    for s in range(2):
                        e = i * 2 + s
                        with v.Fori(0, Q) as q:
                            for j in range(Q):
                                k = (e * Q + q) * Q + j
                                t = q * Q + j
                                v.wait_ge(s_y, y.done(k))
                                v.wait_ge(s_yv, yv.freed(k, 1))
                                v.scalar_tensor_tensor(X[:, ds(t * D, D)], pY[j % 3][0:P, 0:D],
                                                       gates[:, ds(t * NE + e, 1)], X[:, ds(t * D, D)], ALU.mult,
                                                       ALU.add).then_inc(s_yv, 1)
                for t in range(T):
                    k = NE * NK + t
                    v.wait_ge(s_y, y.done(k))
                    v.wait_ge(s_yv, yv.freed(k, 1))
                    v.tensor_tensor(X[:, t * D:(t + 1) * D], pY[t % 2][0:P, 0:D], X[:, t * D:(t + 1) * D],
                                    ALU.add).then_inc(s_yv, 1)
                v.wait_ge(s_yv, NE * NK + T + 3)


def ffn2(nc, C, X, rstd, nbias, dr):
    with ExitStack() as st:
        sb = lambda n, s, d=F32: st.enter_context(nc.sbuf_tensor(f"f2_{n}", s, d))
        gates, YT = sb("gates", [P, T * NE]), sb("YT", [128, KD * N])
        with ExitStack() as s2:
            sc = lambda n, s: s2.enter_context(nc.sbuf_tensor(f"f2_{n}", s, F32))
            logits, gw, gb = sc("logits", [P, T * NE]), sc("gw", [128, KD * NE]), sc("gb", [1, NE])
            load_many(nc, [(gw[:].rearrange("p (c f) -> p c f", c=KD), dr["Wr"].rearrange("(c p) f -> p c f", p=128)),
                           (gb[:], dr["br"].unsqueeze(0))])
            row_stats(nc, X, rstd, nbias, 1e-5)
            project(nc, C, X, rstd, nbias, w=gw, F=NE, brow=gb[:], out=logits, keepT=YT)
            gates2(nc, logits, gates)
        cols = {n: dr[n + "T"] for n in ("b1", "g1", "be1", "m1", "v1", "b2", "g2", "be2", "m2", "v2")}
        experts2(nc, C, YT, gates, [dr[n].rearrange("e d f -> (e d) f") for n in ("W1", "W2", "Wo")], cols, dr["bo"], X)


R3 = 16
C3 = 64
INV3 = 1.0 / float(np.sqrt(np.float32(3.0)))


def normalise_by_axis(nc, src, rstd, nbias, out):
    with Phase(nc, "norm3") as ph:
        s_a, s_v = ph.sem("a"), ph.sem("v")
        with nc.Block() as block:

            @block.vector
            def _(v):
                with v.Fori(0, T // 5) as i:
                    for u in range(5):
                        k = i * 5 + u
                        v.tensor_scalar(out[:, ds(k * D, C3)], src[:, ds(k * D, C3)], rstd[:, ds(k, 1)], nbias[:, ds(k, 1)],
                                        ALU.mult, ALU.add).then_inc(s_v, 1)
                v.wait_ge(s_v, T)

            @block.scalar
            def _(act):
                with act.Fori(0, T // 5) as i:
                    for u in range(5):
                        k = i * 5 + u
                        act.activation(out[:, ds(k * D + C3, 3 * C3)].rearrange("p (a c) -> p a c", a=3),
                                       src[:, ds(k * D + C3, 3 * C3)].rearrange("p (c a) -> p a c", a=3), ACT.Identity,
                                       bias=nbias[:, ds(k, 1)], scale=rstd[:, ds(k, 1)]).then_inc(s_a, 1)
                act.wait_ge(s_a, T)


def block_weights(nc, W, F, parts):
    with Phase(nc, "wblock") as ph:
        s_z, s_in = ph.sem("z"), ph.sem("in")
        with nc.Block() as block:

            @block.vector
            def _(v):
                v.memset(W[:], 0.0).then_inc(s_z, 1)

            @block.sync
            def _(sp):
                sp.wait_ge(s_z, 1)
                for col, w0, w1 in parts:
                    for b in range(4):
                        a = (b // 2) * F + col + b * C3
                        sp.dma_start(W[(b % 2) * C3:(b % 2 + 1) * C3, a:a + C3], w0 if b == 0 else w1).then_inc(s_in, 16)
                sp.wait_ge(s_in, 16 * 4 * len(parts))


def gnn3_sum(nc, C, hdr, blk_i, table, sorted_rows, dr, acc):
    B = 8
    H = B // 2
    GROUPS = NT // B
    with Phase(nc, "sum3") as ph:
        s_w, s_z, s_rbf, s_cur, s_oh, s_rt, s_re, s_h, s_he, s_tp, s_q0, s_q, s_xs, s_msg, s_mm, s_acc = (
            ph.sem(n) for n in ("w", "z", "rbf", "cur", "oh", "rt", "re", "h", "he", "tp", "q0", "q", "xs", "msg", "mm",
                                "acc"))
        s_g = [ph.pool_dma_sem(f"g{i}") for i in range(B)]
        W1 = ph.sb("W1", [128, H * 128])
        Wm = [ph.sb(f"Wm{j}", [128, 128]) for j in range(2)]
        W4 = ph.sb("W4", [128, 4 * C3])
        rbf = ph.sb("rbf", [128, B * R3])
        rT = ph.sb("rT", [B * R3, 128])
        hs = [ph.sb(f"hs{j}", [2 * C3, H * 128]) for j in range(3)]
        cur = ph.sb("cur", [128, B], I32)
        G = ph.ring("G", B, [128, D])
        OH = ph.ring("OH", B, [128, P])
        dl = ph.sb("dl", [128, B])
        pq = ph.ring("pq", 4, [128, 2 * C3])
        xs = ph.ring("xs", 4, [128, 3 * C3])
        qq = ph.ring("qq", B, [128, C3])
        ms = ph.ring("ms", 4, [128, D])
        pR, pH, pT, pS = ph.ps("pR"), ph.ps("pH"), ph.ps("pT", 4), ph.ps("pS", 2)
        STEPS = 5
        cu, mm, ac, tp, q0, msg = (Count(s_cur), Count(s_mm, B), Count(s_acc, B), Count(s_tp),
                                       Count(s_q0), Count(s_msg, B))
        rows = sorted_rows.rearrange("(t p) c -> p t c", p=LANES)

        def radial(i):
            return rows[:, ds(i * B, B), RBF:RBF + R3]

        with nc.Block() as block:

            @block.sync
            def _(sp):
                sp.wait_ge(s_z, 1)
                for t in range(B):
                    j, half = t % H, t // H
                    sp.dma_start(W1[t * R3:(t + 1) * R3, j * 128 + half * C3:j * 128 + (half + 1) * C3],
                                 dr["M1"]).then_inc(s_w, 16)
                for half in range(2):
                    r = slice(half * C3, (half + 1) * C3)
                    for j in range(2):
                        sp.dma_start(Wm[j][r, r], dr[f"M{j + 2}"]).then_inc(s_w, 16)
                    sp.dma_start(W4[r, :], dr["M4"]).then_inc(s_w, 16)
                sp.dma_start(rbf[:].rearrange("p (t c) -> p t c", t=B), radial(0)).then_inc(s_rbf, 16)
                with sp.Fori(0, GROUPS - 1) as i:
                    sp.wait_ge(s_rt, i + 1)
                    sp.dma_start(rbf[:].rearrange("p (t c) -> p t c", t=B), radial(i + 1)).then_inc(s_rbf, 16)

            @block.gpsimd
            def _(pool):
                pool.sem_inc(s_oh, 1)
                with pool.Fori(0, GROUPS) as i:
                    for u in range(B):
                        k = i * B + u
                        pool.wait_ge(s_cur, cu.done(k))
                        pool.nop(nofuse=True)
                        pool.indirect_dma_start(out=G[u][:], out_offset=None, in_=table,
                                                in_offset=bass.IndirectOffsetOnAxis(ap=cur[:, u:u + 1], axis=0)
                                                ).then_inc(s_g[u], 16)
                        if u == 0:
                            pool.wait_ge(s_oh, i * (B + 1) + 1)
                            pool.tensor_copy(dl[:], hdr[:, ds(i * B * HB, B * HB)].rearrange(
                                "p (t c) -> p t c", c=HB)[:, :, DL1]).then_inc(s_oh, 1)
                            pool.wait_ge(s_oh, i * (B + 1) + 2)
                        pool.wait_ge(s_mm, mm.freed(k, B))
                        pool.nop(nofuse=True)
                        pool.tensor_scalar(OH[u][:], C["nodes"][:], dl[:, u:u + 1], None,
                                           ALU.is_equal).then_inc(s_oh, 1)

            @block.scalar
            def _(act):
                def network(i):
                    act.wait_ge(s_rt, i + 1)
                    act.activation(rT[:], pR[0][:, 0:128], ACT.Copy).then_inc(s_re, 1)
                    yield
                    for j in range(3):
                        act.wait_ge(s_h, i * 3 + j + 1)
                        act.activation(hs[j][:], pH[0][:], ACT.Silu).then_inc(s_he, 1)
                        yield

                def fetch(k, u):
                    act.wait_ge(s_msg, msg.freed(k, B))
                    act.activation(cur[:, u:u + 1], hdrx(hdr, k), ACT.Copy).then_inc(s_cur, 1)

                def first_part(k, u):
                    act.wait_ge(s_g[u], (k - u) * 2 + 16)
                    act.activation(qq[u][:], G[u][:, C3:2 * C3], ACT.Copy,
                                   scale=hdr[:, ds(k * HB + SH + 1, 1)]).then_inc(s_q0, 1)

                def scalars_part(k, u):
                    act.wait_ge(s_q, k * STEPS + 2)
                    act.nop(nofuse=True)
                    for a in range(3):
                        last = act.activation(xs[u % 4][:, a * C3:(a + 1) * C3], pq[u % 4][:, C3:], ACT.Copy,
                                              scale=hdr[:, ds(k * HB + SH + 1 + a, 1)])
                    last.then_inc(s_xs, 1)

                AHEAD = 3
                for u in range(B):
                    fetch(u, u)
                for _ in network(0):
                    pass
                for u in range(AHEAD):
                    first_part(u, u)
                scalars_part(0, 0)

                def group(i, last):
                    steps = iter(()) if last else network(i + 1)
                    for u in range(B):
                        if u + AHEAD < B or not last:
                            first_part(i * B + u + AHEAD, (u + AHEAD) % B)
                        if u + 1 < B or not last:
                            scalars_part(i * B + u + 1, (u + 1) % B)
                        next(steps, None)
                        if not last:
                            fetch(i * B + B + u, u)

                with act.Fori(0, GROUPS - 1) as i:
                    group(i, False)
                group(GROUPS - 1, True)

            @block.tensor
            def _(pe):
                def network(i):
                    pe.wait_ge(s_rbf, i * 16 + 16)
                    pe.transpose(pR[0][:, 0:128], rbf[:], C["ident"][:]).then_inc(s_rt, 1)
                    yield
                    pe.wait_ge(s_re, i + 1)
                    for j in range(H):
                        last = pe.matmul(pH[0][:, j * 128:(j + 1) * 128], W1[:, j * 128:(j + 1) * 128], rT[:], start=True,
                                         stop=True)
                    last.then_inc(s_h, 1)
                    yield
                    for j in range(2):
                        pe.wait_ge(s_he, i * 3 + j + 1)
                        pe.matmul(pH[0][:], Wm[j][:], hs[j][:], start=True, stop=True).then_inc(s_h, 1)
                        yield

                def path_weights(u):
                    half, c = u // H, u % H
                    r = slice(half * C3, (half + 1) * C3)
                    pe.matmul(pT[u % 4][:, 0:4 * C3], hs[2][r, c * 128:(c + 1) * 128], W4[r, :], start=True,
                              stop=True).then_inc(s_tp, 1)

                def group(i, last):
                    steps = iter(()) if last else network(i + 1)
                    next(steps, None)
                    for u in range(B):
                        k = i * B + u
                        pe.wait_ge(s_msg, msg.done(k))
                        pe.wait_ge(s_oh, i * (B + 1) + 1 + 2 + u)
                        pe.wait_ge(s_acc, ac.freed(k, 2))
                        pe.matmul(pS[u % 2][0:P, 0:D], OH[u][:], ms[u % 4][:], start=True, stop=False)
                        pe.wait_ge(s_xs, k + 1)
                        pe.matmul(pS[u % 2][0:P, C3:D], OH[u][:], xs[u % 4][:], start=False, stop=True).then_inc(s_mm, 1)
                        if u < 4:
                            path_weights(u + 4)
                        if u in (1, 2, 3):
                            next(steps, None)
                        if u >= 4 and not last:
                            if u == 4:
                                pe.wait_ge(s_he, i * 3 + 6)
                            path_weights(u - 4)

                pe.wait_ge(s_w, 16 * (B + 6))
                pe.sem_inc(s_mm, B)
                for _ in network(0):
                    pass
                pe.wait_ge(s_he, 3)
                for u in range(4):
                    path_weights(u)
                with pe.Fori(0, GROUPS - 1) as i:
                    group(i, False)
                group(GROUPS - 1, True)

            @block.vector
            def _(v):
                for w in [W1, *Wm]:
                    v.memset(w[:], 0.0)
                v.memset(acc[:], 0.0).then_inc(s_z, 1)
                v.wait_ge(s_z, 1)
                v.sem_inc(s_acc, B)
                v.sem_inc(s_msg, B)

                regs = [v.alloc_register(f"sum3_block{u}") for u in range(B)]

                def message(k, u):
                    x, q, p, m = G[u], qq[u], pq[u % 4], ms[u % 4]
                    sh = [hdr[:, ds(k * HB + SH + a, 1)] for a in range(4)]
                    tw = [pT[u % 4][:, a * C3:(a + 1) * C3] for a in range(4)]
                    ax = [x[:, (a + 1) * C3:(a + 2) * C3] for a in range(3)]
                    base = k * STEPS
                    v.wait_ge(s_mm, mm.freed(k, 4))
                    v.wait_ge(s_q0, q0.done(k))
                    v.scalar_tensor_tensor(q[:], ax[1], sh[2], q[:], ALU.mult, ALU.add).then_inc(s_q, 1)
                    v.wait_ge(s_tp, tp.done(k))
                    v.tensor_tensor(p[:].rearrange("p (a c) -> p a c", a=2),
                                    pT[u % 4][:, 0:2 * C3].rearrange("p (a c) -> p a c", a=2),
                                    x[:, 0:C3].unsqueeze(1).to_broadcast([128, 2, C3]), ALU.mult).then_inc(s_q, 1)
                    v.wait_ge(s_q, base + 1)
                    v.scalar_tensor_tensor(q[:], ax[2], sh[3], q[:], ALU.mult, ALU.add).then_inc(s_q, 1)
                    v.scalar_tensor_tensor(m[:, C3:].rearrange("p (a c) -> p a c", a=3),
                                           x[:, C3:].rearrange("p (a c) -> p a c", a=3), sh[0],
                                           tw[2].unsqueeze(1).to_broadcast([128, 3, C3]), ALU.mult,
                                           ALU.mult).then_inc(s_q, 1)
                    v.wait_ge(s_q, base + 3)
                    v.scalar_tensor_tensor(q[:], q[:], INV3, tw[3], ALU.mult, ALU.mult).then_inc(s_q, 1)
                    v.wait_ge(s_q, base + 5)
                    v.scalar_tensor_tensor(m[:, 0:C3], p[:, 0:C3], sh[0], q[:], ALU.mult, ALU.add).then_inc(s_msg, 1)

                def add(k, u, b):
                    v.wait_ge(s_mm, mm.done(k))
                    v.wait_ge(s_acc, ac.freed(k, 1))
                    a = acc[:, ds(b * D, D)]
                    v.tensor_tensor(a, pS[u % 2][0:P, 0:D], a, ALU.add).then_inc(s_acc, 1)

                def group(i, last):
                    blocks = blocks_of(v, regs, blk_i, i * B)
                    for u in range(B):
                        if u < B - 1 or not last:
                            message(i * B + u + 1, (u + 1) % B)
                        add(i * B + u, u, blocks[u])

                message(0, 0)
                with v.Fori(0, GROUPS - 1) as i:
                    group(i, False)
                group(GROUPS - 1, True)
                v.wait_ge(s_acc, NT + B)


def gnn3_body(nc, A, B0, cw, dw, vv, tmp):
    with Phase(nc, "poly3") as ph:
        s_ch = ph.sem("ch")
        a3 = A[:].rearrange("p (t d) -> p t d", d=D)
        b3 = B0[:].rearrange("p (t d) -> p t d", d=D)
        v3 = vv[:].rearrange("p (t c) -> p t c", c=C3)
        t3 = tmp[:].rearrange("p (t c) -> p t c", c=C3)
        sh = [P, T, C3]
        row = lambda w, j: w[:, j * C3:(j + 1) * C3].unsqueeze(1).to_broadcast(sh)
        with nc.Block() as block:

            @block.vector
            def _(v):
                ch = Chain(v, s_ch)
                A0, O0 = a3[:, :, 0:C3], b3[:, :, 0:C3]
                ax = [a3[:, :, (a + 1) * C3:(a + 2) * C3] for a in range(3)]
                ch(v.tensor_tensor(v3, ax[0], ax[0], ALU.mult))
                for a in (1, 2):
                    ch(v.tensor_tensor(t3, ax[a], ax[a], ALU.mult))
                    ch(v.tensor_tensor(v3, v3, t3, ALU.add))
                ch(v.tensor_tensor(t3, A0, row(cw, 3), ALU.mult))
                ch(v.tensor_tensor(t3, t3, row(cw, 1), ALU.add))
                ch(v.tensor_tensor(t3, t3, A0, ALU.mult))
                ch(v.tensor_tensor(t3, t3, row(cw, 0), ALU.add))
                ch(v.tensor_tensor(O0, v3, row(cw, 4), ALU.mult))
                ch(v.tensor_tensor(t3, t3, O0, ALU.add))
                ch(v.tensor_tensor(t3, t3, A0, ALU.mult))
                ch(v.tensor_tensor(O0, v3, row(cw, 2), ALU.mult))
                ch(v.tensor_tensor(O0, t3, O0, ALU.add))
                ch(v.tensor_tensor(t3, A0, row(dw, 2), ALU.mult))
                ch(v.tensor_tensor(t3, t3, row(dw, 1), ALU.add))
                ch(v.tensor_tensor(t3, t3, A0, ALU.mult))
                ch(v.tensor_tensor(v3, v3, row(dw, 3), ALU.mult))
                ch(v.tensor_tensor(t3, t3, v3, ALU.add))
                ch(v.tensor_tensor(t3, t3, row(dw, 0), ALU.add))
                for a in range(3):
                    ch(v.tensor_tensor(b3[:, :, (a + 1) * C3:(a + 2) * C3], ax[a], t3, ALU.mult))


def gnn3_norm(nc, C, o, g0, be0, g1, X):
    with Phase(nc, "norm3b") as ph:
        s_ch, s_r, s_m, s_v, s_q = (ph.sem(n) for n in ("ch", "r", "m", "v", "q"))
        red = ph.sb("red", [P, 2 * C3])
        mean = ph.sb("mean", [P, C3])
        sc = ph.sb("sc", [P, 2 * C3])
        sq = ph.sb("sq", [P, T * D])
        pM, pV = ph.ps("pM"), ph.ps("pV")
        o3 = o[:].rearrange("p (t d) -> p t d", d=D)
        q3 = sq[:].rearrange("p (t d) -> p t d", d=D)
        x3 = X[:].rearrange("p (t d) -> p t d", d=D)
        sh = [P, T, C3]
        bc = lambda a: a.unsqueeze(1).to_broadcast(sh)
        with nc.Block() as block:

            @block.vector
            def _(v):
                ch = Chain(v, s_ch)
                v.tensor_reduce(red[:, 0:C3], o3[:, :, 0:C3].rearrange("p t c -> p c t"), AX, ALU.add).then_inc(s_r, 1)
                v.wait_ge(s_m, 1)
                ch(v.tensor_scalar(mean[:], pM[0][0:P, 0:C3], 1.0 / N, None, ALU.mult))
                ch(v.tensor_tensor(o3[:, :, 0:C3], o3[:, :, 0:C3], bc(mean[:]), ALU.subtract))
                ch(v.tensor_tensor(sq[:], o[:], o[:], ALU.mult))
                ch(v.tensor_reduce(red[:, 0:C3], q3[:, :, 0:C3].rearrange("p t c -> p c t"), AX, ALU.add))
                for a in (1, 2):
                    ch(v.tensor_tensor(q3[:, :, C3:2 * C3], q3[:, :, C3:2 * C3], q3[:, :, (a + 1) * C3:(a + 2) * C3], ALU.add))
                ch(v.tensor_reduce(red[:, C3:], q3[:, :, C3:2 * C3].rearrange("p t c -> p c t"), AX, ALU.add))
                v.sem_inc(s_r, 1)
                v.wait_ge(s_m, 2)
                ch(v.tensor_scalar(sc[:, 0:C3], pV[0][0:P, 0:C3], 1.0 / N, 1e-5, ALU.mult, ALU.add))
                ch(v.tensor_scalar(sc[:, C3:], pV[0][0:P, C3:2 * C3], 1.0 / (3 * N), 1e-5, ALU.mult, ALU.add))
                v.sem_inc(s_v, 1)
                v.wait_ge(s_q, 1)
                ch(v.reciprocal(sc[:], sc[:]))
                ch(v.tensor_tensor(sc[:, 0:C3], sc[:, 0:C3], g0[:], ALU.mult))
                ch(v.tensor_tensor(sc[:, C3:], sc[:, C3:], g1[:], ALU.mult))
                for b in range(4):
                    ob = o3[:, :, b * C3:(b + 1) * C3]
                    ch(v.tensor_tensor(ob, ob, bc(sc[:, 0:C3] if b == 0 else sc[:, C3:]), ALU.mult))
                    if b == 0:
                        ch(v.tensor_tensor(ob, ob, bc(be0[:]), ALU.add))
                        xb = x3[:, :, 0:C3]
                    else:
                        xb = x3[:, :, C3:].rearrange("p t (c a) -> p t a c", a=3)[:, :, b - 1, :]
                    ch(v.tensor_tensor(xb, xb, ob, ALU.add))

            @block.tensor
            def _(pe):
                pe.wait_ge(s_r, 1)
                pe.matmul(pM[0][0:P, 0:C3], C["ones"][0:P, 0:P], red[:, 0:C3], start=True, stop=True).then_inc(s_m, 1)
                pe.wait_ge(s_r, 2)
                pe.matmul(pV[0][0:P, 0:2 * C3], C["ones"][0:P, 0:P], red[:], start=True, stop=True).then_inc(s_m, 1)

            @block.scalar
            def _(act):
                act.wait_ge(s_v, 1)
                act.activation(sc[:], sc[:], ACT.Sqrt).then_inc(s_q, 1)


def gnn3(nc, C, hdr, blk_i, X, rstd, nbias, dr, sorted_rows, table):
    with ExitStack() as st:
        sb = lambda n, s: st.enter_context(nc.sbuf_tensor(f"g3_{n}", s, F32))
        acc, scc = sb("acc", [P, T * D]), sb("scc", [P, T * D])
        row_stats(nc, X, rstd, nbias, 1e-5)
        with ExitStack() as s2:
            sc = lambda n, s: s2.enter_context(nc.sbuf_tensor(f"g3_{n}", s, F32))
            Y, Wu = sc("Y", [P, T * D]), sc("Wu", [128, KD * D])
            normalise_by_axis(nc, X, rstd, nbias, Y)
            plain(nc, rstd, nbias)
            block_weights(nc, Wu, D, [(0, dr["W_up0"], dr["W_up1"])])
            project(nc, C, Y, rstd, nbias, w=Wu, F=D, out=acc, store=[(table, 0)])
            block_weights(nc, Wu, D, [(0, dr["Wsc0"], dr["Wsc1"])])
            project(nc, C, Y, rstd, nbias, w=Wu, F=D, out=scc)
        gnn3_sum(nc, C, hdr, blk_i, table, sorted_rows, dr, acc)
        with ExitStack() as s2:
            sc = lambda n, s: s2.enter_context(nc.sbuf_tensor(f"g3_{n}", s, F32))
            A, Wu = sc("A", [P, T * D]), sc("Wv", [128, KD * D])
            cw, dw = sc("cw", [P, 5 * C3]), sc("dw", [P, 4 * C3])
            vv, tmp = sc("vv", [P, T * C3]), sc("tmp", [P, T * C3])
            g0, be0, g1 = sc("g0", [P, C3]), sc("be0", [P, C3]), sc("g1", [P, C3])
            load_many(nc, [(cw[:], dr["Wc0T"].rearrange("j c -> (j c)").unsqueeze(0).to_broadcast([P, 5 * C3])),
                           (dw[:], dr["Wc1T"].rearrange("j c -> (j c)").unsqueeze(0).to_broadcast([P, 4 * C3]))]
                      + [(t[:], dr[n].unsqueeze(0).to_broadcast([P, C3]))
                         for t, n in ((g0, "gamma0"), (be0, "beta0"), (g1, "gamma1"))])
            block_weights(nc, Wu, D, [(0, dr["W_lin0"], dr["W_lin1"])])
            project(nc, C, acc, rstd, nbias, w=Wu, F=D, out=A)
            gnn3_body(nc, A, acc, cw, dw, vv, tmp)
            block_weights(nc, Wu, D, [(0, dr["WB0"], dr["WB1"])])
            project(nc, C, acc, rstd, nbias, w=Wu, F=D, add_to=scc)
            gnn3_norm(nc, C, scc, g0, be0, g1, X)


H3 = 8
G3 = 64
IN3 = H3 * G3
HP = H3 // 2
FXW = HP * 129


def ffn3_weights(nc, C, WxT, bxT, Wsl, bsl, temp, WS, bS):
    with Phase(nc, "w3") as ph:
        s_in, s_mm, s_ch = ph.sem("in"), ph.sem("mm"), ph.sem("ch")
        wx = ph.sb("wx", [G3, H3 * D])
        bx = ph.sb("bx", [G3, H3])
        wl = ph.sb("wl", [G3, G3])
        bl = ph.sb("bl", [1, G3])
        tr = ph.sb("tr", [128, H3])
        pW, pB = ph.ps("pW", KD), ph.ps("pB")
        with nc.Block() as block:

            @block.sync
            def _(sp):
                sp.dma_start(wx[:].rearrange("p (h d) -> p h d", h=H3), WxT.rearrange("(h p) d -> p h d", p=G3)).then_inc(s_in, 16)
                sp.dma_start(bx[:], bxT).then_inc(s_in, 16)
                sp.dma_start(wl[:], Wsl).then_inc(s_in, 16)
                sp.dma_start(bl[:], bsl.unsqueeze(0)).then_inc(s_in, 16)
                sp.dma_start(tr[:], temp.unsqueeze(0).to_broadcast([128, H3])).then_inc(s_in, 16)

            @block.tensor
            def _(pe):
                pe.wait_ge(s_in, 80)
                for h in range(H3):
                    for c in range(KD):
                        pe.matmul(pW[c][:, h * G3:(h + 1) * G3], wx[:, h * D + c * 128:h * D + (c + 1) * 128], wl[:],
                                  start=True, stop=True)
                    pe.matmul(pB[0][0:1, h * G3:(h + 1) * G3], bx[:, h:h + 1], wl[:], start=True, stop=False)
                    last = pe.matmul(pB[0][0:1, h * G3:(h + 1) * G3], C["ones"][0:1, 0:1], bl[:], start=False, stop=True)
                last.then_inc(s_mm, 1)

            @block.vector
            def _(v):
                ch = Chain(v, s_ch)
                v.wait_ge(s_in, 80)
                ch(v.tensor_scalar(tr[:], tr[:], 0.1, 5.0, ALU.max, ALU.min))
                ch(v.reciprocal(tr[:], tr[:]))
                v.wait_ge(s_mm, 1)
                for c in range(KD):
                    ch(v.tensor_tensor(WS[:, c * IN3:(c + 1) * IN3].rearrange("p (h g) -> p h g", h=H3),
                                       pW[c][:, :].rearrange("p (h g) -> p h g", h=H3),
                                       over(tr[:], [128, H3, G3]), ALU.mult))
                ch(v.tensor_tensor(bS[:].rearrange("p (h g) -> p h g", h=H3),
                                   pB[0][0:1, :].rearrange("p (h g) -> p h g", h=H3),
                                   over(tr[0:1, :], [1, H3, G3]), ALU.mult))


def softmax3(nc, L, pairs):
    rows, runs = pairs
    with Phase(nc, "soft3") as ph:
        s_ch, s_v, s_e = ph.sem("ch"), ph.sem("v"), ph.sem("e")
        m = ph.sb("m", [rows, runs])
        l3 = L[:].rearrange("p (r g) -> p r g", g=G3)
        sh = [rows, runs, G3]
        with nc.Block() as block:

            @block.vector
            def _(v):
                ch = Chain(v, s_ch)
                ch(v.tensor_reduce(m[:], l3, AX, ALU.max))
                ch(v.tensor_tensor(l3, l3, over(m[:], sh), ALU.subtract))
                v.sem_inc(s_v, 1)
                v.wait_ge(s_e, 1)
                ch(v.tensor_reduce(m[:], l3, AX, ALU.add))
                ch(v.reciprocal(m[:], m[:]))
                ch(v.tensor_tensor(l3, l3, over(m[:], sh), ALU.mult))

            @block.scalar
            def _(act):
                act.wait_ge(s_v, 1)
                act.activation(L[:], L[:], ACT.Exp).then_inc(s_e, 1)


def ffn3_tokens(nc, C, SW, FX, tok):
    with Phase(nc, "tok3") as ph:
        s_one, s_ch, s_all = ph.sem("one"), ph.sem("ch"), ph.sem("all")
        rn = ph.sb("rn", [128, HP])
        pS = ph.ps("pS", HP)
        with nc.Block() as block:

            @block.tensor
            def _(pe):
                pe.wait_ge(s_one, 1)
                for t in range(T):
                    for p in range(HP):
                        a, b = t * IN3 + p * 128, t * FXW + p * 129
                        last = pe.matmul(pS[p][:, 0:129], SW[:, a:a + 128], FX[:, b:b + 129], start=(t == 0),
                                         stop=(t == T - 1))
                last.then_inc(s_all, 1)

            @block.vector
            def _(v):
                ch = Chain(v, s_ch)
                v.memset(FX[:].rearrange("p (n c) -> p n c", c=129)[:, :, 128:129], 1.0).then_inc(s_one, 1)
                v.wait_ge(s_all, 1)
                for p in range(HP):
                    ch(v.tensor_scalar(rn[:, p:p + 1], pS[p][:, 128:129], 1e-5, None, ALU.add))
                ch(v.reciprocal(rn[:], rn[:]))
                for p in range(HP):
                    for b in (0, 64):
                        ch(v.tensor_scalar(tok[b:b + 64, p * G3:(p + 1) * G3], pS[p][b:b + 64, b:b + 64],
                                           rn[b:b + 64, p:p + 1], None, ALU.mult))


def ffn3_attention(nc, C, tok, wq, wk, wv, wo, V):
    SCALE = float(G3) ** -0.5
    with Phase(nc, "att3") as ph:
        s_in, s_pe, s_ch, s_v, s_a = ph.sem("in"), ph.sem("pe"), ph.sem("ch"), ph.sem("v"), ph.sem("a")
        ws = [ph.sb(n, [G3, G3]) for n in ("wq", "wk", "wv")]
        wos = ph.sb("wo", [128, HP * D])
        tokT = ph.sb("tokT", [G3, HP * 128])
        qk = ph.ring("qk", 2, [G3, HP * 128])
        vs, osl = ph.sb("vs", [128, HP * G3]), ph.sb("os", [128, HP * G3])
        at = ph.sb("at", [128, HP * G3])
        bd, bdT = ph.sb("bd", [128, HP * 128]), ph.sb("bdT", [128, HP * 128])
        m = ph.sb("m", [128, HP])
        pA, pB, pV = ph.ps("pA", 1), ph.ps("pB", 3), ph.ps("pV", HP)
        a3 = at[:].rearrange("p (h g) -> p h g", h=HP)
        sh = [128, HP, G3]

        def blocks(dst, src):
            d3 = dst[:].rearrange("p (h g) -> p h g", h=HP)
            s3 = src[:].rearrange("p (h g) -> p h g", h=HP)
            for b in (0, 64):
                wide = (d3 if d3.shape[2] == 128 else s3)
                yield (d3[b:b + 64, :, b:b + 64] if wide is d3 else d3[b:b + 64],
                       s3[b:b + 64, :, b:b + 64] if wide is s3 else s3[b:b + 64])

        with nc.Block() as block:

            @block.sync
            def _(sp):
                for t, d in zip(ws, (wq, wk, wv)):
                    sp.dma_start(t[:], d).then_inc(s_in, 16)
                sp.dma_start(wos[:].rearrange("p (c d) -> p c d", c=HP), wo.rearrange("(c p) d -> p c d", p=128)).then_inc(s_in, 16)

            @block.tensor
            def _(pe):
                pe.wait_ge(s_in, 64)
                for p in range(HP):
                    last = pe.transpose(pA[0][0:G3, p * 128:(p + 1) * 128], tok[:, p * G3:(p + 1) * G3], C["ident"][:])
                last.then_inc(s_pe, 1)
                pe.wait_ge(s_v, 1)
                for j in range(2):
                    pe.matmul(pB[j][0:G3, :], ws[j][:], tokT[:], start=True, stop=True)
                for p in range(HP):
                    last = pe.matmul(pB[2][:, p * G3:(p + 1) * G3], tokT[:, p * 128:(p + 1) * 128], ws[2][:],
                                     start=True, stop=True)
                last.then_inc(s_pe, 1)
                pe.wait_ge(s_v, 2)
                for p in range(HP):
                    c = slice(p * 128, (p + 1) * 128)
                    last = pe.matmul(pA[0][:, c], qk[0][:, c], qk[1][:, c], start=True, stop=True)
                last.then_inc(s_pe, 1)
                pe.wait_ge(s_v, 4)
                for p in range(HP):
                    c = slice(p * 128, (p + 1) * 128)
                    last = pe.transpose(pB[0][:, c], bd[:, c], C["ident"][:])
                last.then_inc(s_pe, 1)
                pe.wait_ge(s_v, 5)
                for p in range(HP):
                    last = pe.matmul(pB[1][:, p * G3:(p + 1) * G3], bdT[:, p * 128:(p + 1) * 128],
                                     vs[:, p * G3:(p + 1) * G3], start=True, stop=True)
                last.then_inc(s_pe, 1)
                pe.wait_ge(s_v, 6)
                for p in range(HP):
                    c = slice(p * 128, (p + 1) * 128)
                    last = pe.transpose(pB[2][:, c], bd[:, c], C["ident"][:])
                last.then_inc(s_pe, 1)
                pe.wait_ge(s_v, 7)
                for p in range(HP):
                    last = pe.matmul(pV[p][:, 0:D], bdT[:, p * 128:(p + 1) * 128], wos[:, p * D:(p + 1) * D],
                                     start=True, stop=True)
                last.then_inc(s_pe, 1)

            @block.scalar
            def _(act):
                act.wait_ge(s_v, 3)
                act.activation(at[:], at[:], ACT.Exp, scale=SCALE).then_inc(s_a, 1)

            @block.vector
            def _(v):
                ch = Chain(v, s_ch)
                ch(v.memset(bd[:], 0.0))
                v.wait_ge(s_pe, 1)
                ch(v.tensor_copy(tokT[:], pA[0][0:G3, :]))
                v.sem_inc(s_v, 1)
                v.wait_ge(s_pe, 2)
                for j in range(2):
                    ch(v.tensor_copy(qk[j][:], pB[j][0:G3, :]))
                ch(v.tensor_copy(vs[:], pB[2][:, 0:HP * G3]))
                v.sem_inc(s_v, 1)
                v.wait_ge(s_pe, 3)
                for o, i in blocks(at, pA[0]):
                    ch(v.tensor_copy(o, i))
                ch(v.tensor_reduce(m[:], a3, AX, ALU.max))
                ch(v.tensor_tensor(a3, a3, over(m[:], sh), ALU.subtract))
                v.sem_inc(s_v, 1)
                v.wait_ge(s_a, 1)
                ch(v.tensor_reduce(m[:], a3, AX, ALU.add))
                ch(v.reciprocal(m[:], m[:]))
                ch(v.tensor_tensor(a3, a3, over(m[:], sh), ALU.mult))
                for o, i in blocks(bd, at):
                    ch(v.tensor_copy(o, i))
                v.sem_inc(s_v, 1)
                v.wait_ge(s_pe, 4)
                ch(v.tensor_copy(bdT[:], pB[0][:]))
                v.sem_inc(s_v, 1)
                v.wait_ge(s_pe, 5)
                ch(v.tensor_copy(osl[:], pB[1][:, 0:HP * G3]))
                for o, i in blocks(bd, osl):
                    ch(v.tensor_copy(o, i))
                v.sem_inc(s_v, 1)
                v.wait_ge(s_pe, 6)
                ch(v.tensor_copy(bdT[:], pB[2][:]))
                v.sem_inc(s_v, 1)
                v.wait_ge(s_pe, 7)
                for p in range(HP):
                    ch(v.tensor_copy(V[:, p * D:(p + 1) * D], pV[p][:, 0:D]))


def ffn3(nc, C, X, rstd, nbias, dr):
    with ExitStack() as st:
        sb = lambda n, s: st.enter_context(nc.sbuf_tensor(f"f3_{n}", s, F32))
        SW, V, bo = sb("SW", [P, T * IN3]), sb("V", [128, HP * D]), sb("bo", [1, D])
        row_stats(nc, X, rstd, nbias, 1e-5)
        with ExitStack() as s2:
            sc = lambda n, s: s2.enter_context(nc.sbuf_tensor(f"f3_{n}", s, F32))
            FX, WS, bS = sc("FX", [P, T * FXW]), sc("WS", [128, KD * IN3]), sc("bS", [1, IN3])
            WF, bF, tok = sc("WF", [128, KD * IN3]), sc("bF", [1, IN3]), sc("tok", [128, HP * G3])
            load_many(nc, [(WF[:].rearrange("p (c f) -> p c f", c=KD), dr["W_fx"].rearrange("(c p) f -> p c f", p=128)),
                           (bF[:], dr["b_fx"].unsqueeze(0)), (bo[:], dr["b_out"].unsqueeze(0))])
            ffn3_weights(nc, C, dr["W_xT"], dr["b_xT"], dr["W_slice"], dr["b_slice"], dr["temperature"], WS, bS)
            project(nc, C, X, rstd, nbias, w=WS, F=IN3, brow=bS[:], out=SW)
            project(nc, C, X, rstd, nbias, w=WF, F=IN3, brow=bF[:], out=FX, pieces=HP)
            softmax3(nc, SW, (P, T * H3))
            ffn3_tokens(nc, C, SW, FX, tok)
            ffn3_attention(nc, C, tok, dr["W_q"], dr["W_k"], dr["W_v"], dr["W_out"], V)
        plain(nc, rstd, nbias)
        project(nc, C, SW, rstd, nbias, w=V, F=D, brow=bo[:], add_to=X, kd=HP)


def store_result(nc, X, out):
    with Phase(nc, "result") as ph:
        s = ph.sem("stored")
        with nc.Block() as block:

            @block.sync
            def _(sp):
                sp.dma_start(out.rearrange("(t p) d -> p t d", p=P),
                             X[:].rearrange("p (t d) -> p t d", d=D)).then_inc(s, 16)
                sp.wait_ge(s, 16)


def gnn0(nc, C, sorted_rows, hdr, blk_i, X, rstd, nbias, dis, dr, table):
    with ExitStack() as st:
        W = st.enter_context(nc.sbuf_tensor("g0_W", [128, KD * F0], F32))
        tab = st.enter_context(nc.sbuf_tensor("g0_tab", [P, T * F0], F32))
        gnn0_weights(nc, dr["W_forward"], dr["W_reverse"], dr["attnT"], dr["W_forwardT"], dr["W_reverseT"], W)
        row_stats(nc, X, rstd, nbias, 1e-5)
        project(nc, C, X, rstd, nbias, w=W, F=F0, out=tab, store=[(table, 0)],
                also=[header_words(sorted_rows, hdr)])
    with ExitStack() as st:
        acc = st.enter_context(nc.sbuf_tensor("g0_acc", [P, T * S0], F32))
        with ExitStack() as s2:
            M = s2.enter_context(nc.sbuf_tensor("g0_M", [128, NTL * H0], F32))
            ex = s2.enter_context(nc.sbuf_tensor("g0_ex", [128, NTL * NH], F32))
            gnn0_messages(nc, table, hdr, M)
            gnn0_softmax(nc, hdr, M, ex)
            gnn0_sum(nc, C, hdr, blk_i, M, ex, acc)
        gnn0_update(nc, acc, X, dis)


def program(nc, dr, out):
    def layer(prefix):
        return {n[len(prefix):]: a for n, a in dr.items() if n.startswith(prefix)}

    Phase.opened = Phase.pool_dma_sems = 0
    sorted_rows = nc.dram_tensor("sorted_rows", [NT * LANES, ROW], F32).ap()
    table0 = nc.dram_tensor("table0", [N, F0], F32).ap()
    table = nc.dram_tensor("table", [N, D], F32).ap()
    tscore = nc.dram_tensor("tscore", [N, NH], F32).ap()
    buf = nc.dram_tensor("buf", [BUF, D], F32).ap()
    ybuf = nc.dram_tensor("ybuf", [NE * ES, D], F32).ap()
    ybuf1 = nc.dram_tensor("ybuf1", [NTT * 128, D], F32).ap()
    with ExitStack() as st:
        def sb(name, shape, dt=F32):
            return st.enter_context(nc.sbuf_tensor(name, shape, dt))

        C = {"ident": sb("ident", [128, 128]), "tri": sb("tri", [128, 128]), "ones": sb("ones", [128, 128]),
             "nodes": sb("nodes", [128, P]), "row": sb("row", [128, NT])}
        X, dis = sb("X", [P, T * D]), sb("dis", [P, T])
        rstd, nbias = sb("rstd", [P, T]), sb("nbias", [P, T])
        load_constants(nc, dr["x"], X, C)
        with ExitStack() as edges:
            hdr = edges.enter_context(nc.sbuf_tensor("hdr", [128, NTX * HB], F32))
            blk_i = edges.enter_context(nc.sbuf_tensor("blk_i", [1, NT], I32))
            with ExitStack() as s2:
                slots = s2.enter_context(nc.sbuf_tensor("slots", [P, ET], I32))
                loc1 = s2.enter_context(nc.sbuf_tensor("loc1", [P, ET], F32))
                EA = s2.enter_context(nc.sbuf_tensor("EA", [128, NH * EF], F32))
                edge_attention(nc, C, dr["L2_gnn_lin_edge_W"], dr["L2_gnn_att_edgeT"], EA)
                sort_edges(nc, C, dr["dst"], sorted_rows, slots, loc1, blk_i)
                scatter_edges(nc, dr["src"], dr["edge_attr_2"], dr["edge_weight"], dr["edge_attr_4"],
                              dr["edge_attr_16"], dr["edge_attr_32"], EA, slots, loc1, sorted_rows, hdr)
            gnn0(nc, C, sorted_rows, hdr, blk_i, X, rstd, nbias, dis, layer("L0_gnn_"), table0)
            ffn0(nc, C, X, rstd, nbias, layer("L0_ffn_"), buf, ybuf)
            gnn1(nc, C, hdr, blk_i, X, dis, rstd, nbias, layer("L1_gnn_"), table)
            ffn1(nc, C, X, rstd, nbias, layer("L1_ffn_"), table, ybuf1)
            gnn2(nc, C, hdr, blk_i, X, rstd, nbias, layer("L2_gnn_"), sorted_rows, table, tscore)
            ffn2(nc, C, X, rstd, nbias, layer("L2_ffn_"))
            gnn3(nc, C, hdr, blk_i, X, rstd, nbias, layer("L3_gnn_"), sorted_rows, table)
        ffn3(nc, C, X, rstd, nbias, layer("L3_ffn_"))
        store_result(nc, X, out)


def columns(a):
    e, f = a.shape
    return a.reshape(e, f // 128, 128).transpose(2, 0, 1).reshape(128, -1)


def kernel(**inputs):
    import concourse.bacc as bacc
    from concourse.bass_utils import run_bass_kernel_spmd

    a = {n: np.asarray(v) for n, v in inputs.items()}
    g0 = {"W_forward": a["L0_gnn_W_forward"], "W_reverse": a["L0_gnn_W_reverse"],
          "W_forwardT": a["L0_gnn_W_forward"].T, "W_reverseT": a["L0_gnn_W_reverse"].T,
          "attnT": a["L0_gnn_attn_forward"][0].T}
    f0 = {n: a["L0_ffn_" + n] for n in ("gate_w", "gate_b", "w1", "w2", "b2")} | {"b1T": columns(a["L0_ffn_b1"])}
    g1 = {n: a["L1_gnn_" + n] for n in ("ln6_g", "ln6_b", "ln7_g", "ln7_b", "b6", "b7", "bp")} | {
        n: a["L1_gnn_" + n].T for n in ("W6", "W7", "Wp")}
    f1 = {n: a["L1_ffn_" + n] for n in ("Wr", "br", "W1", "W2", "b2")} | {
        "b1T": columns(a["L1_ffn_b1"]), "gT": columns(a["L1_ffn_ln_g"]), "bT": columns(a["L1_ffn_ln_b"])}
    g2 = {"lin_W": a["L2_gnn_lin_W"], "lin_WT": a["L2_gnn_lin_W"].T, "asT": a["L2_gnn_att_src"].T,
          "adT": a["L2_gnn_att_dst"].T, "bias": a["L2_gnn_bias"], "lin_edge_W": a["L2_gnn_lin_edge_W"],
          "att_edgeT": a["L2_gnn_att_edge"].T}
    f2 = {n: a["L2_ffn_" + n] for n in ("Wr", "br", "W1", "W2", "Wo", "bo")} | {
        n + "T": columns(a["L2_ffn_" + n]) for n in ("b1", "g1", "be1", "m1", "v1", "b2", "g2", "be2", "m2", "v2")}
    g3 = {n: a["L3_gnn_" + n] for n in ("W_up0", "W_up1", "M1", "M2", "M3", "M4", "W_lin0", "W_lin1", "Wsc0", "Wsc1",
                                        "WB0", "WB1", "gamma0", "beta0", "gamma1")} | {
        n + "T": a["L3_gnn_" + n].T for n in ("Wc0", "Wc1")}
    f3 = {n: a["L3_ffn_" + n] for n in ("W_fx", "b_fx", "W_slice", "b_slice", "W_q", "W_k", "W_v", "W_out", "b_out")} | {
        "W_xT": a["L3_ffn_W_x"].T, "b_xT": a["L3_ffn_b_x"].reshape(H3, G3).T,
        "temperature": a["L3_ffn_temperature"].reshape(H3)}
    laid = {n: a[n] for n in ("x", "src", "dst", "edge_attr_16", "edge_attr_2", "edge_attr_32", "edge_attr_4", "edge_weight")}
    for prefix, d in (("L0_gnn_", g0), ("L0_ffn_", f0), ("L1_gnn_", g1), ("L1_ffn_", f1),
                      ("L2_gnn_", g2), ("L2_ffn_", f2), ("L3_gnn_", g3), ("L3_ffn_", f3)):
        laid |= {prefix + n: v for n, v in d.items()}
    laid = {n: np.ascontiguousarray(v) for n, v in laid.items()}

    nc = bacc.Bacc("TRN2", target_bir_lowering=False, num_devices=1)
    dr = {n: nc.dram_tensor(f"in_{n}", v.shape, mybir.dt.from_np(v.dtype), kind="ExternalInput").ap()
          for n, v in laid.items()}
    out = nc.dram_tensor("out_x", (N, D), F32, kind="ExternalOutput").ap()
    program(nc, dr, out)
    r = run_bass_kernel_spmd(nc, [{f"in_{n}": v for n, v in laid.items()}], core_ids=[0])
    return r.results[0]["out_x"]
```
